# Optimizing a Trainium2 kernel written in Bass

```python
import numpy as np
import jax
import jax.numpy as jnp

def _softmax(x, axis=-1):
    return jax.nn.softmax(x, axis=axis)

def _gelu(x):
    return jax.nn.gelu(x, approximate=True)

def _silu(x):
    return jax.nn.silu(x)

def _sigmoid(x):
    return jax.nn.sigmoid(x)

def _layernorm(x, axis=-1, eps=1e-05):
    m = jnp.mean(x, axis=axis, keepdims=True)
    v = jnp.var(x, axis=axis, keepdims=True)
    return (x - m) / jnp.sqrt(v + eps)

def _scatter_add(tgt, idx, src, axis=0):
    return tgt.at[idx].add(src)

def _segment_sum(src, seg, n):
    return jax.ops.segment_sum(src, seg, n)
kernel_name = 'mk_conv_attn_hybrid_d4_conv_nchw256_r2_16fb67'

def setup_inputs(seed: int=0):
    np.random.seed(seed)
    _w = jnp.asarray

    def _rec_inputs():
        import jax
        import jax.numpy as jnp
        _gk = jax.random.key(seed)
        x = 7.22e-05 + 1 * jax.random.normal(jax.random.fold_in(_gk, 1), (8, 128, 32, 32), jnp.float32)
        return x
    x = _rec_inputs()

    def _L0_conv_setup():
        import jax, jax.numpy as jnp
        import numpy as np
        SP = 4
        HEADS = 8
        SHIFTS = (0, 2)

        def _to_windows(t, nh, hs, nw, ws, heads):
            B, C, H, W = t.shape
            hd = C // heads
            t = t.reshape(B, hd, heads, nh, hs, nw, ws)
            t = t.transpose(0, 3, 5, 2, 4, 6, 1)
            return t.reshape(B * nh * nw, heads, hs * ws, hd)

        def _from_windows(t, B, nh, hs, nw, ws, heads):
            hd = t.shape[-1]
            t = t.reshape(B, nh, nw, heads, hs, ws, hd)
            t = t.transpose(0, 6, 3, 1, 4, 2, 5)
            return t.reshape(B, hd * heads, nh * hs, nw * ws)

        def _dwconv3(v, w, b):
            out = jax.lax.conv_general_dilated(v, w, window_strides=(1, 1), padding=((1, 1), (1, 1)), dimension_numbers=('NCHW', 'OIHW', 'NCHW'), feature_group_count=v.shape[1])
            return out + b[None, :, None, None]
        key = jax.random.key(seed)
        k1, k2, k3, k4 = jax.random.split(key, 4)
        B, C, H, W = (8, 128, 32, 32)
        sd = C // 2
        x = jax.random.normal(k1, (B, C, H, W), dtype=jnp.float32)
        w_qkv = jax.random.normal(k2, (3 * sd, sd, 1, 1), dtype=jnp.float32) * 0.05
        w_lepe = jax.random.normal(k3, (sd, 1, 3, 3), dtype=jnp.float32) * 0.1
        b_lepe = jax.random.normal(k4, (sd,), dtype=jnp.float32) * 0.01
        return {'x': x, 'w_qkv': w_qkv, 'w_lepe': w_lepe, 'b_lepe': b_lepe}
    _L0_conv_all = _L0_conv_setup()
    _L0_conv_in = {k: v for k, v in _L0_conv_all.items() if k in ('w_qkv', 'w_lepe', 'b_lepe')}
    del _L0_conv_all

    def _L1_conv_setup():
        import jax, jax.numpy as jnp
        import numpy as np
        EPS = 1e-05
        SLOPE = 0.01
        C = 128
        key = jax.random.key(seed)
        k = jax.random.split(key, 5)
        B, H, W = (8, 64, 64)
        x = jax.random.normal(k[0], (B, C, H, W), dtype=jnp.float32)
        attn_w1 = jax.random.normal(k[1], (C // 4, C), dtype=jnp.float32) * (1.0 / np.sqrt(C))
        attn_w2 = jax.random.normal(k[2], (C, C // 4), dtype=jnp.float32) * (1.0 / np.sqrt(C // 4))
        refine_w = jax.random.normal(k[3], (C, 1, 3, 3), dtype=jnp.float32) * (1.0 / 3.0)
        refine_b = jax.random.normal(k[4], (C,), dtype=jnp.float32) * 0.01
        return {'x': x, 'attn_w1': attn_w1, 'attn_w2': attn_w2, 'refine_w': refine_w, 'refine_b': refine_b}
    _L1_conv_all = _L1_conv_setup()
    _L1_conv_in = {k: v for k, v in _L1_conv_all.items() if k in ('attn_w1', 'attn_w2', 'refine_w', 'refine_b')}
    del _L1_conv_all

    def _L2_attn_setup():
        import jax, jax.numpy as jnp
        import numpy as np
        B, N, C, H = (4, 1024, 128, 16)
        D = C // H
        key = jax.random.key(seed)
        k1, k2, k3 = jax.random.split(key, 3)
        x = jax.random.normal(k1, (B, N, C), dtype=jnp.float32)
        w_qkv = jax.random.normal(k2, (C, 3 * C), dtype=jnp.float32) * C ** (-0.5)
        b_qkv = jnp.zeros((3 * C,), dtype=jnp.float32)
        w_proj = jax.random.normal(k3, (C, C), dtype=jnp.float32) * C ** (-0.5)
        b_proj = jnp.zeros((C,), dtype=jnp.float32)
        return {'x': x, 'w_qkv': w_qkv, 'b_qkv': b_qkv, 'w_proj': w_proj, 'b_proj': b_proj}
    _L2_attn_all = _L2_attn_setup()
    _L2_attn_in = {k: v for k, v in _L2_attn_all.items() if k in ('w_qkv', 'b_qkv', 'w_proj', 'b_proj')}
    del _L2_attn_all

    def _L2_ffn_setup():
        import jax, jax.numpy as jnp
        import numpy as np
        NUM_EXPERTS = 8
        TOP_K = 2
        B, S, D = (8, 4096, 128)

        def _moe(tokens, router_w, w1, b1, w2, b2):
            N = tokens.shape[0]
            E = router_w.shape[0]
            logits = tokens.astype(jnp.float32) @ router_w.astype(jnp.float32).T
            probs = jax.nn.softmax(logits, axis=-1)
            rw, re = jax.lax.top_k(probs, TOP_K)
            if TOP_K > 1:
                rw = rw / jnp.maximum(rw.sum(-1, keepdims=True), 1e-12)
            rw = rw.astype(tokens.dtype)
            combine = jnp.zeros((N, E), tokens.dtype).at[jnp.arange(N)[:, None], re].set(rw)
            out = tokens
            for e in range(E):
                h = jax.nn.gelu(tokens @ w1[e] + b1[e], approximate=False)
                y = h @ w2[e] + b2[e]
                out = out + combine[:, e:e + 1] * y
            return out
        key = jax.random.key(seed)
        ks = jax.random.split(key, 4)
        scale = 1.0 / np.sqrt(D).astype(np.float32)
        return {'input_embeddings': jax.random.normal(ks[0], (B, S, D), jnp.float32), 'router_w': jax.random.normal(ks[1], (NUM_EXPERTS, D), jnp.float32) * scale, 'w1': jax.random.normal(ks[2], (NUM_EXPERTS, D, D), jnp.float32) * scale, 'b1': jnp.zeros((NUM_EXPERTS, D), jnp.float32), 'w2': jax.random.normal(ks[3], (NUM_EXPERTS, D, D), jnp.float32) * scale, 'b2': jnp.zeros((NUM_EXPERTS, D), jnp.float32)}
    _L2_ffn_all = _L2_ffn_setup()
    _L2_ffn_in = {k: v for k, v in _L2_ffn_all.items() if k in ('router_w', 'w1', 'b1', 'w2', 'b2')}
    del _L2_ffn_all

    def _L3_attn_setup():
        import jax, jax.numpy as jnp
        import numpy as np
        WINDOW = 16
        EPS = 1e-05
        key = jax.random.key(seed)
        k1, = jax.random.split(key, 1)
        x = jax.random.normal(k1, (2, 8192, 128), dtype=jnp.float32)
        gamma = jnp.ones((128,), dtype=jnp.float32)
        beta = jnp.zeros((128,), dtype=jnp.float32)
        return {'x': x, 'gamma': gamma, 'beta': beta}
    _L3_attn_all = _L3_attn_setup()
    _L3_attn_in = {k: v for k, v in _L3_attn_all.items() if k in ('gamma', 'beta')}
    del _L3_attn_all

    def _L3_ffn_setup():
        import jax, jax.numpy as jnp
        import numpy as np
        N_EXPERTS = 8
        TOP_K = 2
        key = jax.random.key(seed)
        ks = jax.random.split(key, 5)
        B, T, C, E, H = (8, 1024, 128, 8, 341)
        scale = 1.0 / np.sqrt(C)
        return {'x': jax.random.normal(ks[0], (B, T, C), dtype=jnp.float32), 'router_w': jax.random.normal(ks[1], (E, C), dtype=jnp.float32) * scale, 'w1': jax.random.normal(ks[2], (E, H, C), dtype=jnp.float32) * scale, 'w2': jax.random.normal(ks[3], (E, C, H), dtype=jnp.float32) * (1.0 / np.sqrt(H)), 'w3': jax.random.normal(ks[4], (E, H, C), dtype=jnp.float32) * scale}
    _L3_ffn_all = _L3_ffn_setup()
    _L3_ffn_in = {k: v for k, v in _L3_ffn_all.items() if k in ('router_w', 'w1', 'w2', 'w3')}
    del _L3_ffn_all
    return {'x': x, 'L0_conv_w_qkv': _L0_conv_in['w_qkv'], 'L0_conv_w_lepe': _L0_conv_in['w_lepe'], 'L0_conv_b_lepe': _L0_conv_in['b_lepe'], 'L1_conv_attn_w1': _L1_conv_in['attn_w1'], 'L1_conv_attn_w2': _L1_conv_in['attn_w2'], 'L1_conv_refine_w': _L1_conv_in['refine_w'], 'L1_conv_refine_b': _L1_conv_in['refine_b'], 'L2_attn_w_qkv': _L2_attn_in['w_qkv'], 'L2_attn_b_qkv': _L2_attn_in['b_qkv'], 'L2_attn_w_proj': _L2_attn_in['w_proj'], 'L2_attn_b_proj': _L2_attn_in['b_proj'], 'L2_ffn_router_w': _L2_ffn_in['router_w'], 'L2_ffn_w1': _L2_ffn_in['w1'], 'L2_ffn_b1': _L2_ffn_in['b1'], 'L2_ffn_w2': _L2_ffn_in['w2'], 'L2_ffn_b2': _L2_ffn_in['b2'], 'L3_attn_gamma': _L3_attn_in['gamma'], 'L3_attn_beta': _L3_attn_in['beta'], 'L3_ffn_router_w': _L3_ffn_in['router_w'], 'L3_ffn_w1': _L3_ffn_in['w1'], 'L3_ffn_w2': _L3_ffn_in['w2'], 'L3_ffn_w3': _L3_ffn_in['w3']}

def reference(x, L0_conv_w_qkv, L0_conv_w_lepe, L0_conv_b_lepe, L1_conv_attn_w1, L1_conv_attn_w2, L1_conv_refine_w, L1_conv_refine_b, L2_attn_w_qkv, L2_attn_b_qkv, L2_attn_w_proj, L2_attn_b_proj, L2_ffn_router_w, L2_ffn_w1, L2_ffn_b1, L2_ffn_w2, L2_ffn_b2, L3_attn_gamma, L3_attn_beta, L3_ffn_router_w, L3_ffn_w1, L3_ffn_w2, L3_ffn_w3):
    import jax
    import jax.numpy as jnp

    def _L0_conv_ref(x, w_qkv, w_lepe, b_lepe):
        import jax, jax.numpy as jnp
        import numpy as np
        SP = 4
        HEADS = 8
        SHIFTS = (0, 2)

        def _to_windows(t, nh, hs, nw, ws, heads):
            B, C, H, W = t.shape
            hd = C // heads
            t = t.reshape(B, hd, heads, nh, hs, nw, ws)
            t = t.transpose(0, 3, 5, 2, 4, 6, 1)
            return t.reshape(B * nh * nw, heads, hs * ws, hd)

        def _from_windows(t, B, nh, hs, nw, ws, heads):
            hd = t.shape[-1]
            t = t.reshape(B, nh, nw, heads, hs, ws, hd)
            t = t.transpose(0, 6, 3, 1, 4, 2, 5)
            return t.reshape(B, hd * heads, nh * hs, nw * ws)

        def _dwconv3(v, w, b):
            out = jax.lax.conv_general_dilated(v, w, window_strides=(1, 1), padding=((1, 1), (1, 1)), dimension_numbers=('NCHW', 'OIHW', 'NCHW'), feature_group_count=v.shape[1])
            return out + b[None, :, None, None]
        B, C, H, W = x.shape
        sd = C // 2
        scale = (sd // HEADS) ** (-0.5)
        wq = w_qkv[:, :, 0, 0]
        outs = []
        for s in SHIFTS:
            xs = jnp.roll(x, (-s, -s), axis=(1, 2)) if s > 0 else x
            parts = []
            strip_params = [(1, H, W // SP, SP), (H // SP, SP, 1, W)]
            for idx, (nh, hs, nw, ws) in enumerate(strip_params):
                xsp = xs[:, idx * sd:(idx + 1) * sd]
                qkv = jnp.einsum('bchw,oc->bohw', xsp, wq)
                q, k, v = (qkv[:, :sd], qkv[:, sd:2 * sd], qkv[:, 2 * sd:])
                lepe = _dwconv3(v, w_lepe, b_lepe)
                qw = _to_windows(q, nh, hs, nw, ws, HEADS) * scale
                kw = _to_windows(k, nh, hs, nw, ws, HEADS)
                vw = _to_windows(v, nh, hs, nw, ws, HEADS)
                lw = _to_windows(lepe, nh, hs, nw, ws, HEADS)
                attn = jax.nn.softmax(jnp.einsum('whqc,whkc->whqk', qw, kw), axis=-1)
                ow = jnp.einsum('whqk,whkc->whqc', attn, vw) + lw
                o = _from_windows(ow, B, nh, hs, nw, ws, HEADS)
                if s > 0:
                    o = jnp.roll(o, (s, s), axis=(1, 2))
                parts.append(o)
            outs.append(jnp.concatenate(parts, axis=1))
        return outs[0] + outs[1]

    def _L1_conv_ref(x, attn_w1, attn_w2, refine_w, refine_b):
        import jax, jax.numpy as jnp
        import numpy as np
        EPS = 1e-05
        SLOPE = 0.01
        C = 128
        xw = jax.lax.stop_gradient(x)
        p = jnp.mean(xw, axis=(2, 3))
        h = jax.nn.leaky_relu(p @ attn_w1.T, SLOPE)
        a = jax.nn.sigmoid(h @ attn_w2.T)
        y = xw * a[:, :, None, None]
        y = jax.lax.conv_general_dilated(y, refine_w, window_strides=(1, 1), padding='SAME', feature_group_count=C, dimension_numbers=('NCHW', 'OIHW', 'NCHW'))
        y = y + refine_b[None, :, None, None]
        mu = jnp.mean(y, axis=(2, 3), keepdims=True)
        var = jnp.mean(jnp.square(y - mu), axis=(2, 3), keepdims=True)
        y = (y - mu) * jax.lax.rsqrt(var + EPS)
        return jax.nn.leaky_relu(y, SLOPE)

    def _L2_attn_ref(x, w_qkv, b_qkv, w_proj, b_proj):
        import jax, jax.numpy as jnp
        import numpy as np
        B, N, C, H = (4, 1024, 128, 16)
        D = C // H
        b, n, c = x.shape
        qkv = x @ w_qkv + b_qkv
        qkv = qkv.reshape(b, n, 3, H, D)
        q = jnp.transpose(qkv[:, :, 0], (0, 2, 1, 3))
        k = jnp.transpose(qkv[:, :, 1], (0, 2, 1, 3))
        v = jnp.transpose(qkv[:, :, 2], (0, 2, 1, 3))
        attn = jnp.einsum('bhqd,bhkd->bhqk', q, k)
        attn = jax.nn.softmax(attn, axis=-1)
        out = jnp.einsum('bhqk,bhkd->bhqd', attn, v)
        out = jnp.transpose(out, (0, 2, 1, 3)).reshape(b, n, c)
        return out @ w_proj + b_proj

    def _L2_ffn_ref(input_embeddings, router_w, w1, b1, w2, b2):
        import jax, jax.numpy as jnp
        import numpy as np
        NUM_EXPERTS = 8
        TOP_K = 2
        B, S, D = (8, 4096, 128)

        def _moe(tokens, router_w, w1, b1, w2, b2):
            N = tokens.shape[0]
            E = router_w.shape[0]
            logits = tokens.astype(jnp.float32) @ router_w.astype(jnp.float32).T
            probs = jax.nn.softmax(logits, axis=-1)
            rw, re = jax.lax.top_k(probs, TOP_K)
            if TOP_K > 1:
                rw = rw / jnp.maximum(rw.sum(-1, keepdims=True), 1e-12)
            rw = rw.astype(tokens.dtype)
            combine = jnp.zeros((N, E), tokens.dtype).at[jnp.arange(N)[:, None], re].set(rw)
            out = tokens
            for e in range(E):
                h = jax.nn.gelu(tokens @ w1[e] + b1[e], approximate=False)
                y = h @ w2[e] + b2[e]
                out = out + combine[:, e:e + 1] * y
            return out
        b, s, d = input_embeddings.shape
        tokens = input_embeddings.reshape(b * s, d)
        return _moe(tokens, router_w, w1, b1, w2, b2).reshape(b, s, d)

    def _L3_attn_ref(x, gamma, beta):
        import jax, jax.numpy as jnp
        import numpy as np
        WINDOW = 16
        EPS = 1e-05
        B, N, D = x.shape
        w = WINDOW
        W = 2 * w + 1
        scale = D ** (-0.5)
        kv_pad = jnp.pad(x, ((0, 0), (w, w), (0, 0)))
        idx = jnp.arange(N)[:, None] + jnp.arange(W)[None, :]
        windows = kv_pad[:, idx]
        scores = jnp.einsum('bnd,bnwd->bnw', x, windows) * scale
        attn = jax.nn.softmax(scores, axis=-1)
        out = jnp.einsum('bnw,bnwd->bnd', attn, windows)
        mu = jnp.mean(out, axis=-1, keepdims=True)
        var = jnp.var(out, axis=-1, keepdims=True)
        out = (out - mu) * jax.lax.rsqrt(var + EPS) * gamma + beta
        return out

    def _L3_ffn_ref(x, router_w, w1, w2, w3):
        import jax, jax.numpy as jnp
        import numpy as np
        N_EXPERTS = 8
        TOP_K = 2
        B, T, C = x.shape
        flat = x.reshape(-1, C)
        logits = flat @ router_w.T
        probs = jax.nn.softmax(logits, axis=-1)
        topk_probs, topk_idx = jax.lax.top_k(probs, TOP_K)
        topk_probs = topk_probs / (jnp.sum(topk_probs, axis=-1, keepdims=True) + 1e-09)
        onehot = jax.nn.one_hot(topk_idx, N_EXPERTS, dtype=flat.dtype)
        gates = jnp.einsum('nk,nke->ne', topk_probs, onehot)
        h1 = jnp.einsum('nc,ehc->neh', flat, w1)
        h3 = jnp.einsum('nc,ehc->neh', flat, w3)
        h = jax.nn.silu(h1) * h3
        y = jnp.einsum('neh,ech->nec', h, w2)
        out = jnp.einsum('ne,nec->nc', gates, y)
        return out.reshape(B, T, C)

    def _gn(v, G=32, eps=1e-05):
        B_, C_, H_, W_ = v.shape
        g = v.reshape(B_, G, C_ // G, H_, W_)
        m = jnp.mean(g, axis=(2, 3, 4), keepdims=True)
        s = jnp.var(g, axis=(2, 3, 4), keepdims=True)
        return ((g - m) / jnp.sqrt(s + eps)).reshape(v.shape)

    def _ln_c(v, eps=1e-06):
        m = jnp.mean(v, axis=1, keepdims=True)
        s = jnp.var(v, axis=1, keepdims=True)
        return (v - m) / jnp.sqrt(s + eps)

    def _ln_t(v, eps=1e-05):
        m = jnp.mean(v, axis=-1, keepdims=True)
        s = jnp.var(v, axis=-1, keepdims=True)
        return (v - m) / jnp.sqrt(s + eps)

    def _to_tokens(v):
        B_, C_, H_, W_ = v.shape
        return v.reshape(B_, C_, H_ * W_).transpose(0, 2, 1)

    def _from_tokens(t, like):
        B_, C_, H_, W_ = like.shape
        return t.transpose(0, 2, 1).reshape(B_, C_, H_, W_)
    x = x + _L0_conv_ref(_gn(x), L0_conv_w_qkv, L0_conv_w_lepe, L0_conv_b_lepe)
    x = x + _L1_conv_ref(_gn(x), L1_conv_attn_w1, L1_conv_attn_w2, L1_conv_refine_w, L1_conv_refine_b)
    t = _to_tokens(x)
    t = t + _L2_attn_ref(_ln_t(t), L2_attn_w_qkv, L2_attn_b_qkv, L2_attn_w_proj, L2_attn_b_proj)
    t = t + _L2_ffn_ref(_ln_t(t), L2_ffn_router_w, L2_ffn_w1, L2_ffn_b1, L2_ffn_w2, L2_ffn_b2)
    t = t + _L3_attn_ref(_ln_t(t), L3_attn_gamma, L3_attn_beta)
    t = t + _L3_ffn_ref(_ln_t(t), L3_ffn_router_w, L3_ffn_w1, L3_ffn_w2, L3_ffn_w3)
    x = _from_tokens(t, x)
    return x

_drawn_inputs = setup_inputs


def setup_inputs(seed=0):
    import zlib

    import numpy as np

    out = dict(_drawn_inputs(seed))
    spreads = {'L2_attn_b_qkv': (0.0, 0.1),
     'L2_attn_b_proj': (0.0, 0.1),
     'L2_ffn_b1': (0.0, 0.297),
     'L2_ffn_b2': (0.0, 0.1),
     'L3_attn_gamma': (1.0, 0.2),
     'L3_attn_beta': (0.0, 0.1)}
    factors = {'L1_conv_attn_w1': 36.712, 'L1_conv_attn_w2': 41.007, 'L1_conv_refine_b': 64.0}
    for name, (base, spread) in spreads.items():
        noise = np.random.default_rng([zlib.crc32(name.encode()), seed]).standard_normal(out[name].shape)
        drawn = base * np.exp(spread * noise) if base else spread * noise
        out[name] = jnp.asarray(drawn.astype(out[name].dtype))
    for name, factor in factors.items():
        out[name] = (out[name] * factor).astype(out[name].dtype)
    return out
```

```python
from contextlib import ExitStack, contextmanager

import concourse.bass as bass
from concourse import mybir

F32 = mybir.dt.float32
BF16 = mybir.dt.bfloat16
ALU = mybir.AluOpType
ACT = mybir.ActivationFunctionType
AX = mybir.AxisListType

B, C, H, W = 8, 128, 32, 32
N = H * W
HALF = N // 2
D = 8
PARTS = 3
COMBOS = [(0, 0), (0, 1), (0, 2), (1, 0), (1, 1), (2, 0)]
STACK = len(COMBOS) * D
ROWS = STACK + PARTS
E = 8
HID = 341
HC = 3
BAND = 16
QT = C - 2 * BAND


def grant(nc, scratch, credits):
    for n, (sem, slots) in enumerate(credits):
        nc.vector.memset(scratch[0:1, n:n + 1], 0.0).then_inc(sem, slots)


class Chip:

    def __init__(self, nc):
        self.nc, self.n, self.sems = nc, 0, []

    @contextmanager
    def stage(self):
        outer, self.sems = self.sems, []
        with ExitStack() as ctx:
            yield ctx
        self.nc.clear_and_free_semaphores(self.sems)
        self.nc.all_engine_barrier()
        self.sems = outer

    def sem(self, name):
        self.n += 1
        self.sems.append(self.nc.alloc_semaphore(name=f"{name}_{self.n}"))
        return self.sems[-1]

    def buf(self, ctx, name, shape, dt=F32):
        self.n += 1
        return ctx.enter_context(self.nc.sbuf_tensor(f"{name}_{self.n}", shape, dt))

    def psum(self, ctx, name, shape, dt=F32):
        self.n += 1
        return ctx.enter_context(self.nc.psum_tensor(f"{name}_{self.n}", shape, dt))


def load_inputs(chip, x, X, consts):
    nc = chip.nc
    loaded = chip.sem("inputs_loaded")
    with nc.Block() as block:
        @block.sync
        def _(sp):
            for i in range(B):
                sp.dma_start(X[:, i, :], x[i].rearrange("c h w -> c (h w)")).then_inc(loaded, 16)
            for dst, src in consts:
                sp.dma_start(dst[:], src).then_inc(loaded, 16)
            sp.wait_ge(loaded, 16 * (B + len(consts)))


def group_norm_stats(chip, X, gn_avg, eps5, mean_g, rstd_g, pooled):
    nc = chip.nc
    with chip.stage() as ctx:
        st = chip.buf(ctx, "gn_st", [C, B, 12])
        mv = chip.buf(ctx, "gn_mv", [C, B, 2])
        dev = chip.buf(ctx, "gn_dev", [C, B])
        sq = chip.buf(ctx, "gn_sq", [C, B])
        sd = chip.buf(ctx, "gn_sd", [C, B])
        ps = chip.psum(ctx, "gn_ps", [C, 2, HALF])
        stats, aggr, avg, step, rooted = (chip.sem(s) for s in ("stats", "aggr", "avg", "dvestep", "rooted"))
        with nc.Block() as block:
            @block.vector
            def _(v):
                for i in range(B):
                    for c in range(2):
                        last = nc.vector.bn_stats(st[:, i, 6 * c:6 * c + 6], X[:, i, c * HALF:(c + 1) * HALF])
                    last.then_inc(stats, 1)
                for i in range(B):
                    v.wait_ge(stats, i + 1)
                    nc.vector.bn_aggr(mv[:, i, :], st[:, i, :]).then_inc(aggr, 1)
                v.wait_ge(aggr, B)
                v.wait_ge(avg, 1)
                nc.vector.tensor_copy(mean_g[:], ps[:, 0, 0:B]).then_inc(step, 1)
                nc.vector.tensor_tensor(dev[:], mv[:, :, 0], ps[:, 0, 0:B], ALU.subtract).then_inc(step, 1)
                v.wait_ge(step, 2)
                nc.vector.tensor_tensor(sq[:], dev[:], dev[:], ALU.mult).then_inc(step, 1)
                v.wait_ge(step, 3)
                nc.vector.tensor_tensor(sq[:], sq[:], mv[:, :, 1], ALU.add).then_inc(step, 1)
                v.wait_ge(rooted, 1)
                nc.vector.reciprocal(rstd_g[:], sd[:]).then_inc(step, 1)
                v.wait_ge(step, 5)
                nc.vector.tensor_tensor(pooled[:], dev[:], rstd_g[:], ALU.mult).then_inc(step, 1)

            @block.tensor
            def _(pe):
                pe.wait_ge(aggr, B)
                nc.tensor.matmul(ps[:, 0, 0:B], gn_avg[:], mv[:, :, 0], start=True, stop=True).then_inc(avg, 1)
                pe.wait_ge(step, 4)
                nc.tensor.matmul(ps[:, 1, 0:B], gn_avg[:], sq[:], start=True, stop=True).then_inc(avg, 1)

            @block.scalar
            def _(act):
                act.wait_ge(avg, 2)
                nc.scalar.activation(sd[:], ps[:, 1, 0:B], ACT.Sqrt, bias=eps5[:]).then_inc(rooted, 1)


def lepe_pieces(half):
    lo, hi = 16 * half, 16 * half + 16
    out = [(4, 2, lo, 16, lo)]
    for dh in (0, -1, 1):
        for dw in (-1, 0, 1):
            tap = (dh + 1) * 3 + dw + 1
            if tap == 4:
                continue
            if dh == 0:
                out.append((tap, 2, lo, 16, lo))
                continue
            r = lo
            while r < hi:
                src = r + dh
                if r == (31 if dh == 1 else 0):
                    kind = 1
                elif r == (1 if dh == 1 else 2):
                    kind = 0
                else:
                    kind = 2
                n = 1
                while kind == 2 and r + n < hi and r + n != (31 if dh == 1 else 0) and r + n != (1 if dh == 1 else 2):
                    n += 1
                out.append((tap, kind, r, n, src % H))
                r += n
    return out


def window_projections(chip, X, mean_g, rstd_g, dram, qk_scr, v_scr):
    nc = chip.nc
    U = 4
    with chip.stage() as ctx:
        wqk = chip.buf(ctx, "wqk", [C, 4, C])
        wv = chip.buf(ctx, "wv", [C, 4, 64])
        wl = chip.buf(ctx, "wl", [C, 2, C])
        taps = chip.buf(ctx, "taps", [C, 2, 9, C])
        wt = chip.buf(ctx, "wt", [C, 3, 9, C])
        bl = chip.buf(ctx, "bl", [C, 2])
        bsum = chip.buf(ctx, "bsum", [C, 1])
        scratch = chip.buf(ctx, "scratch", [1, 16])
        xn = chip.buf(ctx, "xn", [C, N + 64])
        xw = chip.buf(ctx, "xw", [C, N])
        xp = chip.buf(ctx, "xp", [C, H, W + 2])
        parts = chip.buf(ctx, "parts", [C, 2, PARTS, N], BF16)
        rest = chip.buf(ctx, "rest", [C, 2, N])
        vs = chip.buf(ctx, "vs", [C, 2, HALF])
        qk_ps = chip.psum(ctx, "qk_ps", [C, 2, N])
        v_ps = chip.psum(ctx, "v_ps", [C, 2, HALF])
        l_ps = chip.psum(ctx, "l_ps", [C, N])
        w_loaded, weights, normed, padded, edge, strips = (chip.sem(s) for s in (
            "w_loaded", "weights", "normed", "padded", "edge", "strips"))
        qk_ready, hi_done, rest_done, mid_done, lo_done = (chip.sem(s) for s in (
            "qk_ready", "hi_done", "rest_done", "mid_done", "lo_done"))
        v_ready, v_copied, l_ready, l_added = (chip.sem(s) for s in ("v_ready", "v_copied", "l_ready", "l_added"))
        parts_out = [chip.sem("parts_out") for _ in range(2)]
        v_out = [chip.sem("v_out") for _ in range(2)]
        with nc.Block() as block:
            @block.sync
            def _(sp):
                for dst, name in ((wqk, "w0_qk"), (wv, "w0_v"), (wl, "w0_lepe"), (bl, "b_lepe")):
                    sp.dma_start(dst[:], dram[name]).then_inc(w_loaded, 16)
                sp.dma_start(taps[:].rearrange("p s t c -> p (s t c)"),
                             dram["lepe_taps"].to_broadcast([C, 2 * 9 * C])).then_inc(w_loaded, 16)
                with sp.Fori(0, B) as i:
                    for u in range(U):
                        sp.wait_ge(lo_done, i * U + u + 3)
                        sp.dma_start(qk_scr[i, u].rearrange("a r t -> r a t"),
                                     parts[:, u % 2]).then_inc(parts_out[u % 2], 16)
                        sp.wait_ge(v_copied, i * U + u + 3)
                        sp.dma_start(v_scr[i, u], vs[:, u % 2]).then_inc(v_out[u % 2], 16)
                for s in (*parts_out, *v_out):
                    sp.wait_ge(s, 16 * (B * U // 2 + 1))

            @block.vector
            def _(v):
                grant(nc, scratch, [(rest_done, 2), (lo_done, 2), (v_copied, 2), (l_added, 1),
                                    (parts_out[0], 16), (parts_out[1], 16), (v_out[0], 16), (v_out[1], 16)])
                nc.vector.memset(xp[:], 0.0).then_inc(weights, 1)
                v.wait_ge(w_loaded, 16 * 5)
                for s in range(2):
                    nc.vector.tensor_tensor(wt[:, s], taps[:, s],
                                            wl[:, s].unsqueeze(1).to_broadcast([C, 9, C]), ALU.mult).then_inc(weights, 1)
                nc.vector.tensor_tensor(bsum[:], bl[:, 0:1], bl[:, 1:2], ALU.add).then_inc(weights, 1)
                v.wait_ge(weights, 4)
                nc.vector.tensor_tensor(wt[:, 2], wt[:, 0], wt[:, 1], ALU.add).then_inc(weights, 1)
                with v.Fori(0, B) as i:
                    nc.vector.tensor_scalar(xn[:, 0:N], X[:, i, :], mean_g[:, i, :], rstd_g[:, i, :],
                                            ALU.subtract, ALU.mult).then_inc(normed, 1)
                    v.wait_ge(normed, i + 1)
                    nc.vector.tensor_copy(xn[:, N:N + 64], xn[:, 0:64]).then_inc(edge, 1)
                    nc.vector.tensor_copy(xw[:].rearrange("p (n h w) -> p n h w", n=8, w=4),
                                          xn[:, 0:N].rearrange("p (h n w) -> p n h w", n=8, w=4)).then_inc(strips, 1)
                    for u in range(U):
                        v.wait_ge(hi_done, i * U + u + 1)
                        v.wait_ge(lo_done, i * U + u + 1)
                        nc.vector.tensor_tensor(rest[:, u % 2], qk_ps[:, u % 2], parts[:, u % 2, 0],
                                                ALU.subtract).then_inc(rest_done, 1)
                    v.wait_ge(l_ready, i + 1)
                    nc.vector.scalar_tensor_tensor(X[:, i, :], l_ps[:], bsum[:], X[:, i, :],
                                                   ALU.add, ALU.add).then_inc(l_added, 1)

            @block.gpsimd
            def _(pool):
                with pool.Fori(0, B) as i:
                    for u in range(U):
                        pool.wait_ge(mid_done, i * U + u + 1)
                        nc.gpsimd.tensor_tensor(parts[:, u % 2, 2], rest[:, u % 2], parts[:, u % 2, 1],
                                                ALU.subtract).then_inc(lo_done, 1)

            @block.scalar
            def _(act):
                act.wait_ge(weights, 1)
                with act.Fori(0, B) as i:
                    act.wait_ge(normed, i + 1)
                    nc.scalar.copy(xp[:, :, 1:W + 1],
                                   xn[:, 0:N].rearrange("p (h w) -> p h w", h=H)).then_inc(padded, 1)
                    for u in range(U):
                        act.wait_ge(qk_ready, i * U + u + 1)
                        act.wait_ge(parts_out[u % 2], (i * 2 + u // 2) * 16 + 16)
                        nc.scalar.copy(parts[:, u % 2, 0], qk_ps[:, u % 2]).then_inc(hi_done, 1)
                        act.wait_ge(v_ready, i * U + u + 1)
                        act.wait_ge(v_out[u % 2], (i * 2 + u // 2) * 16 + 16)
                        nc.scalar.copy(vs[:, u % 2], v_ps[:, u % 2]).then_inc(v_copied, 1)
                        act.wait_ge(rest_done, i * U + u + 3)
                        nc.scalar.copy(parts[:, u % 2, 1], rest[:, u % 2]).then_inc(mid_done, 1)

            @block.tensor
            def _(pe):
                pe.wait_ge(weights, 5)
                with pe.Fori(0, B) as i:
                    pe.wait_ge(strips, i + 1)
                    for u in range(U):
                        src = xw if u % 2 == 0 else xn
                        at = 64 if u == 3 else 0
                        if u == 1:
                            pe.wait_ge(edge, i + 1)
                        pe.wait_ge(rest_done, i * U + u + 1)
                        for c in range(2):
                            last = nc.tensor.matmul(qk_ps[:, u % 2, c * HALF:(c + 1) * HALF], wqk[:, u, :],
                                                    src[:, at + c * HALF:at + (c + 1) * HALF], start=True, stop=True)
                        last.then_inc(qk_ready, 1)
                        pe.wait_ge(v_copied, i * U + u + 1)
                        for w in range(8):
                            last = nc.tensor.matmul(v_ps[:, u % 2, w * 64:(w + 1) * 64],
                                                    src[:, at + w * C:at + (w + 1) * C], wv[:, u, :],
                                                    start=True, stop=True)
                        last.then_inc(v_ready, 1)
                    pe.wait_ge(padded, i + 1)
                    pe.wait_ge(l_added, i + 1)
                    for half in range(2):
                        pieces = lepe_pieces(half)
                        for n, (tap, kind, r, rows, r_in) in enumerate(pieces):
                            last = nc.tensor.matmul(
                                l_ps[:, r * W:(r + rows) * W], wt[:, kind, tap, :],
                                xp[:, r_in:r_in + rows, tap % 3:tap % 3 + W],
                                start=(n == 0), stop=(n == len(pieces) - 1))
                    last.then_inc(l_ready, 1)


def attention(chip, X, dram, qk_rows, v_scr, m_scr, ident, identf, sel, wout_name, bias, subs, kt_quads, scale, finals, reorder):
    nc = chip.nc
    windowed = kt_quads == 1
    QB = subs * kt_quads
    NQ = 4 * QB
    NG = 4 * subs
    HB = 4 * subs
    HP = 2 * subs
    LAST = B - 1

    def ends_output(q):
        return 0 <= q < NQ and q % kt_quads == kt_quads - 1

    def sel_at(q):
        return (q - 2) // kt_quads if ends_output(q - 2) else None

    def final_at(q):
        return (q - 3) // QB if 0 <= q - 3 < NQ and (q - 2) % QB == 0 else None

    def turn_at(q, blocks=4):
        return q // QB - 1 if q and q % QB == 0 and q // QB - 1 < blocks else None

    def uses(blocks):
        st, mx = {}, {}
        for q in range(NQ + 4):
            for j in range(4):
                if q < NQ:
                    st["exp", q, j] = len(st)
                    if q // QB < blocks:
                        for x in (2 * j, 2 * j + 1):
                            mx["max", q, x] = len(mx)
                if j == 1:
                    if turn_at(q, blocks) is not None:
                        for s in range(subs):
                            mx["turn", turn_at(q, blocks), s] = len(mx)
                    if sel_at(q) is not None:
                        st["den", sel_at(q)] = len(st)
                if j == 2 and final_at(q) is not None:
                    st["final", final_at(q)] = len(st)
                if j == 3 and sel_at(q) is not None:
                    st["spread", sel_at(q)] = len(st)
        return st, mx

    st_use, mx_uses = uses(4)
    mx_uses_last = uses(2)[1]
    ST, MX = len(st_use), len(mx_uses)
    assert ST % 2 == 0 and MX % 2 == 0
    MXB = 8 * QB + subs
    MX0 = 2 * MXB

    with chip.stage() as ctx:
        QS = chip.buf(ctx, "QS", [C, 4, HP, N], BF16)
        KS = chip.buf(ctx, "KS", [C, 4, HP, N], BF16)
        VS = chip.buf(ctx, "VS", [C, 2, 8, HB * D])
        VA = chip.buf(ctx, "VA", [C, 2, 8, HB, 32])
        PT = chip.buf(ctx, "PT", [C, 8, N])
        OR = chip.buf(ctx, "OR", [C, 2, N])
        RC = chip.buf(ctx, "RC", [C, 2, 8, 4])
        RW = chip.buf(ctx, "RW", [C, 2, 8, C])
        ON = chip.buf(ctx, "ON", [C, 2, subs, N])
        wout = chip.buf(ctx, "wout", [C, 4 * subs, C])
        unit = chip.buf(ctx, "unit", [C, 1])
        mxv = chip.buf(ctx, "mxv", [C, HB, 8, 1 if windowed else 2])
        nm = chip.buf(ctx, "nm", [C, HB * 8])
        nr = chip.buf(ctx, "nr", [C, 2, HB * 8])
        mp = chip.buf(ctx, "mp", [C, subs, PARTS, 32], BF16)
        mT = chip.buf(ctx, "mT", [PARTS * 32, subs, C], BF16)
        scratch = chip.buf(ctx, "scratch", [1, 16])
        st_ps = chip.psum(ctx, "st_ps", [C, 2, N])
        o_ps = chip.psum(ctx, "o_ps", [C, N])
        mx_ps = chip.psum(ctx, "mx_ps", [C, 2, HALF])
        qk_loaded = [chip.sem("qk_loaded") for _ in range(4)]
        rows_loaded = [chip.sem("rows_loaded") for _ in range(4)]
        v_loaded = [chip.sem("v_loaded") for _ in range(2)]
        st_free = [chip.sem("st_free") for _ in range(2)]
        (w_loaded, filled, rows_out, st_ready, mx_ready, mx_free, pv_done, o_free, va_done, max_taken,
         split, widened) = (chip.sem(s) for s in (
             "w_loaded", "filled", "rows_out", "st_ready", "mx_ready", "mx_free", "pv_done", "o_free",
             "va_done", "max_taken", "split", "widened"))
        QK_DMAS = 2 * 2 * len(COMBOS)

        def st_used(i, use):
            return i * ST + use + 1

        def st_wait(use):
            return st_free[use % 2], ST // 2, use // 2 + 2

        with nc.Block() as block:
            @block.sync
            def _(sp):
                def load_qk(i, k):
                    for o, dst in enumerate((QS, KS)):
                        for c, combo in enumerate(COMBOS):
                            rows = qk_rows(i, k, o)[combo[o]].rearrange("(hp e d) t -> e d hp t", e=2, d=D)
                            for e in range(2):
                                at = 64 * e + D * c
                                sp.dma_start(dst[at:at + D, k], rows[e]).then_inc(qk_loaded[k], 16)

                def load_v(i, k, slot):
                    sp.dma_start(VS[:, slot].rearrange("p t c -> p (t c)"), v_scr[i, k]).then_inc(v_loaded[slot], 16)

                def load_rows(k, half, copies, written):
                    sp.wait_ge(mx_free, copies)
                    for s in range(subs):
                        sp.dma_start(m_scr[half, s].rearrange("a h t q -> (a h t) q"), mT[:, s]).then_inc(rows_out, 16)
                    sp.wait_ge(rows_out, written)
                    for s in range(subs):
                        src = m_scr[half, s].rearrange("a (hp e) t q -> e a hp (t q)", e=2)
                        for e in range(2):
                            sp.dma_start(QS[64 * e + STACK:64 * e + ROWS, k, 2 * s:2 * s + 2, :],
                                         src[e]).then_inc(rows_loaded[k], 16)

                sp.dma_start(wout[:].rearrange("p a c -> p (a c)"), dram[wout_name]).then_inc(w_loaded, 16)
                sp.wait_ge(filled, 3)
                load_v(0, 0, 0)
                load_v(0, 1, 1)
                for k in range(4):
                    load_qk(0, k)
                sp.wait_ge(va_done, 1)
                load_v(0, 2, 0)
                for k in range(2):
                    load_rows(k, k, (k + 1) * MXB + 2, 16 * subs * (k + 1))

                def image(i, last):
                    mx_use = mx_uses_last if last else mx_uses
                    for k in range(4):
                        if turn_at(k * QB) is not None:
                            if not last or k - 1 < 2:
                                load_rows((k + 1) % 4, (k + 1) % 2, i * MX + (MX0 + 2 + 1 + mx_use["turn", k - 1, subs - 1]),
                                          (i * 4 + k - 1) * (16 * subs) + 16 * subs * 3)
                        if not last:
                            sp.wait_ge(st_ready, st_used(i, st_use["exp", (k + 1) * QB - 1, 3]))
                            load_qk(i + 1, k)
                        if not last or k == 0:
                            sp.wait_ge(va_done, i * 4 + k + 2)
                            load_v(i + (k + 3) // 4, (k + 3) % 4, (k + 3) % 2)
                    if not last:
                        load_rows(1, 1, i * MX + (MX0 + 2 + 1 + mx_use["turn", 3, subs - 1]),
                                  (i * 4 + 3) * (16 * subs) + 16 * subs * 3)

                with sp.Fori(0, LAST) as i:
                    image(i, False)
                image(LAST, True)

            @block.tensor
            def _(pe):
                def stack(buf, k, h, rows):
                    e = h % 2
                    return buf[64 * e:64 * e + rows, k, h // 2, :]

                def max_scores(k, n, slot):
                    if windowed:
                        q, kk = (stack(b, k, n // 2, STACK) for b in (QS, KS))
                        for w in range(4):
                            at = ((n % 2) * 4 + w) * C
                            mm = nc.tensor.matmul(mx_ps[:, slot, w * C:(w + 1) * C], q[:, at:at + C], kk[:, at:at + C],
                                                  start=True, stop=True)
                    else:
                        q, kk = (stack(b, k, n // 16, STACK) for b in (QS, KS))
                        at = (n // 2 % 8) * C
                        mm = nc.tensor.matmul(mx_ps[:, slot, :], q[:, at:at + C],
                                              kk[:, (n % 2) * HALF:(n % 2 + 1) * HALF], start=True, stop=True)
                    mm.then_inc(mx_ready, 1)

                def turn(s, slot):
                    nc.tensor.transpose(mx_ps[0:PARTS * 32, slot, 0:C // 2].bitcast(BF16), mp[:, s].rearrange("p a c -> p (a c)"),
                                        ident[:]).then_inc(mx_ready, 1)

                pe.wait_ge(filled, 3)
                for k in range(2):
                    pe.wait_ge(qk_loaded[k], 16 * QK_DMAS)
                    for n in range(8 * QB):
                        pe.wait_ge(mx_free, k * MXB + n + 1)
                        max_scores(k, n, (k * MXB + n) % 2)
                    pe.wait_ge(split, 4 * (k + 1))
                    for s in range(subs):
                        pe.wait_ge(mx_free, k * MXB + 8 * QB + s + 1)
                        turn(s, (k * MXB + 8 * QB + s) % 2)

                def image(i, last):
                    mx_use = mx_uses_last if last else mx_uses
                    for q in range(NQ + 4):
                        k, s, kt = q // QB, q // kt_quads % subs, q % kt_quads
                        for j in range(4):
                            if q < NQ:
                                if q % QB == 0 and j == 0:
                                    pe.wait_ge(qk_loaded[k], (i + 1) * (16 * QK_DMAS))
                                    pe.wait_ge(rows_loaded[k], (i + 1) * (16 * 2 * subs))
                                use = st_use["exp", q, j]
                                sem, per, _ = st_wait(use)
                                pe.wait_ge(sem, i * per + use // 2 + 1)
                                qq, kk = (stack(b, k, 4 * s + j, ROWS) for b in (QS, KS))
                                if windowed:
                                    for w in range(8):
                                        mm = nc.tensor.matmul(st_ps[:, use % 2, w * C:(w + 1) * C], kk[:, w * C:(w + 1) * C],
                                                              qq[:, w * C:(w + 1) * C], start=True, stop=True)
                                else:
                                    for c in range(2):
                                        mm = nc.tensor.matmul(st_ps[:, use % 2, c * HALF:(c + 1) * HALF],
                                                              kk[:, kt * C:(kt + 1) * C],
                                                              qq[:, c * HALF:(c + 1) * HALF], start=True, stop=True)
                                mm.then_inc(st_ready, 1)
                                if not last or k < 2:
                                    target = (k + 2) % 4
                                    if q % QB == 0 and j == 0:
                                        pe.wait_ge(qk_loaded[target], (i + (1 if k < 2 else 2)) * (16 * QK_DMAS))
                                    for x in (2 * j, 2 * j + 1):
                                        pe.wait_ge(mx_free, i * MX + (MX0 + mx_use["max", q, x] + 1))
                                        max_scores(target, (q % QB) * 8 + x, mx_use["max", q, x] % 2)
                            if j == 1 and 1 <= q <= NQ:
                                p = q - 1
                                k1, s1, kt1 = p // QB, p // kt_quads % subs, p % kt_quads
                                if p % QB == 0:
                                    pe.wait_ge(va_done, i * 4 + k1 + 1)
                                if kt1 == 0:
                                    pe.wait_ge(o_free, i * NG + p // kt_quads + 1)
                                slots = {st_use["exp", p, jj] % 2: st_use["exp", p, jj] for jj in range(4)}
                                for use in slots.values():
                                    sem, per, val = st_wait(use)
                                    pe.wait_ge(sem, i * per + val)
                                width = C if windowed else HALF
                                for t in range(8 if windowed else 2):
                                    for jj in range(4):
                                        mm = nc.tensor.matmul(
                                            o_ps[32 * jj:32 * jj + 32, t * width:(t + 1) * width],
                                            VA[:, k1 % 2, t if windowed else kt1, 4 * s1 + jj, :],
                                            PT[:, (p % 2) * 4 + jj, t * width:(t + 1) * width],
                                            start=(kt1 == 0), stop=(kt1 == kt_quads - 1))
                                mm.then_inc(pv_done, 1)
                            if j == 1 and turn_at(q, 2 if last else 4) is not None:
                                m = turn_at(q)
                                pe.wait_ge(split, i * 16 + 4 * (2 + m + 1))
                                for s2 in range(subs):
                                    use = mx_use["turn", m, s2]
                                    pe.wait_ge(mx_free, i * MX + (MX0 + use + 1))
                                    turn(s2, use % 2)
                            if j == 1 and sel_at(q) is not None:
                                g = sel_at(q)
                                use = st_use["den", g]
                                sem, per, _ = st_wait(use)
                                pe.wait_ge(o_free, i * NG + g + 2)
                                pe.wait_ge(sem, i * per + use // 2 + 1)
                                for t in range(8):
                                    mm = nc.tensor.matmul(st_ps[:, use % 2, 4 * t:4 * t + 4], OR[:, g % 2, t * C:(t + 1) * C],
                                                          sel[:], start=True, stop=True)
                                mm.then_inc(st_ready, 1)
                            if j == 2 and final_at(q) is not None:
                                f = final_at(q)
                                use = st_use["final", f]
                                sem, per, _ = st_wait(use)
                                on_sem, on_per, on_val = st_wait(st_use["spread", (f + 1) * subs - 1])
                                if on_sem is not sem:
                                    pe.wait_ge(on_sem, i * on_per + on_val)
                                pe.wait_ge(sem, i * per + use // 2 + 1)
                                if f == 0 and q < NQ:
                                    pe.wait_ge(w_loaded, 16)
                                for dst, src, width in finals(f):
                                    for s2 in range(subs):
                                        mm = nc.tensor.matmul(st_ps[:, use % 2, dst:dst + width], wout[:, f * subs + s2, :],
                                                              ON[:, f % 2, s2, src:src + width],
                                                              start=(s2 == 0), stop=(s2 == subs - 1))
                                mm.then_inc(st_ready, 1)
                            if j == 3 and sel_at(q) is not None:
                                g = sel_at(q)
                                use = st_use["spread", g]
                                sem, per, _ = st_wait(use)
                                pe.wait_ge(widened, i * NG + g + 1)
                                pe.wait_ge(sem, i * per + use // 2 + 1)
                                for t in range(8):
                                    mm = nc.tensor.matmul(st_ps[:, use % 2, t * C:(t + 1) * C],
                                                          RW[:, g % 2, t, :], identf[:], start=True, stop=True)
                                mm.then_inc(st_ready, 1)

                with pe.Fori(0, LAST) as i:
                    image(i, False)
                image(LAST, True)

            @block.scalar
            def _(act):
                def image(i):
                    for q in range(NQ + 4):
                        for j in range(4):
                            if q < NQ:
                                use = st_use["exp", q, j]
                                act.wait_ge(st_ready, st_used(i, use))
                                act.wait_ge(pv_done, i * NQ + q + 1)
                                nc.scalar.activation(PT[:, (q % 2) * 4 + j], st_ps[:, use % 2], ACT.Exp,
                                                     scale=scale).then_inc(st_free[use % 2], 1)
                            if j == 1 and ends_output(q - 1):
                                g = (q - 1) // kt_quads
                                act.wait_ge(pv_done, i * NQ + q + 2)
                                if g >= 2:
                                    sem, per, val = st_wait(st_use["spread", g - 2])
                                    act.wait_ge(sem, i * per + val)
                                nc.scalar.copy(OR[:, g % 2], o_ps[:]).then_inc(o_free, 1)

                with act.Fori(0, B) as i:
                    image(i)

            @block.vector
            def _(v):
                nc.vector.memset(QS[:], 1.0).then_inc(filled, 1)
                nc.vector.memset(KS[:], 1.0).then_inc(filled, 1)
                nc.vector.memset(VA[:], 0.0).then_inc(filled, 1)
                v.wait_ge(filled, 3)
                nc.vector.memset(unit[:], 1.0)
                nc.vector.memset(VA[:, :, :, :, D:D + 1], 1.0).then_inc(filled, 1)
                grant(nc, scratch, [(st_free[0], 1), (st_free[1], 1), (mx_free, 2), (pv_done, 2), (o_free, 1)])

                def reduce_half(n, slot):
                    if windowed:
                        nc.vector.tensor_reduce(mxv[:, n // 2, (n % 2) * 4:(n % 2) * 4 + 4, 0],
                                                mx_ps[:, slot].rearrange("p (w k) -> p w k", w=4),
                                                AX.X, ALU.max).then_inc(mx_free, 1)
                    else:
                        nc.vector.tensor_reduce(mxv[:, n // 16, n // 2 % 8, n % 2:n % 2 + 1], mx_ps[:, slot],
                                                AX.X, ALU.max).then_inc(mx_free, 1)

                def take_max(freed):
                    v.wait_ge(mx_free, freed)
                    nc.vector.tensor_reduce(nm[:], mxv[:].rearrange("p h t c -> p (h t) c"), AX.X, ALU.max,
                                            negate=True).then_inc(max_taken, 1)

                def copy_turned(s, slot):
                    nc.vector.tensor_copy(mT[:, s], mx_ps[0:PARTS * 32, slot, 0:C // 2].bitcast(BF16)).then_inc(mx_free, 1)

                for k in range(2):
                    if k:
                        v.wait_ge(max_taken, k)
                    for n in range(8 * QB):
                        v.wait_ge(mx_ready, k * MXB + n + 1)
                        reduce_half(n, (k * MXB + n) % 2)
                    take_max(k * MXB + 8 * QB + 2)
                    if k:
                        v.wait_ge(rows_out, 16 * subs * k)
                    for s in range(subs):
                        use = k * MXB + 8 * QB + s
                        v.wait_ge(mx_ready, use + 1)
                        copy_turned(s, use % 2)

                def image(i, last):
                    mx_use = mx_uses_last if last else mx_uses
                    for q in range(NQ + 4):
                        k = q // QB
                        for j in range(4):
                            if q < NQ and (not last or k < 2):
                                if q % QB == 0 and j == 0:
                                    v.wait_ge(max_taken, i * 4 + k + 2)
                                for x in (2 * j, 2 * j + 1):
                                    v.wait_ge(mx_ready, i * MX + (MX0 + mx_use["max", q, x] + 1))
                                    reduce_half((q % QB) * 8 + x, mx_use["max", q, x] % 2)
                            if j == 1 and turn_at(q, 2 if last else 4) is not None:
                                m = turn_at(q)
                                v.wait_ge(rows_out, (i * 4 + m) * (16 * subs) + 16 * subs * 2)
                                for s in range(subs):
                                    use = mx_use["turn", m, s]
                                    v.wait_ge(mx_ready, i * MX + (MX0 + use + 1))
                                    copy_turned(s, use % 2)
                            if j == 1 and sel_at(q) is not None:
                                g = sel_at(q)
                                use = st_use["den", g]
                                v.wait_ge(st_ready, st_used(i, use))
                                nc.vector.reciprocal(RC[:, g % 2].rearrange("p t j -> p (t j)"),
                                                     st_ps[:, use % 2, 0:32]).then_inc(st_free[use % 2], 1)
                            if j == 2 and final_at(q) is not None:
                                f = final_at(q)
                                use = st_use["final", f]
                                v.wait_ge(st_ready, st_used(i, use))
                                if bias is not None and f == 0:
                                    nc.vector.scalar_tensor_tensor(X[:, i, :], st_ps[:, use % 2], bias[:], X[:, i, :],
                                                                   ALU.add, ALU.add).then_inc(st_free[use % 2], 1)
                                else:
                                    nc.vector.tensor_tensor(X[:, i, :], st_ps[:, use % 2], X[:, i, :],
                                                            ALU.add).then_inc(st_free[use % 2], 1)
                            if j == 3 and sel_at(q) is not None:
                                g = sel_at(q)
                                use = st_use["spread", g]
                                v.wait_ge(st_ready, st_used(i, use))
                                src, rec, dst = OR[:, g % 2], st_ps[:, use % 2], ON[:, (g // subs) % 2, g % subs]
                                if reorder and (g // subs) % 2 == 0:
                                    src, rec = (a.rearrange("p (n h w) -> p n h w", n=8, w=4) for a in (src, rec))
                                    dst = dst.rearrange("p (h n w) -> p n h w", n=8, w=4)
                                nc.vector.tensor_tensor(dst, rec, src, ALU.mult).then_inc(st_free[use % 2], 1)
                        if q < NQ and (q + 1) % QB == 0 and (not last or k < 2):
                            take_max(i * MX + (MX0 + 2 + mx_use["max", q, 7] + 1))

                with v.Fori(0, LAST) as i:
                    image(i, False)
                image(LAST, True)

            @block.gpsimd
            def _(pool):
                def copy(dst, src):
                    one = unit[:]
                    while len(one.shape) < len(src.shape):
                        one = one.unsqueeze(1)
                    return nc.gpsimd.tensor_tensor(dst, src, one.to_broadcast(list(src.shape)), ALU.mult)

                def expand_v(k, slot):
                    copy(VA[:, slot, :, :, 0:D], VS[:, slot].rearrange("p t (h d) -> p t h d", d=D)).then_inc(va_done, 1)

                def widen(i, g):
                    sem, per, val = st_wait(st_use["den", g])
                    pool.wait_ge(sem, i * per + val)
                    nc.gpsimd.tensor_tensor(RW[:, g % 2].rearrange("p t (j r) -> p (t j) r", r=32),
                                            RC[:, g % 2].rearrange("p t j -> p (t j)").unsqueeze(2).to_broadcast([C, 32, 32]),
                                            unit[:].unsqueeze(1).to_broadcast([C, 32, 32]), ALU.mult).then_inc(widened, 1)

                def split_max(taken, base):
                    view = nm[:].rearrange("p (s c) -> p s c", s=subs)
                    rv = [nr[:, n].rearrange("p (s c) -> p s c", s=subs) for n in range(2)]
                    pool.wait_ge(max_taken, taken)
                    copy(mp[:, :, 0], view).then_inc(split, 1)
                    pool.wait_ge(split, base + 1)
                    nc.gpsimd.tensor_tensor(rv[0], view, mp[:, :, 0], ALU.subtract).then_inc(split, 1)
                    pool.wait_ge(split, base + 2)
                    copy(mp[:, :, 1], rv[0]).then_inc(split, 1)
                    pool.wait_ge(split, base + 3)
                    nc.gpsimd.tensor_tensor(mp[:, :, 2], rv[0], mp[:, :, 1], ALU.subtract).then_inc(split, 1)

                pool.wait_ge(filled, 4)
                pool.wait_ge(v_loaded[0], 16)
                expand_v(0, 0)
                for k in range(2):
                    split_max(k + 1, 4 * k)

                def image(i, last):
                    mx_use = mx_uses_last if last else mx_uses
                    for q in range(NQ + 4):
                        k = q // QB
                        if q < NQ and q % QB == 1 and (not last or k < 3):
                            pool.wait_ge(v_loaded[(k + 1) % 2], (i * 2 + (k + 1) // 2) * 16 + 16)
                            pool.wait_ge(pv_done, i * NQ + k * QB + 2)
                            expand_v((k + 1) % 4, (k + 1) % 2)
                        if sel_at(q) is not None:
                            widen(i, sel_at(q))
                        if q < NQ and (q + 1) % QB == 0 and (not last or k < 2):
                            split_max(i * 4 + k + 3, i * 16 + 4 * (2 + k))

                with pool.Fori(0, LAST) as i:
                    image(i, False)
                image(LAST, True)


PE_TAPS = (0, 1, 2, 3, 5, 6)


def conv_stage(chip, X, dram, mean_g, rstd_g, pooled, eps5, identf):
    nc = chip.nc
    VE_TAPS = [t for t in range(9) if t not in PE_TAPS]
    with chip.stage() as ctx:
        w1, w2 = chip.buf(ctx, "se_w1", [C, C // 4]), chip.buf(ctx, "se_w2", [C // 4, C])
        rw, rb = chip.buf(ctx, "rw", [C, 9]), chip.buf(ctx, "rb", [C, 1])
        diag = chip.buf(ctx, "diag", [C, len(PE_TAPS), C])
        h, hl = chip.buf(ctx, "se_h", [C // 4, B]), chip.buf(ctx, "se_hl", [C // 4, B])
        gate = chip.buf(ctx, "se_gate", [C, B])
        scale = chip.buf(ctx, "scale", [C, B, 1])
        xp = chip.buf(ctx, "xp", [C, 2, H + 2, W + 2])
        acc, z = chip.buf(ctx, "acc", [C, 2, N]), chip.buf(ctx, "z", [C, 2, N])
        st, mv = chip.buf(ctx, "st", [C, 2, 12]), chip.buf(ctx, "mv", [C, 2, 2])
        sd, rs, nb, pause = (chip.buf(ctx, n, [C, 2, 1]) for n in ("sd", "rs", "nb", "pause"))
        scratch = chip.buf(ctx, "scratch", [1, 8])
        ps = chip.psum(ctx, "se_ps", [C, 2, HALF])
        c_ps = chip.psum(ctx, "c_ps", [C, 2, N])
        w_loaded, squeezed, chain, gated, padded, conv, aggr, rooted, scaled, ascaled, added = (chip.sem(s) for s in (
            "w_loaded", "squeezed", "chain", "gated", "padded", "conv", "aggr", "rooted", "scaled", "ascaled", "added"))
        with nc.Block() as block:
            @block.sync
            def _(sp):
                for dst, name in ((w1, "se_w1"), (w2, "se_w2"), (rw, "refine_w"), (rb, "refine_b")):
                    sp.dma_start(dst[:], dram[name]).then_inc(w_loaded, 16)
                sp.wait_ge(w_loaded, 64)

            @block.tensor
            def _(pe):
                pe.wait_ge(w_loaded, 64)
                nc.tensor.matmul(ps[0:C // 4, 0, 0:B], w1[:], pooled[:], start=True, stop=True).then_inc(squeezed, 1)
                pe.wait_ge(chain, 4)
                nc.tensor.matmul(ps[:, 1, 0:B], w2[:], hl[:], start=True, stop=True).then_inc(squeezed, 1)
                with pe.Fori(0, B // 2) as i:
                    for s in range(2):
                        pe.wait_ge(padded, i * 2 + s + 1)
                        pe.wait_ge(added, i * 2 + s + 1)
                        for half in range(2):
                            for n, t in enumerate(PE_TAPS):
                                r = 16 * half + t // 3
                                mm = nc.tensor.matmul(c_ps[:, s, half * HALF:(half + 1) * HALF], diag[:, n, :],
                                                      xp[:, s, r:r + 16, t % 3:t % 3 + W],
                                                      start=(n == 0), stop=(n == len(PE_TAPS) - 1))
                        mm.then_inc(conv, 1)

            @block.scalar
            def _(act):
                act.wait_ge(squeezed, 2)
                nc.scalar.activation(gate[:], ps[:, 1, 0:B], ACT.Sigmoid).then_inc(gated, 1)
                with act.Fori(0, B // 2) as i:
                    for s in range(2):
                        act.wait_ge(aggr, i * 2 + s + 1)
                        nc.scalar.activation(sd[:, s], mv[:, s, 1:2], ACT.Sqrt, bias=eps5[:]).then_inc(rooted, 1)
                    for s in range(2):
                        act.wait_ge(scaled, i * 2 + s + 1)
                        nc.scalar.activation(z[:, s], acc[:, s], ACT.Identity, bias=nb[:, s], scale=rs[:, s]).then_inc(ascaled, 1)

            @block.vector
            def _(v):
                count = [0]

                def chained(ins):
                    count[0] += 1
                    ins.then_inc(chain, 1)
                    v.wait_ge(chain, count[0])

                grant(nc, scratch, [(added, 2)])
                chained(nc.vector.memset(xp[:], 0.0))
                v.wait_ge(w_loaded, 64)
                for n, t in enumerate(PE_TAPS):
                    ins = nc.vector.tensor_scalar(diag[:, n, :], identf[:], rw[:, t:t + 1], None, ALU.mult)
                chained(ins)
                v.wait_ge(squeezed, 1)
                chained(nc.vector.tensor_copy(h[:], ps[0:C // 4, 0, 0:B]))
                chained(nc.vector.scalar_tensor_tensor(hl[:], h[:], 0.01, h[:], ALU.mult, ALU.max))
                v.wait_ge(gated, 1)
                chained(nc.vector.tensor_tensor(scale[:].rearrange("p b o -> p (b o)"), gate[:],
                                                rstd_g[:].rearrange("p b o -> p (b o)"), ALU.mult))
                base = count[0]
                STEPS = len(VE_TAPS) + 4
                with v.Fori(0, B // 2) as i:
                    step = [0]

                    def then(ins):
                        step[0] += 1
                        ins.then_inc(chain, 1)
                        return step[0]

                    def after(n):
                        v.wait_ge(chain, i * (2 * STEPS) + (base + n))

                    done = [0, 0]
                    for s in range(2):
                        nc.vector.tensor_scalar(xp[:, s, 1:H + 1, 1:W + 1],
                                                X[:, i * 2 + s, :].rearrange("p (h w) -> p h w", h=H),
                                                mean_g[:, i * 2 + s, :], scale[:, i * 2 + s, :],
                                                ALU.subtract, ALU.mult).then_inc(padded, 1)
                    for s in range(2):
                        v.wait_ge(padded, i * 2 + s + 1)
                        t = VE_TAPS[0]
                        done[s] = then(nc.vector.tensor_scalar(
                            acc[:, s].rearrange("p (h w) -> p h w", h=H), xp[:, s, t // 3:t // 3 + H, t % 3:t % 3 + W],
                            rw[:, t:t + 1], rb[:], ALU.mult, ALU.add))
                    for t in VE_TAPS[1:]:
                        for s in range(2):
                            after(done[s])
                            src = xp[:, s, t // 3:t // 3 + H, t % 3:t % 3 + W]
                            out = acc[:, s].rearrange("p (h w) -> p h w", h=H)
                            done[s] = then(nc.vector.scalar_tensor_tensor(out, src, rw[:, t:t + 1], out, ALU.mult, ALU.add))
                    for s in range(2):
                        v.wait_ge(conv, i * 2 + s + 1)
                        after(done[s])
                        done[s] = then(nc.vector.tensor_tensor(acc[:, s], c_ps[:, s], acc[:, s], ALU.add))
                    for s in range(2):
                        after(done[s])
                        for c in range(2):
                            ins = nc.vector.bn_stats(st[:, s, 6 * c:6 * c + 6], acc[:, s, c * HALF:(c + 1) * HALF])
                        done[s] = then(ins)
                    for s in range(2):
                        after(done[s])
                        nc.vector.memset(pause[:, s], 0.0)
                        nc.vector.bn_aggr(mv[:, s], st[:, s]).then_inc(aggr, 1)
                    for s in range(2):
                        v.wait_ge(rooted, i * 2 + s + 1)
                        done[s] = then(nc.vector.reciprocal(rs[:, s], sd[:, s]))
                    for s in range(2):
                        after(done[s])
                        nc.vector.scalar_tensor_tensor(nb[:, s], mv[:, s, 0:1], -1.0, rs[:, s],
                                                       ALU.mult, ALU.mult).then_inc(scaled, 1)
                    for s in range(2):
                        v.wait_ge(ascaled, i * 2 + s + 1)
                        done[s] = then(nc.vector.scalar_tensor_tensor(z[:, s], z[:, s], 0.01, z[:, s], ALU.mult, ALU.max))
                    for s in range(2):
                        after(done[s])
                        nc.vector.tensor_tensor(X[:, i * 2 + s, :], X[:, i * 2 + s, :], z[:, s], ALU.add).then_inc(added, 1)
                    assert step[0] == 2 * STEPS, step[0]


def layer_norm(chip, src, mean_w, eps5, identf, dst=None, X=None, gamma=None, beta=None):
    nc = chip.nc
    TILES = HALF // C
    with chip.stage() as ctx:
        xc, sq, t = (chip.buf(ctx, n, [C, 2, HALF]) for n in ("xc", "sq", "t"))
        sd, rs = (chip.buf(ctx, n, [C, 2, TILES]) for n in ("sd", "rs"))
        scratch = chip.buf(ctx, "scratch", [1, 8])
        m_ps, v_ps, r_ps = (chip.psum(ctx, n, [C, 2, HALF]) for n in ("m_ps", "v_ps", "r_ps"))
        mean_ready, centred, squared, var_ready, rooted, inverted, spread, scaled, stored = (chip.sem(s) for s in (
            "mean_ready", "centred", "squared", "var_ready", "rooted", "inverted", "spread", "scaled", "stored"))
        with nc.Block() as block:
            @block.tensor
            def _(pe):
                with pe.Fori(0, B) as i:
                    for c in range(2):
                        pe.wait_ge(centred, i * 2 + c + 1)
                        nc.tensor.matmul(m_ps[:, c], mean_w[:], src[:, i, c * HALF:(c + 1) * HALF],
                                         start=True, stop=True).then_inc(mean_ready, 1)
                    for c in range(2):
                        pe.wait_ge(squared, i * 2 + c + 1)
                        pe.wait_ge(rooted, i * 2 + c + 1)
                        for n in range(TILES):
                            mm = nc.tensor.matmul(v_ps[:, c, n:n + 1], sq[:, c, n * C:(n + 1) * C], mean_w[:, 0:1],
                                                  start=True, stop=True)
                        mm.then_inc(var_ready, 1)
                    for c in range(2):
                        pe.wait_ge(inverted, i * 2 + c + 1)
                        pe.wait_ge(scaled, i * 2 + c + 1)
                        for n in range(TILES):
                            mm = nc.tensor.matmul(r_ps[:, c, n * C:(n + 1) * C],
                                                  rs[:, c, n:n + 1].to_broadcast([C, C]), identf[:], start=True, stop=True)
                        mm.then_inc(spread, 1)

            @block.scalar
            def _(act):
                with act.Fori(0, B) as i:
                    for c in range(2):
                        act.wait_ge(centred, i * 2 + c + 3)
                        act.wait_ge(var_ready, i * 2 + c + 1)
                        nc.scalar.activation(sq[:, c], xc[:, c], ACT.Square).then_inc(squared, 1)
                    for c in range(2):
                        act.wait_ge(var_ready, i * 2 + c + 3)
                        nc.scalar.activation(sd[:, c], v_ps[:, c, 0:TILES], ACT.Sqrt, bias=eps5[:]).then_inc(rooted, 1)

            @block.vector
            def _(v):
                grant(nc, scratch, [(centred, 2), (rooted, 2), (var_ready, 2), (scaled, 2)])
                with v.Fori(0, B) as i:
                    for c in range(2):
                        v.wait_ge(mean_ready, i * 2 + c + 1)
                        v.wait_ge(scaled, i * 2 + c + 1)
                        nc.vector.tensor_tensor(xc[:, c], src[:, i, c * HALF:(c + 1) * HALF], m_ps[:, c],
                                                ALU.subtract).then_inc(centred, 1)
                    for c in range(2):
                        v.wait_ge(rooted, i * 2 + c + 3)
                        nc.vector.reciprocal(rs[:, c], sd[:, c]).then_inc(inverted, 1)
                    for c in range(2):
                        v.wait_ge(spread, i * 2 + c + 1)
                        if dst is not None:
                            nc.vector.tensor_tensor(dst[:, i, c * HALF:(c + 1) * HALF], xc[:, c], r_ps[:, c],
                                                    ALU.mult).then_inc(scaled, 1)
                            continue
                        nc.vector.scalar_tensor_tensor(t[:, c], xc[:, c], gamma[:], r_ps[:, c],
                                                       ALU.mult, ALU.mult).then_inc(scaled, 1)
                        v.wait_ge(scaled, i * 2 + c + 3)
                        at = X[:, i, c * HALF:(c + 1) * HALF]
                        nc.vector.scalar_tensor_tensor(at, t[:, c], beta[:], at, ALU.add, ALU.add).then_inc(stored, 1)


def token_projections(chip, XN, dram, qk_scr, v_scr):
    nc = chip.nc
    with chip.stage() as ctx:
        wqk, wv = chip.buf(ctx, "wqk", [C, 2, C]), chip.buf(ctx, "wv", [C, C])
        bqk, bv = chip.buf(ctx, "bqk", [C, 2]), chip.buf(ctx, "bv", [C, C])
        xs = chip.buf(ctx, "xs", [C, N])
        parts = chip.buf(ctx, "parts", [C, 2, PARTS, N], BF16)
        rest = chip.buf(ctx, "rest", [C, 2, N])
        vs = chip.buf(ctx, "vs", [C, 4, 8, 32])
        scratch = chip.buf(ctx, "scratch", [1, 8])
        qk_ps = chip.psum(ctx, "qk_ps", [C, 2, N])
        v_ps = chip.psum(ctx, "v_ps", [C, 8, C])
        w_loaded, staged, qk_ready, hi_done, rest_done, mid_done, lo_done, v_ready, v_copied, v_out = (
            chip.sem(s) for s in ("w_loaded", "staged", "qk_ready", "hi_done", "rest_done", "mid_done", "lo_done",
                                  "v_ready", "v_copied", "v_out"))
        parts_out = [chip.sem("parts_out") for _ in range(2)]
        with nc.Block() as block:
            @block.sync
            def _(sp):
                for dst, name in ((wqk, "w2_qk"), (wv, "w2_v"), (bqk, "b2_qk")):
                    sp.dma_start(dst[:], dram[name]).then_inc(w_loaded, 16)
                sp.dma_start(bv[:], dram["b2_v"].to_broadcast([C, C])).then_inc(w_loaded, 16)
                with sp.Fori(0, B) as i:
                    for u in range(2):
                        sp.wait_ge(lo_done, i * 2 + u + 3)
                        sp.dma_start(qk_scr[i, u].rearrange("a r t -> r a t"), parts[:, u]).then_inc(parts_out[u], 16)
                    sp.wait_ge(v_copied, i + 2)
                    sp.dma_start(v_scr[i].rearrange("k p c -> p k c"),
                                 vs[:].rearrange("p k t c -> p k (t c)")).then_inc(v_out, 16)
                for s in (*parts_out, v_out):
                    sp.wait_ge(s, 16 * (B + 1))

            @block.tensor
            def _(pe):
                pe.wait_ge(w_loaded, 64)
                with pe.Fori(0, B) as i:
                    pe.wait_ge(staged, i + 1)
                    for u in range(2):
                        pe.wait_ge(rest_done, i * 2 + u + 1)
                        for c in range(2):
                            mm = nc.tensor.matmul(qk_ps[:, u, c * HALF:(c + 1) * HALF], wqk[:, u, :],
                                                  xs[:, c * HALF:(c + 1) * HALF], start=True, stop=True)
                        mm.then_inc(qk_ready, 1)
                    pe.wait_ge(v_copied, i + 1)
                    for t in range(8):
                        mm = nc.tensor.matmul(v_ps[:, t, :], xs[:, t * C:(t + 1) * C], wv[:], start=True, stop=True)
                    mm.then_inc(v_ready, 1)

            @block.scalar
            def _(act):
                act.wait_ge(w_loaded, 64)
                with act.Fori(0, B) as i:
                    for u in range(2):
                        act.wait_ge(qk_ready, i * 2 + u + 1)
                        act.wait_ge(parts_out[u], i * 16 + 16)
                        nc.scalar.activation(parts[:, u, 0], qk_ps[:, u], ACT.Identity,
                                             bias=bqk[:, u:u + 1]).then_inc(hi_done, 1)
                    for u in range(2):
                        act.wait_ge(rest_done, i * 2 + u + 3)
                        nc.scalar.copy(parts[:, u, 1], rest[:, u]).then_inc(mid_done, 1)

            @block.gpsimd
            def _(pool):
                with pool.Fori(0, B) as i:
                    for u in range(2):
                        pool.wait_ge(mid_done, i * 2 + u + 1)
                        nc.gpsimd.tensor_tensor(parts[:, u, 2], rest[:, u], parts[:, u, 1],
                                                ALU.subtract).then_inc(lo_done, 1)

            @block.vector
            def _(v):
                grant(nc, scratch, [(rest_done, 2), (lo_done, 2), (v_copied, 1), (parts_out[0], 16),
                                    (parts_out[1], 16), (v_out, 16), (v_ready, 1)])
                v.wait_ge(w_loaded, 64)
                with v.Fori(0, B) as i:
                    v.wait_ge(v_ready, i + 1)
                    nc.vector.tensor_copy(xs[:], XN[:, i, :]).then_inc(staged, 1)
                    for u in range(2):
                        v.wait_ge(hi_done, i * 2 + u + 1)
                        v.wait_ge(lo_done, i * 2 + u + 1)
                        nc.vector.scalar_tensor_tensor(rest[:, u], qk_ps[:, u], bqk[:, u:u + 1], parts[:, u, 0],
                                                       ALU.add, ALU.subtract).then_inc(rest_done, 1)
                    v.wait_ge(v_ready, i + 2)
                    v.wait_ge(v_out, i * 16 + 16)
                    for k in range(4):
                        ins = nc.vector.tensor_tensor(vs[:, k], v_ps[:, :, 32 * k:32 * k + 32],
                                                      bv[:, 32 * k:32 * k + 32].unsqueeze(1).to_broadcast([C, 8, 32]), ALU.add)
                    ins.then_inc(v_copied, 1)


def route(chip, XN, dram, w_name, identf, prefer, guard, g_scr):
    nc = chip.nc
    T = B * 8
    with chip.stage() as ctx:
        wr = chip.buf(ctx, "wr", [C, E])
        xs = chip.buf(ctx, "xs", [C, 2, N])
        L, P, M, G = (chip.buf(ctx, n, [C, T, E]) for n in ("L", "P", "M", "G"))
        m1, m2, r = (chip.buf(ctx, n, [C, T]) for n in ("m1", "m2", "r"))
        gt = chip.buf(ctx, "gt", [E * 8, B, C])
        scratch = chip.buf(ctx, "scratch", [1, 8])
        l_ps = chip.psum(ctx, "l_ps", [C, 2, HALF])
        g_ps = chip.psum(ctx, "g_ps", [C, B, C])
        w_loaded, staged, logits, copied, chain, expd, gates, turned, gcopied, out = (chip.sem(s) for s in (
            "w_loaded", "staged", "logits", "copied", "chain", "expd", "gates", "turned", "gcopied", "out"))
        wide = lambda a: a[:].unsqueeze(2).to_broadcast([C, T, E])
        with nc.Block() as block:
            @block.sync
            def _(sp):
                sp.dma_start(wr[:], dram[w_name]).then_inc(w_loaded, 16)
                for half in range(2):
                    sp.wait_ge(gcopied, half + 1)
                    for i in range(4 * half, 4 * half + 4):
                        sp.dma_start(g_scr[i].rearrange("e (t q) -> (e t) q", q=C), gt[:, i]).then_inc(out, 16)
                sp.wait_ge(out, 16 * B)

            @block.scalar
            def _(act):
                with act.Fori(0, B // 2) as i:
                    for s in range(2):
                        act.wait_ge(logits, i * 2 + s + 1)
                        nc.scalar.copy(xs[:, s], XN[:, i * 2 + s, :]).then_inc(staged, 1)
                act.wait_ge(chain, 2)
                nc.scalar.activation(P[:], L[:], ACT.Exp).then_inc(expd, 1)

            @block.tensor
            def _(pe):
                pe.wait_ge(w_loaded, 16)
                with pe.Fori(0, B // 2) as i:
                    for s in range(2):
                        pe.wait_ge(staged, i * 2 + s + 1)
                        pe.wait_ge(copied, i * 2 + s + 1)
                        for t in range(8):
                            mm = nc.tensor.matmul(l_ps[:, s, t * E:(t + 1) * E], xs[:, s, t * C:(t + 1) * C], wr[:],
                                                  start=True, stop=True)
                        mm.then_inc(logits, 1)
                pe.wait_ge(gates, 1)
                for i in range(B):
                    mm = nc.tensor.transpose(g_ps[0:E * 8, i, :], G[:, i * 8:(i + 1) * 8, :].rearrange("p t e -> p (t e)"), identf[:])
                    if i % 4 == 3:
                        mm.then_inc(turned, 1)

            @block.vector
            def _(v):
                count = [0]

                def chained(ins):
                    count[0] += 1
                    ins.then_inc(chain, 1)
                    v.wait_ge(chain, count[0])

                grant(nc, scratch, [(logits, 2), (copied, 2)])
                with v.Fori(0, B // 2) as i:
                    for s in range(2):
                        v.wait_ge(logits, i * 2 + s + 3)
                        nc.vector.tensor_copy(L[:].rearrange("p (i c) e -> p i (c e)", i=B)[:, i * 2 + s, :],
                                              l_ps[:, s, 0:8 * E]).then_inc(copied, 1)
                v.wait_ge(copied, B + 2)
                chained(nc.vector.tensor_reduce(m1[:], L[:], AX.X, ALU.max))
                chained(nc.vector.tensor_tensor(L[:], L[:], wide(m1), ALU.subtract))
                v.wait_ge(expd, 1)
                chained(nc.vector.tensor_reduce(m1[:], P[:], AX.X, ALU.add))
                chained(nc.vector.reciprocal(r[:], m1[:]))
                chained(nc.vector.tensor_tensor(P[:], P[:], wide(r), ALU.mult))
                pref = prefer[:].unsqueeze(1).to_broadcast([C, T, E])
                chained(nc.vector.tensor_reduce(m1[:], P[:], AX.X, ALU.max))
                chained(nc.vector.tensor_tensor(M[:], P[:], wide(m1), ALU.is_equal))
                chained(nc.vector.tensor_tensor(M[:], M[:], pref, ALU.mult))
                chained(nc.vector.tensor_reduce(r[:], M[:], AX.X, ALU.max))
                chained(nc.vector.tensor_tensor(G[:], M[:], wide(r), ALU.is_equal))
                chained(nc.vector.scalar_tensor_tensor(L[:].rearrange("p t e -> p (t e)"), G[:].rearrange("p t e -> p (t e)"),
                                                       -4.0, P[:].rearrange("p t e -> p (t e)"), ALU.mult, ALU.add))
                chained(nc.vector.tensor_reduce(m2[:], L[:], AX.X, ALU.max))
                chained(nc.vector.tensor_tensor(M[:], L[:], wide(m2), ALU.is_equal))
                chained(nc.vector.tensor_tensor(M[:], M[:], pref, ALU.mult))
                chained(nc.vector.tensor_reduce(r[:], M[:], AX.X, ALU.max))
                chained(nc.vector.tensor_tensor(M[:], M[:], wide(r), ALU.is_equal))
                chained(nc.vector.tensor_tensor(G[:], G[:], M[:], ALU.add))
                chained(nc.vector.tensor_tensor(m1[:], m1[:], m2[:], ALU.add))
                if guard == "max":
                    chained(nc.vector.tensor_scalar(m1[:], m1[:], 1e-12, None, ALU.max))
                else:
                    chained(nc.vector.tensor_scalar(m1[:], m1[:], 1e-9, None, ALU.add))
                chained(nc.vector.reciprocal(r[:], m1[:]))
                chained(nc.vector.tensor_tensor(P[:], P[:], wide(r), ALU.mult))
                chained(nc.vector.tensor_tensor(P[:], P[:], G[:], ALU.mult))
                nc.vector.tensor_copy(G[:].rearrange("p (i c) e -> p i (c e)", i=B).rearrange("p i (e t) -> p i e t", e=E),
                                      P[:].rearrange("p (i t) e -> p i e t", i=B)).then_inc(gates, 1)
                for half in range(2):
                    v.wait_ge(turned, half + 1)
                    nc.vector.tensor_copy(gt[:, 4 * half:4 * half + 4], g_ps[0:E * 8, 4 * half:4 * half + 4]).then_inc(gcopied, 1)


def gelu_experts(chip, X, XN, dram, g_scr):
    nc = chip.nc
    GS = 4
    with chip.stage() as ctx:
        w1, w2 = chip.buf(ctx, "w1", [C, E, C]), chip.buf(ctx, "w2", [C, E, C])
        b1, b2 = chip.buf(ctx, "b1", [C, E]), chip.buf(ctx, "b2", [E, C])
        gb = chip.buf(ctx, "gb", [C, GS, N])
        gt = chip.buf(ctx, "gt", [E, 2, N])
        hs, hg = chip.buf(ctx, "hs", [C, 2, N]), chip.buf(ctx, "hg", [C, 2, N])
        scratch = chip.buf(ctx, "scratch", [1, 8])
        h_ps = chip.psum(ctx, "h_ps", [C, 2, N])
        y_ps = chip.psum(ctx, "y_ps", [C, N])
        w_loaded, h_ready, gelu_done, gated, image_done, added, y_steps = (chip.sem(s) for s in (
            "w_loaded", "h_ready", "gelu_done", "gated", "image_done", "added", "y_steps"))
        gb_loaded = [chip.sem("gb_loaded") for _ in range(GS)]
        gt_loaded = [chip.sem("gt_loaded") for _ in range(2)]
        with nc.Block() as block:
            @block.sync
            def _(sp):
                for dst, name in ((w1, "m2_w1"), (w2, "m2_w2"), (b1, "m2_b1"), (b2, "m2_b2")):
                    sp.dma_start(dst[:], dram[name]).then_inc(w_loaded, 16)
                with sp.Fori(0, B // 2) as i:
                    for s in range(2):
                        sp.wait_ge(image_done, i * 2 + s + 1)
                        sp.dma_start(gt[:, s], g_scr[i * 2 + s]).then_inc(gt_loaded[s], 16)
                        for e in range(E):
                            sp.wait_ge(gated, i * 2 * E + (s * E + e) + 1)
                            sp.dma_start(gb[:, e % GS], g_scr[i * 2 + s, e:e + 1].to_broadcast([C, N])).then_inc(gb_loaded[e % GS], 16)

            @block.tensor
            def _(pe):
                pe.wait_ge(w_loaded, 64)
                with pe.Fori(0, B // 2) as i:
                    for s in range(2):
                        base = i * 2 * E
                        for e in range(E + 1):
                            n = s * E + e
                            if e < E:
                                pe.wait_ge(gelu_done, base + n + 1)
                                for c in range(2):
                                    mm = nc.tensor.matmul(h_ps[:, e % 2, c * HALF:(c + 1) * HALF], w1[:, e, :],
                                                          XN[:, i * 2 + s, c * HALF:(c + 1) * HALF], start=True, stop=True)
                                mm.then_inc(h_ready, 1)
                            if e == 0:
                                pe.wait_ge(gt_loaded[s], i * 16 + 16)
                                pe.wait_ge(added, i * 2 + s + 1)
                                for c in range(2):
                                    nc.tensor.matmul(y_ps[:, c * HALF:(c + 1) * HALF], b2[:],
                                                     gt[:, s, c * HALF:(c + 1) * HALF], start=True, stop=False)
                            else:
                                pe.wait_ge(gated, base + (n - 1) + GS + 1)
                                for c in range(2):
                                    mm = nc.tensor.matmul(y_ps[:, c * HALF:(c + 1) * HALF], w2[:, e - 1, :],
                                                          hg[:, (e - 1) % 2, c * HALF:(c + 1) * HALF],
                                                          start=False, stop=(e == E))
                                mm.then_inc(y_steps, 1)

            @block.scalar
            def _(act):
                act.wait_ge(w_loaded, 64)
                with act.Fori(0, B) as i:
                    for e in range(E):
                        act.wait_ge(h_ready, i * E + e + 1)
                        act.wait_ge(gated, i * E + e + GS - 1)
                        nc.scalar.activation(hs[:, e % 2], h_ps[:, e % 2], ACT.Gelu, bias=b1[:, e:e + 1]).then_inc(gelu_done, 1)

            @block.gpsimd
            def _(pool):
                with pool.Fori(0, B) as i:
                    for e in range(E):
                        pool.wait_ge(gelu_done, i * E + e + 3)
                        pool.wait_ge(gb_loaded[e % GS], (i * (E // GS) + e // GS) * 16 + 16)
                        pool.wait_ge(y_steps, i * E + e + 1)
                        nc.gpsimd.tensor_tensor(hg[:, e % 2], hs[:, e % 2], gb[:, e % GS], ALU.mult).then_inc(gated, 1)

            @block.vector
            def _(v):
                grant(nc, scratch, [(gelu_done, 2), (gated, GS), (y_steps, 2), (added, 1), (image_done, 2)])
                with v.Fori(0, B) as i:
                    v.wait_ge(y_steps, i * E + E + 2)
                    nc.vector.tensor_tensor(X[:, i, :], y_ps[:], X[:, i, :], ALU.add).then_inc(added, 1)
                    v.wait_ge(added, i + 2)
                    nc.vector.tensor_tensor(X[:, i, :], X[:, i, :], XN[:, i, :], ALU.add).then_inc(image_done, 1)


def silu_experts(chip, X, XN, dram, g_scr):
    nc = chip.nc
    STEPS = E * HC
    R = 3
    LAG = 2
    with chip.stage() as ctx:
        w1, w3, w2 = (chip.buf(ctx, n, [C, E, HC, C]) for n in ("w1", "w3", "w2"))
        gb = chip.buf(ctx, "gb", [C, 2, E, HALF])
        s1, sg, hg = (chip.buf(ctx, n, [C, R, HALF]) for n in ("s1", "sg", "hg"))
        scratch = chip.buf(ctx, "scratch", [1, 8])
        h_ps = chip.psum(ctx, "h_ps", [C, R, 2, HALF])
        y_ps = chip.psum(ctx, "y_ps", [C, 2, HALF])
        w_loaded, h_ready, silu_done, gated, hidden, y_steps, added = (chip.sem(s) for s in (
            "w_loaded", "h_ready", "silu_done", "gated", "hidden", "y_steps", "added"))
        gb_loaded = [chip.sem("gb_loaded") for _ in range(2)]
        PER = 2 * STEPS
        with nc.Block() as block:
            @block.sync
            def _(sp):
                for dst, name in ((w1, "m3_w1"), (w3, "m3_w3"), (w2, "m3_w2")):
                    sp.dma_start(dst[:].rearrange("p e c m -> p (e c m)"), dram[name]).then_inc(w_loaded, 16)
                with sp.Fori(0, B) as i:
                    for s in range(2):
                        sp.wait_ge(added, i * 2 + s + 1)
                        sp.dma_start(gb[:, s], g_scr[i, :, s * HALF:(s + 1) * HALF].unsqueeze(0).to_broadcast([C, E, HALF])
                                     ).then_inc(gb_loaded[s], 16)

            @block.tensor
            def _(pe):
                pe.wait_ge(w_loaded, 48)
                with pe.Fori(0, B) as i:
                    for n in range(PER + LAG):
                        if n < PER:
                            s, e, c = n // STEPS, n % STEPS // HC, n % HC
                            pe.wait_ge(hidden, i * PER + n + 1)
                            x = XN[:, i, s * HALF:(s + 1) * HALF]
                            nc.tensor.matmul(h_ps[:, n % R, 0], w1[:, e, c, :], x, start=True, stop=True)
                            nc.tensor.matmul(h_ps[:, n % R, 1], w3[:, e, c, :], x, start=True, stop=True).then_inc(h_ready, 1)
                        if n >= LAG:
                            m = n - LAG
                            s, e, c = m // STEPS, m % STEPS // HC, m % HC
                            if m % STEPS == 0:
                                pe.wait_ge(added, i * 2 + s + 1)
                            pe.wait_ge(hidden, i * PER + m + R + 1)
                            nc.tensor.matmul(y_ps[:, s], w2[:, e, c, :], hg[:, m % R], start=(m % STEPS == 0),
                                             stop=(m % STEPS == STEPS - 1)).then_inc(y_steps, 1)

            @block.scalar
            def _(act):
                with act.Fori(0, B) as i:
                    for n in range(PER):
                        act.wait_ge(h_ready, i * PER + n + 1)
                        act.wait_ge(gated, i * PER + n + 1)
                        nc.scalar.activation(s1[:, n % R], h_ps[:, n % R, 0], ACT.Silu).then_inc(silu_done, 1)

            @block.gpsimd
            def _(pool):
                with pool.Fori(0, B) as i:
                    for n in range(PER):
                        s, e = n // STEPS, n % STEPS // HC
                        if n % STEPS == 0:
                            pool.wait_ge(gb_loaded[s], i * 16 + 16)
                        pool.wait_ge(silu_done, i * PER + n + 1)
                        pool.wait_ge(hidden, i * PER + n + 1)
                        nc.gpsimd.tensor_tensor(sg[:, n % R], s1[:, n % R], gb[:, s, e], ALU.mult).then_inc(gated, 1)

            @block.vector
            def _(v):
                grant(nc, scratch, [(hidden, R), (gated, R), (y_steps, R), (added, 2)])
                with v.Fori(0, B) as i:
                    for n in range(PER):
                        v.wait_ge(gated, i * PER + n + R + 1)
                        v.wait_ge(y_steps, i * PER + n + 1)
                        nc.vector.tensor_tensor(hg[:, n % R], h_ps[:, n % R, 1], sg[:, n % R], ALU.mult).then_inc(hidden, 1)
                        if n % STEPS == LAG + 1 and n > STEPS:
                            v.wait_ge(y_steps, i * PER + (STEPS + R))
                            at = X[:, i, 0:HALF]
                            nc.vector.tensor_tensor(at, y_ps[:, 0], at, ALU.add).then_inc(added, 1)
                    v.wait_ge(y_steps, i * PER + (PER + R))
                    at = X[:, i, HALF:N]
                    nc.vector.tensor_tensor(at, y_ps[:, 1], at, ALU.add).then_inc(added, 1)


def local_attention(chip, XN, dram, identf, out):
    nc = chip.nc
    TILES = -(-N // QT)
    GROUPS = [(0, 3), (3, 3), (6, 3), (9, 2)]
    assert GROUPS[-1][0] + GROUPS[-1][1] == TILES
    WIDE = 3 * QT
    with chip.stage() as ctx:
        band = chip.buf(ctx, "band", [C, QT])
        ones = chip.buf(ctx, "ones", [C, C])
        xs = chip.buf(ctx, "xs", [C, 2, N + 64])
        tk = chip.buf(ctx, "tk", [C, 2, 3, C])
        ex, em, rd = (chip.buf(ctx, n, [C, 2, WIDE]) for n in ("ex", "em", "rd"))
        scratch = chip.buf(ctx, "scratch", [1, 8])
        t_ps = chip.psum(ctx, "t_ps", [C, 2, HALF])
        s_ps = chip.psum(ctx, "s_ps", [C, 2, HALF])
        n_ps = chip.psum(ctx, "n_ps", [C, 2, HALF])
        d_ps = chip.psum(ctx, "d_ps", [C, 2, HALF])
        w_loaded, filled, staged, turned, scored, copied, expd, masked, summed, inverted, stored = (chip.sem(s) for s in (
            "w_loaded", "filled", "staged", "turned", "scored", "copied", "expd", "masked", "summed", "inverted", "stored"))

        def queries(t):
            return min(QT, N - t * QT)

        with nc.Block() as block:
            @block.sync
            def _(sp):
                sp.dma_start(band[:], dram["band"]).then_inc(w_loaded, 16)
                sp.wait_ge(w_loaded, 16)

            @block.tensor
            def _(pe):
                def front(i, s, g):
                    n = s * 4 + g
                    t0, cnt = GROUPS[g]
                    if g == 0:
                        pe.wait_ge(staged, i * 2 + s + 1)
                    pe.wait_ge(copied, i * 8 + n + 1)
                    for t in range(cnt):
                        mm = nc.tensor.transpose(t_ps[:, n % 2, t * C:(t + 1) * C],
                                                 xs[:, s, (t0 + t) * QT:(t0 + t) * QT + C], identf[:])
                    mm.then_inc(turned, 1)
                    pe.wait_ge(expd, i * 8 + n + 1)
                    for t in range(cnt):
                        q = queries(t0 + t)
                        at = (t0 + t) * QT
                        mm = nc.tensor.matmul(s_ps[:, n % 2, t * QT:t * QT + q], xs[:, s, at:at + C],
                                              xs[:, s, BAND + at:BAND + at + q], start=True, stop=True)
                    mm.then_inc(scored, 1)

                def back(i, s, g):
                    n = s * 4 + g
                    t0, cnt = GROUPS[g]
                    pe.wait_ge(masked, i * 8 + n + 3)
                    pe.wait_ge(copied, i * 8 + n + 3)
                    pe.wait_ge(stored, i * 8 + n + 1)
                    for t in range(cnt):
                        q = queries(t0 + t)
                        nc.tensor.matmul(n_ps[:, n % 2, t * QT:t * QT + q], tk[:, n % 2, t], em[:, n % 2, t * QT:t * QT + q],
                                         start=True, stop=True)
                    width = (cnt - 1) * QT + queries(t0 + cnt - 1)
                    nc.tensor.matmul(d_ps[:, n % 2, 0:width], ones[:], em[:, n % 2, 0:width],
                                     start=True, stop=True).then_inc(summed, 1)

                pe.wait_ge(filled, 3)
                with pe.Fori(0, B // 2) as i:
                    for n in range(9):
                        if n < 8:
                            front(i, n // 4, n % 4)
                        if n:
                            back(i, (n - 1) // 4, (n - 1) % 4)

            @block.scalar
            def _(act):
                act.wait_ge(filled, 3)
                with act.Fori(0, B // 2) as i:
                    for n in range(8):
                        s, g = n // 4, n % 4
                        t0, cnt = GROUPS[g]
                        if g == 0:
                            act.wait_ge(summed, i * 8 + 4 * s + 1)
                            nc.scalar.copy(xs[:, s, BAND:BAND + N], XN[:, i * 2 + s, :]).then_inc(staged, 1)
                        width = (cnt - 1) * QT + queries(t0 + cnt - 1)
                        act.wait_ge(scored, i * 8 + n + 1)
                        act.wait_ge(masked, i * 8 + n + 1)
                        nc.scalar.activation(ex[:, n % 2, 0:width], s_ps[:, n % 2, 0:width], ACT.Exp,
                                             scale=float(C) ** -0.5).then_inc(expd, 1)

            @block.vector
            def _(v):
                nc.vector.memset(xs[:], 0.0).then_inc(filled, 1)
                nc.vector.memset(ones[:], 1.0).then_inc(filled, 1)
                grant(nc, scratch, [(copied, 2), (expd, 2), (masked, 2), (stored, 2), (summed, 4), (filled, 1)])
                v.wait_ge(w_loaded, 16)

                def finish(i, n):
                    s, g = n // 4, n % 4
                    t0, cnt = GROUPS[g]
                    width = (cnt - 1) * QT + queries(t0 + cnt - 1)
                    v.wait_ge(summed, i * 8 + n + 5)
                    nc.vector.reciprocal(rd[:, n % 2, 0:width], d_ps[:, n % 2, 0:width]).then_inc(inverted, 1)
                    v.wait_ge(inverted, i * 8 + n + 1)
                    nc.vector.tensor_tensor(out[:, i * 2 + s, t0 * QT:t0 * QT + width], n_ps[:, n % 2, 0:width],
                                            rd[:, n % 2, 0:width], ALU.mult).then_inc(stored, 1)

                with v.Fori(0, B // 2) as i:
                    for n in range(9):
                        if n < 8:
                            cnt = GROUPS[n % 4][1]
                            t0 = GROUPS[n % 4][0]
                            v.wait_ge(turned, i * 8 + n + 1)
                            v.wait_ge(summed, i * 8 + n + 3)
                            nc.vector.tensor_copy(tk[:, n % 2, 0:cnt].rearrange("p t c -> p (t c)"),
                                                  t_ps[:, n % 2, 0:cnt * C]).then_inc(copied, 1)
                            v.wait_ge(expd, i * 8 + n + 3)
                            full = cnt if queries(t0 + cnt - 1) == QT else cnt - 1
                            ins = nc.vector.tensor_tensor(
                                em[:, n % 2, 0:full * QT].rearrange("p (t q) -> p t q", q=QT),
                                ex[:, n % 2, 0:full * QT].rearrange("p (t q) -> p t q", q=QT),
                                band[:].unsqueeze(1).to_broadcast([C, full, QT]), ALU.mult)
                            if full < cnt:
                                q = queries(t0 + full)
                                ins = nc.vector.tensor_tensor(em[:, n % 2, full * QT:full * QT + q],
                                                              ex[:, n % 2, full * QT:full * QT + q], band[:, 0:q], ALU.mult)
                            ins.then_inc(masked, 1)
                        if n:
                            finish(i, n - 1)


def store(chip, X, out):
    nc = chip.nc
    stored = chip.sem("stored")
    with nc.Block() as block:
        @block.sync
        def _(sp):
            with sp.Fori(0, B) as i:
                sp.dma_start(out[i].rearrange("c h w -> c (h w)"), X[:, i, :]).then_inc(stored, 16)
            sp.wait_ge(stored, 16 * B)


def network(nc, x, dram, out):
    def scratch(name, shape, dt=F32):
        return nc.dram_tensor(name, shape, dt, kind="Internal").ap()

    qk0 = scratch("qk0", [B, 4, PARTS, C, N], BF16)
    v0 = scratch("v0", [B, 4, C, 8 * 64])
    qk2 = scratch("qk2", [B, 2, PARTS, C, N], BF16)
    v2 = scratch("v2", [B, 4, C, 8 * 32])
    m0 = scratch("m0", [2, 2, PARTS, 4, 8, C], BF16)
    m2 = scratch("m2", [2, 1, PARTS, 4, 8, C], BF16)
    g2 = scratch("g2", [B, E, N])
    g3 = scratch("g3", [B, E, N])

    with ExitStack() as ctx:
        chip = Chip(nc)
        X = chip.buf(ctx, "X", [C, B, N])
        identf = chip.buf(ctx, "identf", [C, C])
        ident = chip.buf(ctx, "ident", [C, C], BF16)
        sel = chip.buf(ctx, "sel", [C, 4])
        gn_avg = chip.buf(ctx, "gn_avg", [C, C])
        mean_w = chip.buf(ctx, "mean_w", [C, C])
        prefer = chip.buf(ctx, "prefer", [C, E])
        bproj = chip.buf(ctx, "bproj", [C, 1])
        gamma, beta = chip.buf(ctx, "gamma", [C, 1]), chip.buf(ctx, "beta", [C, 1])
        eps5 = chip.buf(ctx, "eps5", [C, 1])
        mean_g, rstd_g = chip.buf(ctx, "mean_g", [C, B, 1]), chip.buf(ctx, "rstd_g", [C, B, 1])
        pooled = chip.buf(ctx, "pooled", [C, B])
        load_inputs(chip, x, X, [(identf, dram["ident"]), (sel, dram["sel"]), (gn_avg, dram["gn_avg"]),
                                 (mean_w, dram["mean_w"]), (prefer, dram["prefer"]), (bproj, dram["b_proj"]),
                                 (gamma, dram["gamma"]), (beta, dram["beta"])])
        prepared = chip.sem("prepared")
        with nc.Block() as block:
            @block.vector
            def _(v):
                nc.vector.memset(eps5[:], 1e-5).then_inc(prepared, 1)
                nc.vector.tensor_copy(ident[:], identf[:]).then_inc(prepared, 1)

        def flat(a):
            return a[:].rearrange("p b o -> p (b o)")

        group_norm_stats(chip, X, gn_avg, eps5, flat(mean_g), flat(rstd_g), pooled)
        window_projections(chip, X, mean_g, rstd_g, dram, qk0, v0)

        def window_finals(block):
            if block == 3:
                return [(64, 0, HALF - 64), (HALF, HALF - 64, HALF), (0, N - 64, 64)]
            return [(0, 0, HALF), (HALF, HALF, HALF)]

        attention(chip, X, dram, lambda i, k, o: qk0[i, k, :, 64 * o:64 * o + 64, :], v0, m0, ident, identf, sel, "w0_out",
                  None, 2, 1, float(D) ** -0.5, window_finals, True)

        group_norm_stats(chip, X, gn_avg, eps5, flat(mean_g), flat(rstd_g), pooled)
        conv_stage(chip, X, dram, mean_g, rstd_g, pooled, eps5, identf)

        with ExitStack() as c2:
            XN = chip.buf(c2, "XN", [C, B, N])
            layer_norm(chip, X, mean_w, eps5, identf, dst=XN)
            token_projections(chip, XN, dram, qk2, v2)
        attention(chip, X, dram, lambda i, k, o: qk2[i, o, :, 32 * k:32 * k + 32, :], v2, m2, ident, identf, sel, "w2_out",
                  bproj, 1, 8, 1.0, lambda f: [(0, 0, HALF), (HALF, HALF, HALF)], False)

        with ExitStack() as c2:
            XN = chip.buf(c2, "XN", [C, B, N])
            layer_norm(chip, X, mean_w, eps5, identf, dst=XN)
            route(chip, XN, dram, "m2_router", identf, prefer, "max", g2)
            gelu_experts(chip, X, XN, dram, g2)
            layer_norm(chip, X, mean_w, eps5, identf, dst=XN)
            with ExitStack() as c3:
                O = chip.buf(c3, "O", [C, B, N])
                local_attention(chip, XN, dram, identf, O)
                layer_norm(chip, O, mean_w, eps5, identf, X=X, gamma=gamma, beta=beta)
            layer_norm(chip, X, mean_w, eps5, identf, dst=XN)
            route(chip, XN, dram, "m3_router", identf, prefer, "add", g3)
            silu_experts(chip, X, XN, dram, g3)
        store(chip, X, out)


def constants():
    import numpy as np

    c = np.arange(C)
    one = np.float32(1)
    sel = np.where(c[:, None] == 32 * np.arange(4)[None, :] + D, one, 0 * one)
    w0_out = np.zeros((C, 4, 2, C), np.float32)
    for u in range(4):
        s, part = u // 2 * 2, u % 2
        for sub in range(2):
            for j in range(4):
                for d in range(D):
                    w0_out[32 * j + d, u, sub, part * 64 + (d * 8 + 4 * sub + j + s) % 64] = 1
    key, query = np.arange(C)[:, None], np.arange(QT)[None, :]
    band = np.where((key >= query) & (key <= query + 2 * BAND), one, 0 * one)
    return {
        "ident": np.eye(C, dtype=np.float32),
        "sel": sel.astype(np.float32),
        "gn_avg": np.where(c[:, None] // 4 == c[None, :] // 4, one / 4, 0 * one).astype(np.float32),
        "mean_w": np.full((C, C), 1 / C, np.float32),
        "prefer": np.tile(np.arange(E, 0, -1, dtype=np.float32), (C, 1)),
        "w0_out": w0_out.reshape(C, 8 * C),
        "band": band.astype(np.float32),
    }


def laid_out(a):
    import numpy as np

    out = {}
    wq = a["L0_conv_w_qkv"][:, :, 0, 0]
    head_major = np.array([d * 8 + h for h in range(8) for d in range(D)])
    qk, vv = np.zeros((C, 4, C), np.float32), np.zeros((C, 4, 64), np.float32)
    lepe, taps, bl = np.zeros((C, 2, C), np.float32), np.zeros((2, 9, C), np.float32), np.zeros((C, 2), np.float32)
    for u in range(4):
        s, part = u // 2 * 2, u % 2
        rows = (part * 64 + np.arange(64) + s) % C
        qk[rows, u, 0:64] = wq[head_major].T
        qk[rows, u, 64:128] = wq[64 + head_major].T
        vv[rows, u] = wq[128 + head_major].T
        conv = (np.arange(64) - s) % 64
        at = slice(part * 64, part * 64 + 64)
        lepe[rows, s // 2, at] = wq[128 + conv].T
        taps[s // 2, :, at] = a["L0_conv_w_lepe"][conv, 0].reshape(64, 9).T
        bl[at, s // 2] = a["L0_conv_b_lepe"][conv]
    out["w0_qk"], out["w0_v"], out["w0_lepe"] = qk, vv, lepe
    out["lepe_taps"], out["b_lepe"] = taps.reshape(1, -1), bl
    out["se_w1"], out["se_w2"] = a["L1_conv_attn_w1"].T, a["L1_conv_attn_w2"].T
    out["refine_w"], out["refine_b"] = a["L1_conv_refine_w"].reshape(C, 9), a["L1_conv_refine_b"].reshape(C, 1)
    w = a["L2_attn_w_qkv"]
    out["w2_qk"], out["w2_v"] = w[:, :2 * C].reshape(C, 2, C), w[:, 2 * C:]
    b = a["L2_attn_b_qkv"]
    out["b2_qk"], out["b2_v"] = b[:2 * C].reshape(2, C).T, b[2 * C:].reshape(1, C)
    proj = np.zeros((4, 32, 4, C), np.float32)
    proj[:, 0:D] = a["L2_attn_w_proj"].reshape(4, 4, D, C).transpose(1, 2, 0, 3)
    out["w2_out"], out["b_proj"] = proj.reshape(C, 4 * C), a["L2_attn_b_proj"].reshape(C, 1)
    out["m2_router"], out["m3_router"] = a["L2_ffn_router_w"].T, a["L3_ffn_router_w"].T
    out["m2_w1"], out["m2_w2"] = a["L2_ffn_w1"].transpose(1, 0, 2), a["L2_ffn_w2"].transpose(1, 0, 2)
    out["m2_b1"], out["m2_b2"] = a["L2_ffn_b1"].T, a["L2_ffn_b2"]
    out["gamma"], out["beta"] = a["L3_attn_gamma"].reshape(C, 1), a["L3_attn_beta"].reshape(C, 1)
    for name in ("w1", "w3"):
        padded = np.zeros((C, E, HC * C), np.float32)
        padded[:, :, :HID] = a[f"L3_ffn_{name}"].transpose(2, 0, 1)
        out["m3_" + name] = padded.reshape(C, -1)
    w2 = np.zeros((E, HC * C, C), np.float32)
    w2[:, :HID] = a["L3_ffn_w2"].transpose(0, 2, 1)
    out["m3_w2"] = w2.reshape(E, HC, C, C).transpose(2, 0, 1, 3).reshape(C, -1)
    return out


def kernel(**inputs):
    import numpy as np
    import concourse.bacc as bacc
    from concourse.bass_utils import run_bass_kernel_spmd as run

    inputs = {name: np.asarray(value) for name, value in inputs.items()}
    nc = bacc.Bacc("TRN2", target_bir_lowering=False, num_devices=1)
    arrays, dram = {}, {}
    for name, value in {"x": inputs["x"], **constants(), **laid_out(inputs)}.items():
        value = np.ascontiguousarray(value)
        arrays[f"in_{name}"] = value
        dram[name] = nc.dram_tensor(f"in_{name}", value.shape, mybir.dt.from_np(value.dtype), kind="ExternalInput").ap()
    out = nc.dram_tensor("out", inputs["x"].shape, F32, kind="ExternalOutput").ap()
    network(nc, dram["x"], dram, out)
    return run(nc, [arrays], core_ids=[0]).results[0]["out"]
```

```python
from contextlib import ExitStack, contextmanager

import concourse.bass as bass
from concourse import mybir

F32 = mybir.dt.float32
BF16 = mybir.dt.bfloat16
F16 = mybir.dt.float16
ALU = mybir.AluOpType
ACT = mybir.ActivationFunctionType
AX = mybir.AxisListType

B, C, H, W = 8, 128, 32, 32
N = H * W
HALF = N // 2
D = 8
PARTS = 3
COMBOS = [(0, 0), (0, 1), (0, 2), (1, 0), (1, 1), (2, 0)]
STACK = len(COMBOS) * D
ROWS = STACK + PARTS
E = 8
HID = 341
BAND = 16
QT = C - 2 * BAND


def grant(nc, scratch, credits):
    for n, (sem, slots) in enumerate(credits):
        nc.vector.memset(scratch[0:1, n:n + 1], 0.0).then_inc(sem, slots)


class Chip:

    def __init__(self, nc):
        self.nc, self.n, self.sems = nc, 0, []

    @contextmanager
    def stage(self):
        outer, self.sems = self.sems, []
        with ExitStack() as ctx:
            yield ctx
        self.nc.clear_and_free_semaphores(self.sems)
        self.nc.all_engine_barrier()
        self.sems = outer

    def sem(self, name):
        self.n += 1
        self.sems.append(self.nc.alloc_semaphore(name=f"{name}_{self.n}"))
        return self.sems[-1]

    def buf(self, ctx, name, shape, dt=F32):
        self.n += 1
        return ctx.enter_context(self.nc.sbuf_tensor(f"{name}_{self.n}", shape, dt))

    def psum(self, ctx, name, shape, dt=F32):
        self.n += 1
        return ctx.enter_context(self.nc.psum_tensor(f"{name}_{self.n}", shape, dt))


def load_inputs(chip, x, X, consts):
    nc = chip.nc
    loaded = chip.sem("inputs_loaded")
    with nc.Block() as block:
        @block.sync
        def _(sp):
            for i in range(B):
                sp.dma_start(X[:, i, :], x[i].rearrange("c h w -> c (h w)")).then_inc(loaded, 16)
            for dst, src in consts:
                sp.dma_start(dst[:], src).then_inc(loaded, 16)
            sp.wait_ge(loaded, 16 * (B + len(consts)))


def group_norm_stats(chip, X, gn_avg, eps5, mean_g, rstd_g, pooled):
    nc = chip.nc
    with chip.stage() as ctx:
        st = chip.buf(ctx, "gn_st", [C, B, 12])
        mv = chip.buf(ctx, "gn_mv", [C, B, 2])
        dev = chip.buf(ctx, "gn_dev", [C, B])
        sq = chip.buf(ctx, "gn_sq", [C, B])
        sd = chip.buf(ctx, "gn_sd", [C, B])
        ps = chip.psum(ctx, "gn_ps", [C, 2, HALF])
        stats, aggr, avg, step, rooted = (chip.sem(s) for s in ("stats", "aggr", "avg", "dvestep", "rooted"))
        with nc.Block() as block:
            @block.vector
            def _(v):
                for i in range(B):
                    for c in range(2):
                        last = nc.vector.bn_stats(st[:, i, 6 * c:6 * c + 6], X[:, i, c * HALF:(c + 1) * HALF])
                    last.then_inc(stats, 1)
                for i in range(B):
                    v.wait_ge(stats, i + 1)
                    nc.vector.bn_aggr(mv[:, i, :], st[:, i, :]).then_inc(aggr, 1)
                v.wait_ge(aggr, B)
                v.wait_ge(avg, 1)
                nc.vector.tensor_copy(mean_g[:], ps[:, 0, 0:B]).then_inc(step, 1)
                nc.vector.tensor_tensor(dev[:], mv[:, :, 0], ps[:, 0, 0:B], ALU.subtract).then_inc(step, 1)
                v.wait_ge(step, 2)
                nc.vector.tensor_tensor(sq[:], dev[:], dev[:], ALU.mult).then_inc(step, 1)
                v.wait_ge(step, 3)
                nc.vector.tensor_tensor(sq[:], sq[:], mv[:, :, 1], ALU.add).then_inc(step, 1)
                v.wait_ge(rooted, 1)
                nc.vector.reciprocal(rstd_g[:], sd[:]).then_inc(step, 1)
                v.wait_ge(step, 5)
                nc.vector.tensor_tensor(pooled[:], dev[:], rstd_g[:], ALU.mult).then_inc(step, 1)

            @block.tensor
            def _(pe):
                pe.wait_ge(aggr, B)
                nc.tensor.matmul(ps[:, 0, 0:B], gn_avg[:], mv[:, :, 0], start=True, stop=True).then_inc(avg, 1)
                pe.wait_ge(step, 4)
                nc.tensor.matmul(ps[:, 1, 0:B], gn_avg[:], sq[:], start=True, stop=True).then_inc(avg, 1)

            @block.scalar
            def _(act):
                act.wait_ge(avg, 2)
                nc.scalar.activation(sd[:], ps[:, 1, 0:B], ACT.Sqrt, bias=eps5[:]).then_inc(rooted, 1)


def lepe_pieces(half):
    lo, hi = 16 * half, 16 * half + 16
    out = [(4, 2, lo, 16, lo)]
    for dh in (0, -1, 1):
        for dw in (-1, 0, 1):
            tap = (dh + 1) * 3 + dw + 1
            if tap == 4:
                continue
            if dh == 0:
                out.append((tap, 2, lo, 16, lo))
                continue
            r = lo
            while r < hi:
                src = r + dh
                if r == (31 if dh == 1 else 0):
                    kind = 1
                elif r == (1 if dh == 1 else 2):
                    kind = 0
                else:
                    kind = 2
                n = 1
                while kind == 2 and r + n < hi and r + n != (31 if dh == 1 else 0) and r + n != (1 if dh == 1 else 2):
                    n += 1
                out.append((tap, kind, r, n, src % H))
                r += n
    return out


def window_projections(chip, X, mean_g, rstd_g, dram, qk_scr, v_scr):
    nc = chip.nc
    U = 4
    with chip.stage() as ctx:
        wqk = chip.buf(ctx, "wqk", [C, 4, C])
        wv = chip.buf(ctx, "wv", [C, 4, 64])
        wl = chip.buf(ctx, "wl", [C, 2, C])
        taps = chip.buf(ctx, "taps", [C, 2, 9, C])
        wt = chip.buf(ctx, "wt", [C, 3, 9, C])
        bl = chip.buf(ctx, "bl", [C, 2])
        bsum = chip.buf(ctx, "bsum", [C, 1])
        scratch = chip.buf(ctx, "scratch", [1, 16])
        xn = chip.buf(ctx, "xn", [C, N + 64])
        xw = chip.buf(ctx, "xw", [C, N])
        xp = chip.buf(ctx, "xp", [C, H, W + 2])
        parts = chip.buf(ctx, "parts", [C, 2, PARTS, N], BF16)
        rest = chip.buf(ctx, "rest", [C, 2, N])
        vs = chip.buf(ctx, "vs", [C, 2, HALF])
        qk_ps = chip.psum(ctx, "qk_ps", [C, 2, N])
        v_ps = chip.psum(ctx, "v_ps", [C, 2, HALF])
        l_ps = chip.psum(ctx, "l_ps", [C, N])
        w_loaded, weights, normed, padded, edge, strips = (chip.sem(s) for s in (
            "w_loaded", "weights", "normed", "padded", "edge", "strips"))
        qk_ready, hi_done, rest_done, mid_done, lo_done = (chip.sem(s) for s in (
            "qk_ready", "hi_done", "rest_done", "mid_done", "lo_done"))
        v_ready, v_copied, l_ready, l_added = (chip.sem(s) for s in ("v_ready", "v_copied", "l_ready", "l_added"))
        parts_out = [chip.sem("parts_out") for _ in range(2)]
        v_out = [chip.sem("v_out") for _ in range(2)]
        with nc.Block() as block:
            @block.sync
            def _(sp):
                for dst, name in ((wqk, "w0_qk"), (wv, "w0_v"), (wl, "w0_lepe"), (bl, "b_lepe")):
                    sp.dma_start(dst[:], dram[name]).then_inc(w_loaded, 16)
                sp.dma_start(taps[:].rearrange("p s t c -> p (s t c)"),
                             dram["lepe_taps"].to_broadcast([C, 2 * 9 * C])).then_inc(w_loaded, 16)
                with sp.Fori(0, B) as i:
                    for u in range(U):
                        sp.wait_ge(lo_done, i * U + u + 3)
                        sp.dma_start(qk_scr[i, u].rearrange("a r t -> r a t"),
                                     parts[:, u % 2]).then_inc(parts_out[u % 2], 16)
                        sp.wait_ge(v_copied, i * U + u + 3)
                        sp.dma_start(v_scr[i, u], vs[:, u % 2]).then_inc(v_out[u % 2], 16)
                for s in (*parts_out, *v_out):
                    sp.wait_ge(s, 16 * (B * U // 2 + 1))

            @block.vector
            def _(v):
                grant(nc, scratch, [(rest_done, 2), (lo_done, 2), (v_copied, 2), (l_added, 1),
                                    (parts_out[0], 16), (parts_out[1], 16), (v_out[0], 16), (v_out[1], 16)])
                nc.vector.memset(xp[:], 0.0).then_inc(weights, 1)
                v.wait_ge(w_loaded, 16 * 5)
                for s in range(2):
                    nc.vector.tensor_tensor(wt[:, s], taps[:, s],
                                            wl[:, s].unsqueeze(1).to_broadcast([C, 9, C]), ALU.mult).then_inc(weights, 1)
                nc.vector.tensor_tensor(bsum[:], bl[:, 0:1], bl[:, 1:2], ALU.add).then_inc(weights, 1)
                v.wait_ge(weights, 4)
                nc.vector.tensor_tensor(wt[:, 2], wt[:, 0], wt[:, 1], ALU.add).then_inc(weights, 1)
                with v.Fori(0, B) as i:
                    nc.vector.tensor_scalar(xn[:, 0:N], X[:, i, :], mean_g[:, i, :], rstd_g[:, i, :],
                                            ALU.subtract, ALU.mult).then_inc(normed, 1)
                    v.wait_ge(normed, i + 1)
                    nc.vector.tensor_copy(xn[:, N:N + 64], xn[:, 0:64]).then_inc(edge, 1)
                    nc.vector.tensor_copy(xw[:].rearrange("p (n h w) -> p n h w", n=8, w=4),
                                          xn[:, 0:N].rearrange("p (h n w) -> p n h w", n=8, w=4)).then_inc(strips, 1)
                    for u in range(U):
                        v.wait_ge(hi_done, i * U + u + 1)
                        v.wait_ge(lo_done, i * U + u + 1)
                        nc.vector.tensor_tensor(rest[:, u % 2], qk_ps[:, u % 2], parts[:, u % 2, 0],
                                                ALU.subtract).then_inc(rest_done, 1)
                    v.wait_ge(l_ready, i + 1)
                    nc.vector.scalar_tensor_tensor(X[:, i, :], l_ps[:], bsum[:], X[:, i, :],
                                                   ALU.add, ALU.add).then_inc(l_added, 1)

            @block.gpsimd
            def _(pool):
                with pool.Fori(0, B) as i:
                    for u in range(U):
                        pool.wait_ge(mid_done, i * U + u + 1)
                        nc.gpsimd.tensor_tensor(parts[:, u % 2, 2], rest[:, u % 2], parts[:, u % 2, 1],
                                                ALU.subtract).then_inc(lo_done, 1)

            @block.scalar
            def _(act):
                act.wait_ge(weights, 1)
                with act.Fori(0, B) as i:
                    act.wait_ge(normed, i + 1)
                    nc.scalar.copy(xp[:, :, 1:W + 1],
                                   xn[:, 0:N].rearrange("p (h w) -> p h w", h=H)).then_inc(padded, 1)
                    for u in range(U):
                        act.wait_ge(qk_ready, i * U + u + 1)
                        act.wait_ge(parts_out[u % 2], (i * 2 + u // 2) * 16 + 16)
                        nc.scalar.copy(parts[:, u % 2, 0], qk_ps[:, u % 2]).then_inc(hi_done, 1)
                        act.wait_ge(v_ready, i * U + u + 1)
                        act.wait_ge(v_out[u % 2], (i * 2 + u // 2) * 16 + 16)
                        nc.scalar.copy(vs[:, u % 2], v_ps[:, u % 2]).then_inc(v_copied, 1)
                        act.wait_ge(rest_done, i * U + u + 3)
                        nc.scalar.copy(parts[:, u % 2, 1], rest[:, u % 2]).then_inc(mid_done, 1)

            @block.tensor
            def _(pe):
                pe.wait_ge(weights, 5)
                with pe.Fori(0, B) as i:
                    pe.wait_ge(strips, i + 1)
                    for u in range(U):
                        src = xw if u % 2 == 0 else xn
                        at = 64 if u == 3 else 0
                        if u == 1:
                            pe.wait_ge(edge, i + 1)
                        pe.wait_ge(rest_done, i * U + u + 1)
                        for c in range(2):
                            last = nc.tensor.matmul(qk_ps[:, u % 2, c * HALF:(c + 1) * HALF], wqk[:, u, :],
                                                    src[:, at + c * HALF:at + (c + 1) * HALF], start=True, stop=True)
                        last.then_inc(qk_ready, 1)
                        pe.wait_ge(v_copied, i * U + u + 1)
                        for w in range(8):
                            last = nc.tensor.matmul(v_ps[:, u % 2, w * 64:(w + 1) * 64],
                                                    src[:, at + w * C:at + (w + 1) * C], wv[:, u, :],
                                                    start=True, stop=True)
                        last.then_inc(v_ready, 1)
                    pe.wait_ge(padded, i + 1)
                    pe.wait_ge(l_added, i + 1)
                    for half in range(2):
                        pieces = lepe_pieces(half)
                        for n, (tap, kind, r, rows, r_in) in enumerate(pieces):
                            last = nc.tensor.matmul(
                                l_ps[:, r * W:(r + rows) * W], wt[:, kind, tap, :],
                                xp[:, r_in:r_in + rows, tap % 3:tap % 3 + W],
                                start=(n == 0), stop=(n == len(pieces) - 1))
                    last.then_inc(l_ready, 1)


def attention(chip, X, dram, qk_rows, v_scr, m_scr, ident, identf, proj_name, bias, subs, kt_quads, scale):
    nc = chip.nc
    windowed = kt_quads == 1
    QB = subs * kt_quads
    NQ = 4 * QB
    NG = 4 * subs
    HB = 4 * subs
    HP = 2 * subs
    LAST = B - 1

    def ends_output(q):
        return 0 <= q < NQ and q % kt_quads == kt_quads - 1

    def norm_at(q):
        return (q - 2) // kt_quads if ends_output(q - 2) else None

    def final_at(q):
        g = (q - 3) // kt_quads
        return g // 4 if ends_output(q - 3) and g % 4 == 3 else None

    def turn_at(q, blocks=4):
        return q // QB - 1 if q and q % QB == 0 and q // QB - 1 < blocks else None

    def order(i, kind):
        for q in range(4 if kind == "drain" else NQ):
            for j in range(4):
                if kind != "drain":
                    yield i, q, j, kind == "last"
                if kind != "first" and q < 4:
                    yield i - 1, q + NQ, j, kind == "drain"

    def numbers(kind):
        st, mx = [], []
        for i, q, j, last in order(1, kind):
            blocks = 2 if last else 4
            if q < NQ:
                st.append((i, "exp", q, j))
                if q // QB < blocks:
                    mx += [(i, "max", q, 2 * j), (i, "max", q, 2 * j + 1)]
            if j == 1:
                if turn_at(q, blocks) is not None:
                    mx += [(i, "turn", turn_at(q, blocks), s) for s in range(subs)]
                if norm_at(q) is not None:
                    st.append((i, "norm", norm_at(q)))
            if j == 2 and final_at(q) is not None:
                st.append((i, "back", final_at(q)))
            if j == 3 and final_at(q) is not None and not windowed:
                st.append((i, "proj", final_at(q)))
        return st, mx

    ST, MX = (len(uses) for uses in numbers("mid"))
    assert ST % 2 == 0 and MX % 2 == 0

    def tables(kind):
        out = []
        for uses, middle, size in zip(numbers(kind), numbers("mid"), (ST, MX)):
            left = 0 if kind == "first" else sum(u[0] == 0 for u in middle)
            out.append({u[1:]: n - left + (size if u[0] == 0 else 0) for n, u in enumerate(uses)})
        return out

    NUMBER = {kind: tables(kind) for kind in ("mid", "first", "last", "drain")}
    for kind in ("first", "last", "drain"):
        NUMBER[kind] = [{**NUMBER["mid"][n], **NUMBER[kind][n]} for n in range(2)]

    def norm_places(g, nt):
        if not windowed:
            at = nt[:, :, g % 4 * 4 * D:(g % 4 + 1) * 4 * D]
            return [(at.rearrange("p t (j d) -> p t j d", d=D), 0, 4, 0, D)]
        shift, sub = g // 4 * 2, g % 2
        part = g // 2 % 2
        at = nt[:, :, 64 * part:64 * part + 64].rearrange("p t (d h) -> p t h d", h=8)
        h = 4 * sub + shift
        if h + 4 <= 8:
            return [(at[:, :, h:h + 4, :], 0, 4, 0, D)]
        return [(at[:, :, h:8, :], 0, 8 - h, 0, D),
                (at[:, :, 0:h - 4, 1:D], 8 - h, h - 4, 0, D - 1),
                (at[:, :, 0:h - 4, 0:1], 8 - h, h - 4, D - 1, 1)]

    def window_places(f, x, turned):
        strips = (x[0:64].rearrange("p (h n w) -> p n h w", n=8, w=4),
                  turned[0:64].rearrange("p (n h w) -> p n h w", n=8, w=4))
        if f == 0:
            return [strips, (x[64:C], turned[64:C])]
        return [strips, (x[64:C, 2 * W:N], turned[64:C, 0:N - 2 * W]), (x[64:C, 0:2 * W], turned[64:C, N - 2 * W:N])]

    MXB = 8 * QB + subs
    MX0 = 2 * MXB

    with chip.stage() as ctx:
        QS = chip.buf(ctx, "QS", [C, 4, HP, N], BF16)
        KS = chip.buf(ctx, "KS", [C, 4, HP, N], BF16)
        VS = chip.buf(ctx, "VS", [C, 2, 8, HB * D])
        VA = chip.buf(ctx, "VA", [C, 2, 8, HB, 32])
        PT = chip.buf(ctx, "PT", [C, 8, N])
        OR = chip.buf(ctx, "OR", [C, 2, N])
        RC = chip.buf(ctx, "RC", [C, 2, 8, 4])
        NT = chip.buf(ctx, "NT", [C, 2, 8, C])
        if not windowed:
            ON = chip.buf(ctx, "ON", [C, N])
            wproj = chip.buf(ctx, "wproj", [C, C])
        unit = chip.buf(ctx, "unit", [C, 1])
        mxv = chip.buf(ctx, "mxv", [C, HB, 8, 1 if windowed else 2])
        nm = chip.buf(ctx, "nm", [C, HB * 8])
        nr = chip.buf(ctx, "nr", [C, 2, HB * 8])
        mp = chip.buf(ctx, "mp", [C, subs, PARTS, 32], BF16)
        mT = chip.buf(ctx, "mT", [PARTS * 32, subs, C], BF16)
        scratch = chip.buf(ctx, "scratch", [1, 16])
        st_ps = chip.psum(ctx, "st_ps", [C, 2, N])
        o_ps = chip.psum(ctx, "o_ps", [C, N])
        mx_ps = chip.psum(ctx, "mx_ps", [C, 2, HALF])
        qk_loaded = [chip.sem("qk_loaded") for _ in range(4)]
        rows_loaded = [chip.sem("rows_loaded") for _ in range(4)]
        v_loaded = [chip.sem("v_loaded") for _ in range(2)]
        st_free = [chip.sem("st_free") for _ in range(2)]
        (w_loaded, filled, rows_out, st_ready, mx_ready, mx_free, pv_done, o_free, va_done, max_taken,
         split, inverted) = (chip.sem(s) for s in (
             "w_loaded", "filled", "rows_out", "st_ready", "mx_ready", "mx_free", "pv_done", "o_free",
             "va_done", "max_taken", "split", "inverted"))
        QK_DMAS = 2 * 2 * len(COMBOS)

        def st_used(i, use):
            return i * ST + use + 1

        def periods(engine, period):
            period(0, "first")
            with engine.Fori(1, LAST) as i:
                period(i, "mid")
            period(LAST, "last")

        def st_wait(use):
            return st_free[use % 2], ST // 2, use // 2 + 2

        with nc.Block() as block:
            @block.sync
            def _(sp):
                def load_qk(i, k):
                    for o, dst in enumerate((QS, KS)):
                        for c, combo in enumerate(COMBOS):
                            rows = qk_rows(i, k, o)[combo[o]].rearrange("(hp e d) t -> e d hp t", e=2, d=D)
                            for e in range(2):
                                at = 64 * e + D * c
                                sp.dma_start(dst[at:at + D, k], rows[e]).then_inc(qk_loaded[k], 16)

                def load_v(i, k, slot):
                    sp.dma_start(VS[:, slot].rearrange("p t c -> p (t c)"), v_scr[i, k]).then_inc(v_loaded[slot], 16)

                def load_rows(k, half, copies, written):
                    sp.wait_ge(mx_free, copies)
                    for s in range(subs):
                        sp.dma_start(m_scr[half, s].rearrange("a h t q -> (a h t) q"), mT[:, s]).then_inc(rows_out, 16)
                    sp.wait_ge(rows_out, written)
                    for s in range(subs):
                        src = m_scr[half, s].rearrange("a (hp e) t q -> e a hp (t q)", e=2)
                        for e in range(2):
                            sp.dma_start(QS[64 * e + STACK:64 * e + ROWS, k, 2 * s:2 * s + 2, :],
                                         src[e]).then_inc(rows_loaded[k], 16)

                if not windowed:
                    sp.dma_start(wproj[:], dram[proj_name]).then_inc(w_loaded, 16)
                sp.wait_ge(filled, 3)
                load_v(0, 0, 0)
                load_v(0, 1, 1)
                for k in range(4):
                    load_qk(0, k)
                sp.wait_ge(va_done, 1)
                load_v(0, 2, 0)
                for k in range(2):
                    load_rows(k, k, (k + 1) * MXB + 2, 16 * subs * (k + 1))

                def image(i, kind):
                    last = kind == "last"
                    st_use, mx_use = NUMBER[kind]
                    for k in range(4):
                        if turn_at(k * QB) is not None:
                            if not last or k - 1 < 2:
                                load_rows((k + 1) % 4, (k + 1) % 2, i * MX + (MX0 + 2 + 1 + mx_use["turn", k - 1, subs - 1]),
                                          (i * 4 + k - 1) * (16 * subs) + 16 * subs * 3)
                        if not last:
                            sp.wait_ge(st_ready, st_used(i, st_use["exp", (k + 1) * QB - 1, 3]))
                            load_qk(i + 1, k)
                        if not last or k == 0:
                            sp.wait_ge(va_done, i * 4 + k + 2)
                            load_v(i + (k + 3) // 4, (k + 3) % 4, (k + 3) % 2)
                    if not last:
                        load_rows(1, 1, i * MX + (MX0 + 2 + 1 + mx_use["turn", 3, subs - 1]),
                                  (i * 4 + 3) * (16 * subs) + 16 * subs * 3)

                periods(sp, image)

            @block.tensor
            def _(pe):
                def stack(buf, k, h, rows):
                    e = h % 2
                    return buf[64 * e:64 * e + rows, k, h // 2, :]

                def max_scores(k, n, slot):
                    if windowed:
                        q, kk = (stack(b, k, n // 2, STACK) for b in (QS, KS))
                        for w in range(4):
                            at = ((n % 2) * 4 + w) * C
                            mm = nc.tensor.matmul(mx_ps[:, slot, w * C:(w + 1) * C], q[:, at:at + C], kk[:, at:at + C],
                                                  start=True, stop=True)
                    else:
                        q, kk = (stack(b, k, n // 16, STACK) for b in (QS, KS))
                        at = (n // 2 % 8) * C
                        mm = nc.tensor.matmul(mx_ps[:, slot, :], q[:, at:at + C],
                                              kk[:, (n % 2) * HALF:(n % 2 + 1) * HALF], start=True, stop=True)
                    mm.then_inc(mx_ready, 1)

                def turn(s, slot):
                    nc.tensor.transpose(mx_ps[0:PARTS * 32, slot, 0:C // 2].bitcast(BF16), mp[:, s].rearrange("p a c -> p (a c)"),
                                        ident[:]).then_inc(mx_ready, 1)

                pe.wait_ge(filled, 3)
                for k in range(2):
                    pe.wait_ge(qk_loaded[k], 16 * QK_DMAS)
                    for n in range(8 * QB):
                        pe.wait_ge(mx_free, k * MXB + n + 1)
                        max_scores(k, n, (k * MXB + n) % 2)
                    pe.wait_ge(split, 4 * (k + 1))
                    for s in range(subs):
                        pe.wait_ge(mx_free, k * MXB + 8 * QB + s + 1)
                        turn(s, (k * MXB + 8 * QB + s) % 2)

                def values(i, q, half, st_use):
                    k, s, kt, g = q // QB, q // kt_quads % subs, q % kt_quads, q // kt_quads
                    if q % QB == 0 and half == 0:
                        pe.wait_ge(va_done, i * 4 + k + 1)
                    if kt == 0:
                        pe.wait_ge(o_free, i * (2 * NG) + 2 * g + half + 1)
                    if half == 0:
                        for use in {st_use["exp", q, j] % 2: st_use["exp", q, j] for j in range(4)}.values():
                            sem, per, val = st_wait(use)
                            pe.wait_ge(sem, i * per + val)
                    width = C if windowed else HALF
                    for t in range(HALF * half // width, HALF * (half + 1) // width):
                        for j in range(4):
                            mm = nc.tensor.matmul(
                                o_ps[32 * j:32 * j + 32, t * width:(t + 1) * width],
                                VA[:, k % 2, t if windowed else kt, 4 * s + j, :],
                                PT[:, (q % 2) * 4 + j, t * width:(t + 1) * width],
                                start=(kt == 0), stop=(kt == kt_quads - 1))
                    mm.then_inc(pv_done, 1)

                def step(i, q, j, last, st_use, mx_use):
                    k, s, kt = q // QB, q // kt_quads % subs, q % kt_quads
                    if q < NQ:
                        if q % QB == 0 and j == 0:
                            pe.wait_ge(qk_loaded[k], (i + 1) * (16 * QK_DMAS))
                            pe.wait_ge(rows_loaded[k], (i + 1) * (16 * 2 * subs))
                        use = st_use["exp", q, j]
                        sem, per, _ = st_wait(use)
                        pe.wait_ge(sem, i * per + use // 2 + 1)
                        qq, kk = (stack(b, k, 4 * s + j, ROWS) for b in (QS, KS))
                        if windowed:
                            for w in range(8):
                                mm = nc.tensor.matmul(st_ps[:, use % 2, w * C:(w + 1) * C], kk[:, w * C:(w + 1) * C],
                                                      qq[:, w * C:(w + 1) * C], start=True, stop=True)
                        else:
                            for c in range(2):
                                mm = nc.tensor.matmul(st_ps[:, use % 2, c * HALF:(c + 1) * HALF],
                                                      kk[:, kt * C:(kt + 1) * C],
                                                      qq[:, c * HALF:(c + 1) * HALF], start=True, stop=True)
                        mm.then_inc(st_ready, 1)
                    with_max = q < NQ and (not last or k < 2)
                    if with_max and q % QB == 0 and j == 0:
                        pe.wait_ge(qk_loaded[(k + 2) % 4], (i + (1 if k < 2 else 2)) * (16 * QK_DMAS))
                    for x in (2 * j, 2 * j + 1):
                        if with_max:
                            pe.wait_ge(mx_free, i * MX + (MX0 + mx_use["max", q, x] + 1))
                            max_scores((k + 2) % 4, (q % QB) * 8 + x, mx_use["max", q, x] % 2)
                        if x % 4 == 2 and 1 <= q <= NQ:
                            values(i, q - 1, x // 4, st_use)
                    if j == 1 and turn_at(q, 2 if last else 4) is not None:
                        m = turn_at(q)
                        pe.wait_ge(split, i * 16 + 4 * (2 + m + 1))
                        for s2 in range(subs):
                            use = mx_use["turn", m, s2]
                            pe.wait_ge(mx_free, i * MX + (MX0 + use + 1))
                            turn(s2, use % 2)
                    if j == 1 and norm_at(q) is not None:
                        g = norm_at(q)
                        use = st_use["norm", g]
                        sem, per, _ = st_wait(use)
                        pe.wait_ge(o_free, i * (2 * NG) + 2 * g + 4)
                        pe.wait_ge(sem, i * per + use // 2 + 1)
                        for t in range(8):
                            mm = nc.tensor.transpose(st_ps[:, use % 2, t * C:(t + 1) * C],
                                                     OR[:, g % 2, t * C:(t + 1) * C], identf[:])
                        mm.then_inc(st_ready, 1)
                    if j == 2 and final_at(q) is not None:
                        f = final_at(q)
                        use = st_use["back", f]
                        sem, per, _ = st_wait(use)
                        norm_sem, norm_per, norm_val = st_wait(st_use["norm", 4 * f + 3])
                        if norm_sem is not sem:
                            pe.wait_ge(norm_sem, i * norm_per + norm_val)
                        pe.wait_ge(sem, i * per + use // 2 + 1)
                        for t in range(8):
                            mm = nc.tensor.transpose(st_ps[:, use % 2, t * C:(t + 1) * C], NT[:, f % 2, t, :], identf[:])
                        mm.then_inc(st_ready, 1)
                    if j == 3 and final_at(q) is not None and not windowed:
                        use = st_use["proj", final_at(q)]
                        sem, per, _ = st_wait(use)
                        back_sem, back_per, back_val = st_wait(st_use["back", final_at(q)])
                        pe.wait_ge(w_loaded, 16)
                        if back_sem is not sem:
                            pe.wait_ge(back_sem, i * back_per + back_val)
                        pe.wait_ge(sem, i * per + use // 2 + 1)
                        for c in range(2):
                            mm = nc.tensor.matmul(st_ps[:, use % 2, c * HALF:(c + 1) * HALF], wproj[:],
                                                  ON[:, c * HALF:(c + 1) * HALF], start=True, stop=True)
                        mm.then_inc(st_ready, 1)

                def period(i, kind):
                    for n, q, j, last in order(i, kind):
                        step(n, q, j, last, *NUMBER[kind])

                periods(pe, period)
                period(B, "drain")

            @block.scalar
            def _(act):
                def take_half(i, q, half, st_use):
                    g = q // kt_quads
                    act.wait_ge(pv_done, i * (2 * NQ) + 2 * q + half + 5)
                    if g >= 2:
                        sem, per, val = st_wait(st_use["norm", g - 2])
                        act.wait_ge(sem, i * per + val)
                    at = slice(half * HALF, (half + 1) * HALF)
                    nc.scalar.copy(OR[:, g % 2, at], o_ps[:, at]).then_inc(o_free, 1)

                def step(i, q, j, st_use):
                    if q < NQ:
                        use = st_use["exp", q, j]
                        act.wait_ge(st_ready, st_used(i, use))
                        act.wait_ge(pv_done, i * (2 * NQ) + 2 * q + 2)
                        nc.scalar.activation(PT[:, (q % 2) * 4 + j], st_ps[:, use % 2], ACT.Exp,
                                             scale=scale).then_inc(st_free[use % 2], 1)
                    if j == 0 and ends_output(q - 2):
                        take_half(i, q - 2, 1, st_use)
                    if j == 2 and ends_output(q - 1):
                        take_half(i, q - 1, 0, st_use)
                    if j == 2 and final_at(q) is not None and not windowed:
                        use = st_use["back", final_at(q)]
                        act.wait_ge(st_ready, st_used(i, use))
                        nc.scalar.copy(ON[:], st_ps[:, use % 2]).then_inc(st_free[use % 2], 1)

                def period(i, kind):
                    for n, q, j, _ in order(i, kind):
                        step(n, q, j, NUMBER[kind][0])

                periods(act, period)
                period(B, "drain")

            @block.vector
            def _(v):
                nc.vector.memset(QS[:], 1.0).then_inc(filled, 1)
                nc.vector.memset(KS[:], 1.0).then_inc(filled, 1)
                nc.vector.memset(VA[:], 0.0).then_inc(filled, 1)
                v.wait_ge(filled, 3)
                nc.vector.memset(unit[:], 1.0)
                nc.vector.memset(VA[:, :, :, :, D:D + 1], 1.0).then_inc(filled, 1)
                grant(nc, scratch, [(st_free[0], 1), (st_free[1], 1), (mx_free, 2), (pv_done, 4), (o_free, 2)])

                def reduce_half(n, slot):
                    if windowed:
                        nc.vector.tensor_reduce(mxv[:, n // 2, (n % 2) * 4:(n % 2) * 4 + 4, 0],
                                                mx_ps[:, slot].rearrange("p (w k) -> p w k", w=4),
                                                AX.X, ALU.max).then_inc(mx_free, 1)
                    else:
                        nc.vector.tensor_reduce(mxv[:, n // 16, n // 2 % 8, n % 2:n % 2 + 1], mx_ps[:, slot],
                                                AX.X, ALU.max).then_inc(mx_free, 1)

                def take_max(freed):
                    v.wait_ge(mx_free, freed)
                    nc.vector.tensor_reduce(nm[:], mxv[:].rearrange("p h t c -> p (h t) c"), AX.X, ALU.max,
                                            negate=True).then_inc(max_taken, 1)

                def copy_turned(s, slot):
                    nc.vector.tensor_copy(mT[:, s], mx_ps[0:PARTS * 32, slot, 0:C // 2].bitcast(BF16)).then_inc(mx_free, 1)

                for k in range(2):
                    if k:
                        v.wait_ge(max_taken, k)
                    for n in range(8 * QB):
                        v.wait_ge(mx_ready, k * MXB + n + 1)
                        reduce_half(n, (k * MXB + n) % 2)
                    take_max(k * MXB + 8 * QB + 2)
                    if k:
                        v.wait_ge(rows_out, 16 * subs * k)
                    for s in range(subs):
                        use = k * MXB + 8 * QB + s
                        v.wait_ge(mx_ready, use + 1)
                        copy_turned(s, use % 2)

                def normalise(i, g, st_use):
                    use = st_use["norm", g]
                    turned = st_ps[:, use % 2].rearrange("p (t j r) -> p t j r", t=8, j=4)
                    v.wait_ge(st_ready, st_used(i, use))
                    nc.vector.reciprocal(RC[:, g % 2], turned[:, :, :, D]).then_inc(inverted, 1)
                    v.wait_ge(inverted, i * NG + g + 1)
                    for dst, j0, js, d0, ds in norm_places(g, NT[:, g // 4 % 2]):
                        ins = nc.vector.tensor_tensor(
                            dst, turned[:, :, j0:j0 + js, d0:d0 + ds],
                            RC[:, g % 2, :, j0:j0 + js].unsqueeze(3).to_broadcast([C, 8, js, ds]), ALU.mult)
                    ins.then_inc(st_free[use % 2], 1)

                def step(i, q, j, last, st_use, mx_use):
                    k = q // QB
                    if q < NQ and (not last or k < 2):
                        if q % QB == 0 and j == 0:
                            v.wait_ge(max_taken, i * 4 + k + 2)
                        for x in (2 * j, 2 * j + 1):
                            v.wait_ge(mx_ready, i * MX + (MX0 + mx_use["max", q, x] + 1))
                            reduce_half((q % QB) * 8 + x, mx_use["max", q, x] % 2)
                    if j == 1 and turn_at(q, 2 if last else 4) is not None:
                        m = turn_at(q)
                        v.wait_ge(rows_out, (i * 4 + m) * (16 * subs) + 16 * subs * 2)
                        for s in range(subs):
                            use = mx_use["turn", m, s]
                            v.wait_ge(mx_ready, i * MX + (MX0 + use + 1))
                            copy_turned(s, use % 2)
                    if j == 1 and norm_at(q) is not None:
                        normalise(i, norm_at(q), st_use)
                    if j == 2 and final_at(q) is not None and windowed:
                        f = final_at(q)
                        use = st_use["back", f]
                        v.wait_ge(st_ready, st_used(i, use))
                        for dst, src in window_places(f, X[:, i, :], st_ps[:, use % 2]):
                            ins = nc.vector.tensor_tensor(dst, src, dst, ALU.add)
                        ins.then_inc(st_free[use % 2], 1)
                    if j == 3 and final_at(q) is not None and not windowed:
                        use = st_use["proj", final_at(q)]
                        v.wait_ge(st_ready, st_used(i, use))
                        nc.vector.scalar_tensor_tensor(X[:, i, :], st_ps[:, use % 2], bias[:], X[:, i, :],
                                                       ALU.add, ALU.add).then_inc(st_free[use % 2], 1)
                    if j == 3 and q < NQ and (q + 1) % QB == 0 and (not last or k < 2):
                        take_max(i * MX + (MX0 + 2 + mx_use["max", q, 7] + 1))

                def period(i, kind):
                    for n, q, j, last in order(i, kind):
                        step(n, q, j, last, *NUMBER[kind])

                periods(v, period)
                period(B, "drain")

            @block.gpsimd
            def _(pool):
                def copy(dst, src):
                    one = unit[:]
                    while len(one.shape) < len(src.shape):
                        one = one.unsqueeze(1)
                    return nc.gpsimd.tensor_tensor(dst, src, one.to_broadcast(list(src.shape)), ALU.mult)

                def expand_v(k, slot):
                    copy(VA[:, slot, :, :, 0:D], VS[:, slot].rearrange("p t (h d) -> p t h d", d=D)).then_inc(va_done, 1)

                def split_max(taken, base):
                    view = nm[:].rearrange("p (s c) -> p s c", s=subs)
                    rv = [nr[:, n].rearrange("p (s c) -> p s c", s=subs) for n in range(2)]
                    pool.wait_ge(max_taken, taken)
                    copy(mp[:, :, 0], view).then_inc(split, 1)
                    pool.wait_ge(split, base + 1)
                    nc.gpsimd.tensor_tensor(rv[0], view, mp[:, :, 0], ALU.subtract).then_inc(split, 1)
                    pool.wait_ge(split, base + 2)
                    copy(mp[:, :, 1], rv[0]).then_inc(split, 1)
                    pool.wait_ge(split, base + 3)
                    nc.gpsimd.tensor_tensor(mp[:, :, 2], rv[0], mp[:, :, 1], ALU.subtract).then_inc(split, 1)

                pool.wait_ge(filled, 4)
                pool.wait_ge(v_loaded[0], 16)
                expand_v(0, 0)
                for k in range(2):
                    split_max(k + 1, 4 * k)

                def image(i, last):
                    for q in range(NQ):
                        k = q // QB
                        if q % QB == 1 and (not last or k < 3):
                            pool.wait_ge(v_loaded[(k + 1) % 2], (i * 2 + (k + 1) // 2) * 16 + 16)
                            pool.wait_ge(pv_done, i * (2 * NQ) + 2 * k * QB + 4)
                            expand_v((k + 1) % 4, (k + 1) % 2)
                        if (q + 1) % QB == 0 and (not last or k < 2):
                            split_max(i * 4 + k + 3, i * 16 + 4 * (2 + k))

                with pool.Fori(0, LAST) as i:
                    image(i, False)
                image(LAST, True)


PE_TAPS = (0, 1, 2, 3, 5, 6)


def conv_stage(chip, X, dram, mean_g, rstd_g, pooled, eps5, identf):
    nc = chip.nc
    VE_TAPS = [t for t in range(9) if t not in PE_TAPS]
    with chip.stage() as ctx:
        w1, w2 = chip.buf(ctx, "se_w1", [C, C // 4]), chip.buf(ctx, "se_w2", [C // 4, C])
        rw, rb = chip.buf(ctx, "rw", [C, 9]), chip.buf(ctx, "rb", [C, 1])
        diag = chip.buf(ctx, "diag", [C, len(PE_TAPS), C])
        h, hl = chip.buf(ctx, "se_h", [C // 4, B]), chip.buf(ctx, "se_hl", [C // 4, B])
        gate = chip.buf(ctx, "se_gate", [C, B])
        scale = chip.buf(ctx, "scale", [C, B, 1])
        xp = chip.buf(ctx, "xp", [C, 2, H + 2, W + 2])
        acc, z = chip.buf(ctx, "acc", [C, 2, N]), chip.buf(ctx, "z", [C, 2, N])
        st, mv = chip.buf(ctx, "st", [C, 2, 12]), chip.buf(ctx, "mv", [C, 2, 2])
        sd, rs, nb, pause = (chip.buf(ctx, n, [C, 2, 1]) for n in ("sd", "rs", "nb", "pause"))
        scratch = chip.buf(ctx, "scratch", [1, 8])
        ps = chip.psum(ctx, "se_ps", [C, 2, HALF])
        c_ps = chip.psum(ctx, "c_ps", [C, 2, N])
        w_loaded, squeezed, chain, gated, padded, conv, aggr, rooted, scaled, ascaled, added = (chip.sem(s) for s in (
            "w_loaded", "squeezed", "chain", "gated", "padded", "conv", "aggr", "rooted", "scaled", "ascaled", "added"))
        with nc.Block() as block:
            @block.sync
            def _(sp):
                for dst, name in ((w1, "se_w1"), (w2, "se_w2"), (rw, "refine_w"), (rb, "refine_b")):
                    sp.dma_start(dst[:], dram[name]).then_inc(w_loaded, 16)
                sp.wait_ge(w_loaded, 64)

            @block.tensor
            def _(pe):
                pe.wait_ge(w_loaded, 64)
                nc.tensor.matmul(ps[0:C // 4, 0, 0:B], w1[:], pooled[:], start=True, stop=True).then_inc(squeezed, 1)
                pe.wait_ge(chain, 4)
                nc.tensor.matmul(ps[:, 1, 0:B], w2[:], hl[:], start=True, stop=True).then_inc(squeezed, 1)
                with pe.Fori(0, B // 2) as i:
                    for s in range(2):
                        pe.wait_ge(padded, i * 2 + s + 1)
                        pe.wait_ge(added, i * 2 + s + 1)
                        for half in range(2):
                            for n, t in enumerate(PE_TAPS):
                                r = 16 * half + t // 3
                                mm = nc.tensor.matmul(c_ps[:, s, half * HALF:(half + 1) * HALF], diag[:, n, :],
                                                      xp[:, s, r:r + 16, t % 3:t % 3 + W],
                                                      start=(n == 0), stop=(n == len(PE_TAPS) - 1))
                        mm.then_inc(conv, 1)

            @block.scalar
            def _(act):
                act.wait_ge(squeezed, 2)
                nc.scalar.activation(gate[:], ps[:, 1, 0:B], ACT.Sigmoid).then_inc(gated, 1)
                with act.Fori(0, B // 2) as i:
                    for s in range(2):
                        act.wait_ge(aggr, i * 2 + s + 1)
                        nc.scalar.activation(sd[:, s], mv[:, s, 1:2], ACT.Sqrt, bias=eps5[:]).then_inc(rooted, 1)
                    for s in range(2):
                        act.wait_ge(scaled, i * 2 + s + 1)
                        nc.scalar.activation(z[:, s], acc[:, s], ACT.Identity, bias=nb[:, s], scale=rs[:, s]).then_inc(ascaled, 1)

            @block.vector
            def _(v):
                count = [0]

                def chained(ins):
                    count[0] += 1
                    ins.then_inc(chain, 1)
                    v.wait_ge(chain, count[0])

                grant(nc, scratch, [(added, 2)])
                chained(nc.vector.memset(xp[:], 0.0))
                v.wait_ge(w_loaded, 64)
                for n, t in enumerate(PE_TAPS):
                    ins = nc.vector.tensor_scalar(diag[:, n, :], identf[:], rw[:, t:t + 1], None, ALU.mult)
                chained(ins)
                v.wait_ge(squeezed, 1)
                chained(nc.vector.tensor_copy(h[:], ps[0:C // 4, 0, 0:B]))
                chained(nc.vector.scalar_tensor_tensor(hl[:], h[:], 0.01, h[:], ALU.mult, ALU.max))
                v.wait_ge(gated, 1)
                chained(nc.vector.tensor_tensor(scale[:].rearrange("p b o -> p (b o)"), gate[:],
                                                rstd_g[:].rearrange("p b o -> p (b o)"), ALU.mult))
                base = count[0]
                STEPS = len(VE_TAPS) + 4
                with v.Fori(0, B // 2) as i:
                    step = [0]

                    def then(ins):
                        step[0] += 1
                        ins.then_inc(chain, 1)
                        return step[0]

                    def after(n):
                        v.wait_ge(chain, i * (2 * STEPS) + (base + n))

                    done = [0, 0]
                    for s in range(2):
                        nc.vector.tensor_scalar(xp[:, s, 1:H + 1, 1:W + 1],
                                                X[:, i * 2 + s, :].rearrange("p (h w) -> p h w", h=H),
                                                mean_g[:, i * 2 + s, :], scale[:, i * 2 + s, :],
                                                ALU.subtract, ALU.mult).then_inc(padded, 1)
                    for s in range(2):
                        v.wait_ge(padded, i * 2 + s + 1)
                        t = VE_TAPS[0]
                        done[s] = then(nc.vector.tensor_scalar(
                            acc[:, s].rearrange("p (h w) -> p h w", h=H), xp[:, s, t // 3:t // 3 + H, t % 3:t % 3 + W],
                            rw[:, t:t + 1], rb[:], ALU.mult, ALU.add))
                    for t in VE_TAPS[1:]:
                        for s in range(2):
                            after(done[s])
                            src = xp[:, s, t // 3:t // 3 + H, t % 3:t % 3 + W]
                            out = acc[:, s].rearrange("p (h w) -> p h w", h=H)
                            done[s] = then(nc.vector.scalar_tensor_tensor(out, src, rw[:, t:t + 1], out, ALU.mult, ALU.add))
                    for s in range(2):
                        v.wait_ge(conv, i * 2 + s + 1)
                        after(done[s])
                        done[s] = then(nc.vector.tensor_tensor(acc[:, s], c_ps[:, s], acc[:, s], ALU.add))
                    for s in range(2):
                        after(done[s])
                        for c in range(2):
                            ins = nc.vector.bn_stats(st[:, s, 6 * c:6 * c + 6], acc[:, s, c * HALF:(c + 1) * HALF])
                        done[s] = then(ins)
                    for s in range(2):
                        after(done[s])
                        nc.vector.memset(pause[:, s], 0.0)
                        nc.vector.bn_aggr(mv[:, s], st[:, s]).then_inc(aggr, 1)
                    for s in range(2):
                        v.wait_ge(rooted, i * 2 + s + 1)
                        done[s] = then(nc.vector.reciprocal(rs[:, s], sd[:, s]))
                    for s in range(2):
                        after(done[s])
                        nc.vector.scalar_tensor_tensor(nb[:, s], mv[:, s, 0:1], -1.0, rs[:, s],
                                                       ALU.mult, ALU.mult).then_inc(scaled, 1)
                    for s in range(2):
                        v.wait_ge(ascaled, i * 2 + s + 1)
                        done[s] = then(nc.vector.scalar_tensor_tensor(z[:, s], z[:, s], 0.01, z[:, s], ALU.mult, ALU.max))
                    for s in range(2):
                        after(done[s])
                        nc.vector.tensor_tensor(X[:, i * 2 + s, :], X[:, i * 2 + s, :], z[:, s], ALU.add).then_inc(added, 1)
                    assert step[0] == 2 * STEPS, step[0]


def layer_norm(chip, src, mean_w, eps5, identf, dst=None, X=None, gamma=None, beta=None):
    nc = chip.nc
    TILES = HALF // C
    with chip.stage() as ctx:
        xc, sq, t = (chip.buf(ctx, n, [C, 2, HALF]) for n in ("xc", "sq", "t"))
        sd, rs = (chip.buf(ctx, n, [C, 2, TILES]) for n in ("sd", "rs"))
        scratch = chip.buf(ctx, "scratch", [1, 8])
        m_ps, v_ps, r_ps = (chip.psum(ctx, n, [C, 2, HALF]) for n in ("m_ps", "v_ps", "r_ps"))
        mean_ready, centred, squared, var_ready, rooted, inverted, spread, scaled, stored = (chip.sem(s) for s in (
            "mean_ready", "centred", "squared", "var_ready", "rooted", "inverted", "spread", "scaled", "stored"))
        with nc.Block() as block:
            @block.tensor
            def _(pe):
                with pe.Fori(0, B) as i:
                    for c in range(2):
                        pe.wait_ge(centred, i * 2 + c + 1)
                        nc.tensor.matmul(m_ps[:, c], mean_w[:], src[:, i, c * HALF:(c + 1) * HALF],
                                         start=True, stop=True).then_inc(mean_ready, 1)
                    for c in range(2):
                        pe.wait_ge(squared, i * 2 + c + 1)
                        pe.wait_ge(rooted, i * 2 + c + 1)
                        for n in range(TILES):
                            mm = nc.tensor.matmul(v_ps[:, c, n:n + 1], sq[:, c, n * C:(n + 1) * C], mean_w[:, 0:1],
                                                  start=True, stop=True)
                        mm.then_inc(var_ready, 1)
                    for c in range(2):
                        pe.wait_ge(inverted, i * 2 + c + 1)
                        pe.wait_ge(scaled, i * 2 + c + 1)
                        for n in range(TILES):
                            mm = nc.tensor.matmul(r_ps[:, c, n * C:(n + 1) * C],
                                                  rs[:, c, n:n + 1].to_broadcast([C, C]), identf[:], start=True, stop=True)
                        mm.then_inc(spread, 1)

            @block.scalar
            def _(act):
                with act.Fori(0, B) as i:
                    for c in range(2):
                        act.wait_ge(centred, i * 2 + c + 3)
                        act.wait_ge(var_ready, i * 2 + c + 1)
                        nc.scalar.activation(sq[:, c], xc[:, c], ACT.Square).then_inc(squared, 1)
                    for c in range(2):
                        act.wait_ge(var_ready, i * 2 + c + 3)
                        nc.scalar.activation(sd[:, c], v_ps[:, c, 0:TILES], ACT.Sqrt, bias=eps5[:]).then_inc(rooted, 1)

            @block.vector
            def _(v):
                grant(nc, scratch, [(centred, 2), (rooted, 2), (var_ready, 2), (scaled, 2)])
                with v.Fori(0, B) as i:
                    for c in range(2):
                        v.wait_ge(mean_ready, i * 2 + c + 1)
                        v.wait_ge(scaled, i * 2 + c + 1)
                        nc.vector.tensor_tensor(xc[:, c], src[:, i, c * HALF:(c + 1) * HALF], m_ps[:, c],
                                                ALU.subtract).then_inc(centred, 1)
                    for c in range(2):
                        v.wait_ge(rooted, i * 2 + c + 3)
                        nc.vector.reciprocal(rs[:, c], sd[:, c]).then_inc(inverted, 1)
                    for c in range(2):
                        v.wait_ge(spread, i * 2 + c + 1)
                        if dst is not None:
                            nc.vector.tensor_tensor(dst[:, i, c * HALF:(c + 1) * HALF], xc[:, c], r_ps[:, c],
                                                    ALU.mult).then_inc(scaled, 1)
                            continue
                        nc.vector.scalar_tensor_tensor(t[:, c], xc[:, c], gamma[:], r_ps[:, c],
                                                       ALU.mult, ALU.mult).then_inc(scaled, 1)
                        v.wait_ge(scaled, i * 2 + c + 3)
                        at = X[:, i, c * HALF:(c + 1) * HALF]
                        nc.vector.scalar_tensor_tensor(at, t[:, c], beta[:], at, ALU.add, ALU.add).then_inc(stored, 1)


def token_projections(chip, XN, dram, qk_scr, v_scr):
    nc = chip.nc
    with chip.stage() as ctx:
        wqk, wv = chip.buf(ctx, "wqk", [C, 2, C]), chip.buf(ctx, "wv", [C, C])
        bqk, bv = chip.buf(ctx, "bqk", [C, 2]), chip.buf(ctx, "bv", [C, C])
        xs = chip.buf(ctx, "xs", [C, N])
        parts = chip.buf(ctx, "parts", [C, 2, PARTS, N], BF16)
        rest = chip.buf(ctx, "rest", [C, 2, N])
        vs = chip.buf(ctx, "vs", [C, 4, 8, 32])
        scratch = chip.buf(ctx, "scratch", [1, 8])
        qk_ps = chip.psum(ctx, "qk_ps", [C, 2, N])
        v_ps = chip.psum(ctx, "v_ps", [C, 8, C])
        w_loaded, staged, qk_ready, hi_done, rest_done, mid_done, lo_done, v_ready, v_copied, v_out = (
            chip.sem(s) for s in ("w_loaded", "staged", "qk_ready", "hi_done", "rest_done", "mid_done", "lo_done",
                                  "v_ready", "v_copied", "v_out"))
        parts_out = [chip.sem("parts_out") for _ in range(2)]
        with nc.Block() as block:
            @block.sync
            def _(sp):
                for dst, name in ((wqk, "w2_qk"), (wv, "w2_v"), (bqk, "b2_qk")):
                    sp.dma_start(dst[:], dram[name]).then_inc(w_loaded, 16)
                sp.dma_start(bv[:], dram["b2_v"].to_broadcast([C, C])).then_inc(w_loaded, 16)
                with sp.Fori(0, B) as i:
                    for u in range(2):
                        sp.wait_ge(lo_done, i * 2 + u + 3)
                        sp.dma_start(qk_scr[i, u].rearrange("a r t -> r a t"), parts[:, u]).then_inc(parts_out[u], 16)
                    sp.wait_ge(v_copied, i + 2)
                    sp.dma_start(v_scr[i].rearrange("k p c -> p k c"),
                                 vs[:].rearrange("p k t c -> p k (t c)")).then_inc(v_out, 16)
                for s in (*parts_out, v_out):
                    sp.wait_ge(s, 16 * (B + 1))

            @block.tensor
            def _(pe):
                pe.wait_ge(w_loaded, 64)
                with pe.Fori(0, B) as i:
                    pe.wait_ge(staged, i + 1)
                    for u in range(2):
                        pe.wait_ge(rest_done, i * 2 + u + 1)
                        for c in range(2):
                            mm = nc.tensor.matmul(qk_ps[:, u, c * HALF:(c + 1) * HALF], wqk[:, u, :],
                                                  xs[:, c * HALF:(c + 1) * HALF], start=True, stop=True)
                        mm.then_inc(qk_ready, 1)
                    pe.wait_ge(v_copied, i + 1)
                    for t in range(8):
                        mm = nc.tensor.matmul(v_ps[:, t, :], xs[:, t * C:(t + 1) * C], wv[:], start=True, stop=True)
                    mm.then_inc(v_ready, 1)

            @block.scalar
            def _(act):
                act.wait_ge(w_loaded, 64)
                with act.Fori(0, B) as i:
                    for u in range(2):
                        act.wait_ge(qk_ready, i * 2 + u + 1)
                        act.wait_ge(parts_out[u], i * 16 + 16)
                        nc.scalar.activation(parts[:, u, 0], qk_ps[:, u], ACT.Identity,
                                             bias=bqk[:, u:u + 1]).then_inc(hi_done, 1)
                    for u in range(2):
                        act.wait_ge(rest_done, i * 2 + u + 3)
                        nc.scalar.copy(parts[:, u, 1], rest[:, u]).then_inc(mid_done, 1)

            @block.gpsimd
            def _(pool):
                with pool.Fori(0, B) as i:
                    for u in range(2):
                        pool.wait_ge(mid_done, i * 2 + u + 1)
                        nc.gpsimd.tensor_tensor(parts[:, u, 2], rest[:, u], parts[:, u, 1],
                                                ALU.subtract).then_inc(lo_done, 1)

            @block.vector
            def _(v):
                grant(nc, scratch, [(rest_done, 2), (lo_done, 2), (v_copied, 1), (parts_out[0], 16),
                                    (parts_out[1], 16), (v_out, 16), (v_ready, 1)])
                v.wait_ge(w_loaded, 64)
                with v.Fori(0, B) as i:
                    v.wait_ge(v_ready, i + 1)
                    nc.vector.tensor_copy(xs[:], XN[:, i, :]).then_inc(staged, 1)
                    for u in range(2):
                        v.wait_ge(hi_done, i * 2 + u + 1)
                        v.wait_ge(lo_done, i * 2 + u + 1)
                        nc.vector.scalar_tensor_tensor(rest[:, u], qk_ps[:, u], bqk[:, u:u + 1], parts[:, u, 0],
                                                       ALU.add, ALU.subtract).then_inc(rest_done, 1)
                    v.wait_ge(v_ready, i + 2)
                    v.wait_ge(v_out, i * 16 + 16)
                    for k in range(4):
                        ins = nc.vector.tensor_tensor(vs[:, k], v_ps[:, :, 32 * k:32 * k + 32],
                                                      bv[:, 32 * k:32 * k + 32].unsqueeze(1).to_broadcast([C, 8, 32]), ALU.add)
                    ins.then_inc(v_copied, 1)


def route(chip, XN, dram, w_name, identf, prefer, guard, g_scr):
    nc = chip.nc
    T = B * 8
    with chip.stage() as ctx:
        wr = chip.buf(ctx, "wr", [C, E])
        xs = chip.buf(ctx, "xs", [C, 2, N])
        L, P, M, G = (chip.buf(ctx, n, [C, T, E]) for n in ("L", "P", "M", "G"))
        m1, m2, r = (chip.buf(ctx, n, [C, T]) for n in ("m1", "m2", "r"))
        gt = chip.buf(ctx, "gt", [E * 8, B, C])
        scratch = chip.buf(ctx, "scratch", [1, 8])
        l_ps = chip.psum(ctx, "l_ps", [C, 2, HALF])
        g_ps = chip.psum(ctx, "g_ps", [C, B, C])
        w_loaded, staged, logits, copied, chain, expd, gates, turned, gcopied, out = (chip.sem(s) for s in (
            "w_loaded", "staged", "logits", "copied", "chain", "expd", "gates", "turned", "gcopied", "out"))
        wide = lambda a: a[:].unsqueeze(2).to_broadcast([C, T, E])
        with nc.Block() as block:
            @block.sync
            def _(sp):
                sp.dma_start(wr[:], dram[w_name]).then_inc(w_loaded, 16)
                for half in range(2):
                    sp.wait_ge(gcopied, half + 1)
                    for i in range(4 * half, 4 * half + 4):
                        sp.dma_start(g_scr[i].rearrange("e (t q) -> (e t) q", q=C), gt[:, i]).then_inc(out, 16)
                sp.wait_ge(out, 16 * B)

            @block.scalar
            def _(act):
                with act.Fori(0, B // 2) as i:
                    for s in range(2):
                        act.wait_ge(logits, i * 2 + s + 1)
                        nc.scalar.copy(xs[:, s], XN[:, i * 2 + s, :]).then_inc(staged, 1)
                act.wait_ge(chain, 2)
                nc.scalar.activation(P[:], L[:], ACT.Exp).then_inc(expd, 1)

            @block.tensor
            def _(pe):
                pe.wait_ge(w_loaded, 16)
                with pe.Fori(0, B // 2) as i:
                    for s in range(2):
                        pe.wait_ge(staged, i * 2 + s + 1)
                        pe.wait_ge(copied, i * 2 + s + 1)
                        for t in range(8):
                            mm = nc.tensor.matmul(l_ps[:, s, t * E:(t + 1) * E], xs[:, s, t * C:(t + 1) * C], wr[:],
                                                  start=True, stop=True)
                        mm.then_inc(logits, 1)
                pe.wait_ge(gates, 1)
                for i in range(B):
                    mm = nc.tensor.transpose(g_ps[0:E * 8, i, :], G[:, i * 8:(i + 1) * 8, :].rearrange("p t e -> p (t e)"), identf[:])
                    if i % 4 == 3:
                        mm.then_inc(turned, 1)

            @block.vector
            def _(v):
                count = [0]

                def chained(ins):
                    count[0] += 1
                    ins.then_inc(chain, 1)
                    v.wait_ge(chain, count[0])

                grant(nc, scratch, [(logits, 2), (copied, 2)])
                with v.Fori(0, B // 2) as i:
                    for s in range(2):
                        v.wait_ge(logits, i * 2 + s + 3)
                        nc.vector.tensor_copy(L[:].rearrange("p (i c) e -> p i (c e)", i=B)[:, i * 2 + s, :],
                                              l_ps[:, s, 0:8 * E]).then_inc(copied, 1)
                v.wait_ge(copied, B + 2)
                chained(nc.vector.tensor_reduce(m1[:], L[:], AX.X, ALU.max))
                chained(nc.vector.tensor_tensor(L[:], L[:], wide(m1), ALU.subtract))
                v.wait_ge(expd, 1)
                chained(nc.vector.tensor_reduce(m1[:], P[:], AX.X, ALU.add))
                chained(nc.vector.reciprocal(r[:], m1[:]))
                chained(nc.vector.tensor_tensor(P[:], P[:], wide(r), ALU.mult))
                pref = prefer[:].unsqueeze(1).to_broadcast([C, T, E])
                chained(nc.vector.tensor_reduce(m1[:], P[:], AX.X, ALU.max))
                chained(nc.vector.tensor_tensor(M[:], P[:], wide(m1), ALU.is_equal))
                chained(nc.vector.tensor_tensor(M[:], M[:], pref, ALU.mult))
                chained(nc.vector.tensor_reduce(r[:], M[:], AX.X, ALU.max))
                chained(nc.vector.tensor_tensor(G[:], M[:], wide(r), ALU.is_equal))
                chained(nc.vector.scalar_tensor_tensor(L[:].rearrange("p t e -> p (t e)"), G[:].rearrange("p t e -> p (t e)"),
                                                       -4.0, P[:].rearrange("p t e -> p (t e)"), ALU.mult, ALU.add))
                chained(nc.vector.tensor_reduce(m2[:], L[:], AX.X, ALU.max))
                chained(nc.vector.tensor_tensor(M[:], L[:], wide(m2), ALU.is_equal))
                chained(nc.vector.tensor_tensor(M[:], M[:], pref, ALU.mult))
                chained(nc.vector.tensor_reduce(r[:], M[:], AX.X, ALU.max))
                chained(nc.vector.tensor_tensor(M[:], M[:], wide(r), ALU.is_equal))
                chained(nc.vector.tensor_tensor(G[:], G[:], M[:], ALU.add))
                chained(nc.vector.tensor_tensor(m1[:], m1[:], m2[:], ALU.add))
                if guard == "max":
                    chained(nc.vector.tensor_scalar(m1[:], m1[:], 1e-12, None, ALU.max))
                else:
                    chained(nc.vector.tensor_scalar(m1[:], m1[:], 1e-9, None, ALU.add))
                chained(nc.vector.reciprocal(r[:], m1[:]))
                chained(nc.vector.tensor_tensor(P[:], P[:], wide(r), ALU.mult))
                chained(nc.vector.tensor_tensor(P[:], P[:], G[:], ALU.mult))
                nc.vector.tensor_copy(G[:].rearrange("p (i c) e -> p i (c e)", i=B).rearrange("p i (e t) -> p i e t", e=E),
                                      P[:].rearrange("p (i t) e -> p i e t", i=B)).then_inc(gates, 1)
                for half in range(2):
                    v.wait_ge(turned, half + 1)
                    nc.vector.tensor_copy(gt[:, 4 * half:4 * half + 4], g_ps[0:E * 8, 4 * half:4 * half + 4]).then_inc(gcopied, 1)


def gelu_experts(chip, X, XN, dram, g_scr):
    nc = chip.nc
    GS = 4
    with chip.stage() as ctx:
        w1, w2 = chip.buf(ctx, "w1", [C, E, C]), chip.buf(ctx, "w2", [C, E, C])
        b1, b2 = chip.buf(ctx, "b1", [C, E]), chip.buf(ctx, "b2", [E, C])
        gb = chip.buf(ctx, "gb", [C, GS, N])
        gt = chip.buf(ctx, "gt", [E, 2, N])
        hs, hg = chip.buf(ctx, "hs", [C, 2, N]), chip.buf(ctx, "hg", [C, 2, N])
        scratch = chip.buf(ctx, "scratch", [1, 8])
        h_ps = chip.psum(ctx, "h_ps", [C, 2, N])
        y_ps = chip.psum(ctx, "y_ps", [C, N])
        w_loaded, h_ready, gelu_done, gated, image_done, added, y_steps = (chip.sem(s) for s in (
            "w_loaded", "h_ready", "gelu_done", "gated", "image_done", "added", "y_steps"))
        gb_loaded = [chip.sem("gb_loaded") for _ in range(GS)]
        gt_loaded = [chip.sem("gt_loaded") for _ in range(2)]
        with nc.Block() as block:
            @block.sync
            def _(sp):
                for dst, name in ((w1, "m2_w1"), (w2, "m2_w2"), (b1, "m2_b1"), (b2, "m2_b2")):
                    sp.dma_start(dst[:], dram[name]).then_inc(w_loaded, 16)
                with sp.Fori(0, B // 2) as i:
                    for s in range(2):
                        sp.wait_ge(image_done, i * 2 + s + 1)
                        sp.dma_start(gt[:, s], g_scr[i * 2 + s]).then_inc(gt_loaded[s], 16)
                        for e in range(E):
                            sp.wait_ge(gated, i * 2 * E + (s * E + e) + 1)
                            sp.dma_start(gb[:, e % GS], g_scr[i * 2 + s, e:e + 1].to_broadcast([C, N])).then_inc(gb_loaded[e % GS], 16)

            @block.tensor
            def _(pe):
                pe.wait_ge(w_loaded, 64)
                with pe.Fori(0, B // 2) as i:
                    for s in range(2):
                        base = i * 2 * E
                        for e in range(E + 1):
                            n = s * E + e
                            if e < E:
                                pe.wait_ge(gelu_done, base + n + 1)
                                for c in range(2):
                                    mm = nc.tensor.matmul(h_ps[:, e % 2, c * HALF:(c + 1) * HALF], w1[:, e, :],
                                                          XN[:, i * 2 + s, c * HALF:(c + 1) * HALF], start=True, stop=True)
                                mm.then_inc(h_ready, 1)
                            if e == 0:
                                pe.wait_ge(gt_loaded[s], i * 16 + 16)
                                pe.wait_ge(added, i * 2 + s + 1)
                                for c in range(2):
                                    nc.tensor.matmul(y_ps[:, c * HALF:(c + 1) * HALF], b2[:],
                                                     gt[:, s, c * HALF:(c + 1) * HALF], start=True, stop=False)
                            else:
                                pe.wait_ge(gated, base + (n - 1) + GS + 1)
                                for c in range(2):
                                    mm = nc.tensor.matmul(y_ps[:, c * HALF:(c + 1) * HALF], w2[:, e - 1, :],
                                                          hg[:, (e - 1) % 2, c * HALF:(c + 1) * HALF],
                                                          start=False, stop=(e == E))
                                mm.then_inc(y_steps, 1)

            @block.scalar
            def _(act):
                act.wait_ge(w_loaded, 64)
                with act.Fori(0, B) as i:
                    for e in range(E):
                        act.wait_ge(h_ready, i * E + e + 1)
                        act.wait_ge(gated, i * E + e + GS - 1)
                        nc.scalar.activation(hs[:, e % 2], h_ps[:, e % 2], ACT.Gelu, bias=b1[:, e:e + 1]).then_inc(gelu_done, 1)

            @block.gpsimd
            def _(pool):
                with pool.Fori(0, B) as i:
                    for e in range(E):
                        pool.wait_ge(gelu_done, i * E + e + 3)
                        pool.wait_ge(gb_loaded[e % GS], (i * (E // GS) + e // GS) * 16 + 16)
                        pool.wait_ge(y_steps, i * E + e + 1)
                        nc.gpsimd.tensor_tensor(hg[:, e % 2], hs[:, e % 2], gb[:, e % GS], ALU.mult).then_inc(gated, 1)

            @block.vector
            def _(v):
                grant(nc, scratch, [(gelu_done, 2), (gated, GS), (y_steps, 2), (added, 1), (image_done, 2)])
                with v.Fori(0, B) as i:
                    v.wait_ge(y_steps, i * E + E + 2)
                    nc.vector.tensor_tensor(X[:, i, :], y_ps[:], X[:, i, :], ALU.add).then_inc(added, 1)
                    v.wait_ge(added, i + 2)
                    nc.vector.tensor_tensor(X[:, i, :], X[:, i, :], XN[:, i, :], ALU.add).then_inc(image_done, 1)


CHUNKS = -(-E * HID // C)
LO = 2.0 ** 11


def chunk_experts(c):
    first, last = c * C // HID, min((c + 1) * C, E * HID) - 1
    return first, last // HID, (first + 1) * HID - c * C


def silu_experts(chip, X, XN, dram, g_scr):
    nc = chip.nc
    MIXED = [c for c in range(CHUNKS) if chunk_experts(c)[0] != chunk_experts(c)[1]]
    GB = E + len(MIXED)
    H_SLOTS, HG_SLOTS, LAG = 2, 4, 2
    PER = 2 * CHUNKS
    assert PER % HG_SLOTS == 0
    with chip.stage() as ctx:
        wh, wl = (chip.buf(ctx, n, [C, 2, CHUNKS, C], F16) for n in ("wh", "wl"))
        w2 = chip.buf(ctx, "w2", [C, CHUNKS, C])
        xh, xs, xl = (chip.buf(ctx, n, [C, 2, HALF], F16) for n in ("xh", "xs", "xl"))
        gb = chip.buf(ctx, "gb", [C, 2, GB, HALF])
        s1, u = (chip.buf(ctx, n, [C, H_SLOTS, HALF]) for n in ("s1", "u"))
        hg = chip.buf(ctx, "hg", [C, HG_SLOTS, HALF])
        scratch = chip.buf(ctx, "scratch", [1, 8])
        h_ps = chip.psum(ctx, "h_ps", [C, H_SLOTS, 2, HALF])
        y_ps = chip.psum(ctx, "y_ps", [C, 2, HALF])
        w_loaded, w_hi, w_rest, w_split, x_hi, x_scaled, x_lo = (chip.sem(s) for s in (
            "w_loaded", "w_hi", "w_rest", "w_split", "x_hi", "x_scaled", "x_lo"))
        w2_loaded, h_ready, silu_done, hidden, gated, y_steps, added = (chip.sem(s) for s in (
            "w2_loaded", "h_ready", "silu_done", "hidden", "gated", "y_steps", "added"))
        gb_loaded = [chip.sem("gb_loaded") for _ in range(2)]

        def whole(n):
            return gb[:, n].rearrange("p g t -> p (g t)")[:, 0:CHUNKS * C]

        def flat(part, n):
            return part[:, n].rearrange("p c m -> p (c m)")

        with nc.Block() as block:
            @block.sync
            def _(sp):
                for n, name in enumerate(("m3_w1", "m3_w3")):
                    sp.dma_start(whole(n), dram[name]).then_inc(w_loaded, 16)
                sp.dma_start(w2[:].rearrange("p c m -> p (c m)"), dram["m3_w2"]).then_inc(w2_loaded, 16)
                sp.wait_ge(w_split, 2)
                with sp.Fori(0, B) as i:
                    for s in range(2):
                        gates = g_scr[i, :, s * HALF:(s + 1) * HALF]
                        sp.wait_ge(added, i * 2 + s + 1)
                        sp.dma_start(gb[:, s, 0:E], gates.unsqueeze(0).to_broadcast([C, E, HALF])).then_inc(gb_loaded[s], 16)
                        for n, c in enumerate(MIXED):
                            first, last, row = chunk_experts(c)
                            for e, rows in ((first, slice(0, row)), (last, slice(row, C))):
                                sp.dma_start(gb[rows, s, E + n],
                                             gates[e:e + 1].to_broadcast([rows.stop - rows.start, HALF])
                                             ).then_inc(gb_loaded[s], 16)

            @block.tensor
            def _(pe):
                def image(i):
                    for n in range(PER + LAG):
                        if n < PER:
                            s, c = n // CHUNKS, n % CHUNKS
                            if c == 0:
                                pe.wait_ge(x_scaled, i * 2 + s + 1)
                                pe.wait_ge(x_lo, i * 2 + s + 1)
                            pe.wait_ge(hidden, i * PER + n + 1)
                            for m in range(2):
                                out = h_ps[:, n % H_SLOTS, m]
                                nc.tensor.matmul(out, wh[:, m, c, :], xh[:, s], start=True, stop=False)
                                nc.tensor.matmul(out, wh[:, m, c, :], xl[:, s], start=False, stop=False)
                                mm = nc.tensor.matmul(out, wl[:, m, c, :], xs[:, s], start=False, stop=True)
                            mm.then_inc(h_ready, 1)
                        if n >= LAG:
                            m = n - LAG
                            s, c = m // CHUNKS, m % CHUNKS
                            if c == 0:
                                pe.wait_ge(added, i * 2 + s + 1)
                            pe.wait_ge(gated, i * PER + m + H_SLOTS + 1)
                            nc.tensor.matmul(y_ps[:, s], w2[:, c, :], hg[:, m % HG_SLOTS], start=(c == 0),
                                             stop=(c == CHUNKS - 1)).then_inc(y_steps, 1)

                pe.wait_ge(w_split, 2)
                pe.wait_ge(w2_loaded, 16)
                with pe.Fori(0, B) as i:
                    image(i)

            @block.scalar
            def _(act):
                def high(i, s):
                    x = XN[:, i, s * HALF:(s + 1) * HALF]
                    nc.scalar.copy(xh[:, s], x).then_inc(x_hi, 1)
                    nc.scalar.activation(xs[:, s], x, ACT.Copy, scale=1 / LO).then_inc(x_scaled, 1)

                def image(i, last):
                    for n in range(PER):
                        act.wait_ge(h_ready, i * PER + n + 1)
                        nc.scalar.activation(s1[:, n % H_SLOTS], h_ps[:, n % H_SLOTS, 0], ACT.Silu).then_inc(silu_done, 1)
                        if n == CHUNKS // 2:
                            high(i, 1)
                        if n == CHUNKS // 2 + CHUNKS and not last:
                            high(i + 1, 0)

                act.wait_ge(w_loaded, 32)
                for n in range(2):
                    nc.scalar.copy(flat(wh, n), whole(n)).then_inc(w_hi, 1)
                high(0, 0)
                with act.Fori(0, B - 1) as i:
                    image(i, False)
                image(B - 1, True)

            @block.vector
            def _(v):
                def low(i, s):
                    v.wait_ge(x_hi, i * 2 + s + 1)
                    nc.vector.tensor_tensor(xl[:, s], XN[:, i, s * HALF:(s + 1) * HALF], xh[:, s],
                                            ALU.subtract).then_inc(x_lo, 1)

                def image(i, last):
                    for n in range(PER):
                        v.wait_ge(silu_done, i * PER + n + 1)
                        v.wait_ge(gated, i * PER + n + 1)
                        nc.vector.tensor_tensor(u[:, n % H_SLOTS], h_ps[:, n % H_SLOTS, 1], s1[:, n % H_SLOTS],
                                                ALU.mult).then_inc(hidden, 1)
                        if n == CHUNKS // 2:
                            low(i, 1)
                        if n == CHUNKS // 2 + CHUNKS and not last:
                            low(i + 1, 0)
                        if n == CHUNKS + LAG + 1:
                            v.wait_ge(y_steps, i * PER + (CHUNKS + HG_SLOTS))
                            at = X[:, i, 0:HALF]
                            nc.vector.tensor_tensor(at, y_ps[:, 0], at, ALU.add).then_inc(added, 1)
                    v.wait_ge(y_steps, i * PER + (PER + HG_SLOTS))
                    at = X[:, i, HALF:N]
                    nc.vector.tensor_tensor(at, y_ps[:, 1], at, ALU.add).then_inc(added, 1)

                grant(nc, scratch, [(hidden, H_SLOTS), (gated, H_SLOTS), (y_steps, HG_SLOTS), (added, 2)])
                for n in range(2):
                    v.wait_ge(w_hi, n + 1)
                    nc.vector.tensor_tensor(whole(n), whole(n), flat(wh, n), ALU.subtract).then_inc(w_rest, 1)
                for n in range(2):
                    v.wait_ge(w_rest, n + 1)
                    nc.vector.tensor_scalar(flat(wl, n), whole(n), LO, None, ALU.mult).then_inc(w_split, 1)
                low(0, 0)
                with v.Fori(0, B - 1) as i:
                    image(i, False)
                image(B - 1, True)

            @block.gpsimd
            def _(pool):
                with pool.Fori(0, B) as i:
                    for n in range(PER):
                        s, c = n // CHUNKS, n % CHUNKS
                        if c == 0:
                            pool.wait_ge(gb_loaded[s], (i + 1) * (16 * (1 + 2 * len(MIXED))))
                        tile = E + MIXED.index(c) if c in MIXED else chunk_experts(c)[0]
                        pool.wait_ge(hidden, i * PER + n + H_SLOTS + 1)
                        pool.wait_ge(y_steps, i * PER + n + 1)
                        nc.gpsimd.tensor_tensor(hg[:, n % HG_SLOTS], u[:, n % H_SLOTS], gb[:, s, tile],
                                                ALU.mult).then_inc(gated, 1)


def local_attention(chip, XN, dram, identf, out):
    nc = chip.nc
    TILES = -(-N // QT)
    GROUPS = [(0, 3), (3, 3), (6, 3), (9, 2)]
    assert GROUPS[-1][0] + GROUPS[-1][1] == TILES
    WIDE = 3 * QT
    with chip.stage() as ctx:
        band = chip.buf(ctx, "band", [C, QT])
        ones = chip.buf(ctx, "ones", [C, C])
        xs = chip.buf(ctx, "xs", [C, 2, N + 64])
        tk = chip.buf(ctx, "tk", [C, 2, 3, C])
        ex, em, rd = (chip.buf(ctx, n, [C, 2, WIDE]) for n in ("ex", "em", "rd"))
        scratch = chip.buf(ctx, "scratch", [1, 8])
        t_ps = chip.psum(ctx, "t_ps", [C, 2, HALF])
        s_ps = chip.psum(ctx, "s_ps", [C, 2, HALF])
        n_ps = chip.psum(ctx, "n_ps", [C, 2, HALF])
        d_ps = chip.psum(ctx, "d_ps", [C, 2, HALF])
        w_loaded, filled, staged, turned, scored, copied, expd, masked, summed, inverted, stored = (chip.sem(s) for s in (
            "w_loaded", "filled", "staged", "turned", "scored", "copied", "expd", "masked", "summed", "inverted", "stored"))

        def queries(t):
            return min(QT, N - t * QT)

        with nc.Block() as block:
            @block.sync
            def _(sp):
                sp.dma_start(band[:], dram["band"]).then_inc(w_loaded, 16)
                sp.wait_ge(w_loaded, 16)

            @block.tensor
            def _(pe):
                def front(i, s, g):
                    n = s * 4 + g
                    t0, cnt = GROUPS[g]
                    if g == 0:
                        pe.wait_ge(staged, i * 2 + s + 1)
                    pe.wait_ge(copied, i * 8 + n + 1)
                    for t in range(cnt):
                        mm = nc.tensor.transpose(t_ps[:, n % 2, t * C:(t + 1) * C],
                                                 xs[:, s, (t0 + t) * QT:(t0 + t) * QT + C], identf[:])
                    mm.then_inc(turned, 1)
                    pe.wait_ge(expd, i * 8 + n + 1)
                    for t in range(cnt):
                        q = queries(t0 + t)
                        at = (t0 + t) * QT
                        mm = nc.tensor.matmul(s_ps[:, n % 2, t * QT:t * QT + q], xs[:, s, at:at + C],
                                              xs[:, s, BAND + at:BAND + at + q], start=True, stop=True)
                    mm.then_inc(scored, 1)

                def back(i, s, g):
                    n = s * 4 + g
                    t0, cnt = GROUPS[g]
                    pe.wait_ge(masked, i * 8 + n + 3)
                    pe.wait_ge(copied, i * 8 + n + 3)
                    pe.wait_ge(stored, i * 8 + n + 1)
                    for t in range(cnt):
                        q = queries(t0 + t)
                        nc.tensor.matmul(n_ps[:, n % 2, t * QT:t * QT + q], tk[:, n % 2, t], em[:, n % 2, t * QT:t * QT + q],
                                         start=True, stop=True)
                    width = (cnt - 1) * QT + queries(t0 + cnt - 1)
                    nc.tensor.matmul(d_ps[:, n % 2, 0:width], ones[:], em[:, n % 2, 0:width],
                                     start=True, stop=True).then_inc(summed, 1)

                pe.wait_ge(filled, 3)
                with pe.Fori(0, B // 2) as i:
                    for n in range(9):
                        if n < 8:
                            front(i, n // 4, n % 4)
                        if n:
                            back(i, (n - 1) // 4, (n - 1) % 4)

            @block.scalar
            def _(act):
                act.wait_ge(filled, 3)
                with act.Fori(0, B // 2) as i:
                    for n in range(8):
                        s, g = n // 4, n % 4
                        t0, cnt = GROUPS[g]
                        if g == 0:
                            act.wait_ge(summed, i * 8 + 4 * s + 1)
                            nc.scalar.copy(xs[:, s, BAND:BAND + N], XN[:, i * 2 + s, :]).then_inc(staged, 1)
                        width = (cnt - 1) * QT + queries(t0 + cnt - 1)
                        act.wait_ge(scored, i * 8 + n + 1)
                        act.wait_ge(masked, i * 8 + n + 1)
                        nc.scalar.activation(ex[:, n % 2, 0:width], s_ps[:, n % 2, 0:width], ACT.Exp,
                                             scale=float(C) ** -0.5).then_inc(expd, 1)

            @block.vector
            def _(v):
                nc.vector.memset(xs[:], 0.0).then_inc(filled, 1)
                nc.vector.memset(ones[:], 1.0).then_inc(filled, 1)
                grant(nc, scratch, [(copied, 2), (expd, 2), (masked, 2), (stored, 2), (summed, 4), (filled, 1)])
                v.wait_ge(w_loaded, 16)

                def finish(i, n):
                    s, g = n // 4, n % 4
                    t0, cnt = GROUPS[g]
                    width = (cnt - 1) * QT + queries(t0 + cnt - 1)
                    v.wait_ge(summed, i * 8 + n + 5)
                    nc.vector.reciprocal(rd[:, n % 2, 0:width], d_ps[:, n % 2, 0:width]).then_inc(inverted, 1)
                    v.wait_ge(inverted, i * 8 + n + 1)
                    nc.vector.tensor_tensor(out[:, i * 2 + s, t0 * QT:t0 * QT + width], n_ps[:, n % 2, 0:width],
                                            rd[:, n % 2, 0:width], ALU.mult).then_inc(stored, 1)

                with v.Fori(0, B // 2) as i:
                    for n in range(9):
                        if n < 8:
                            cnt = GROUPS[n % 4][1]
                            t0 = GROUPS[n % 4][0]
                            v.wait_ge(turned, i * 8 + n + 1)
                            v.wait_ge(summed, i * 8 + n + 3)
                            nc.vector.tensor_copy(tk[:, n % 2, 0:cnt].rearrange("p t c -> p (t c)"),
                                                  t_ps[:, n % 2, 0:cnt * C]).then_inc(copied, 1)
                            v.wait_ge(expd, i * 8 + n + 3)
                            full = cnt if queries(t0 + cnt - 1) == QT else cnt - 1
                            ins = nc.vector.tensor_tensor(
                                em[:, n % 2, 0:full * QT].rearrange("p (t q) -> p t q", q=QT),
                                ex[:, n % 2, 0:full * QT].rearrange("p (t q) -> p t q", q=QT),
                                band[:].unsqueeze(1).to_broadcast([C, full, QT]), ALU.mult)
                            if full < cnt:
                                q = queries(t0 + full)
                                ins = nc.vector.tensor_tensor(em[:, n % 2, full * QT:full * QT + q],
                                                              ex[:, n % 2, full * QT:full * QT + q], band[:, 0:q], ALU.mult)
                            ins.then_inc(masked, 1)
                        if n:
                            finish(i, n - 1)


def store(chip, X, out):
    nc = chip.nc
    stored = chip.sem("stored")
    with nc.Block() as block:
        @block.sync
        def _(sp):
            with sp.Fori(0, B) as i:
                sp.dma_start(out[i].rearrange("c h w -> c (h w)"), X[:, i, :]).then_inc(stored, 16)
            sp.wait_ge(stored, 16 * B)


def network(nc, x, dram, out):
    def scratch(name, shape, dt=F32):
        return nc.dram_tensor(name, shape, dt, kind="Internal").ap()

    qk0 = scratch("qk0", [B, 4, PARTS, C, N], BF16)
    v0 = scratch("v0", [B, 4, C, 8 * 64])
    qk2 = scratch("qk2", [B, 2, PARTS, C, N], BF16)
    v2 = scratch("v2", [B, 4, C, 8 * 32])
    m0 = scratch("m0", [2, 2, PARTS, 4, 8, C], BF16)
    m2 = scratch("m2", [2, 1, PARTS, 4, 8, C], BF16)
    g2 = scratch("g2", [B, E, N])
    g3 = scratch("g3", [B, E, N])

    with ExitStack() as ctx:
        chip = Chip(nc)
        X = chip.buf(ctx, "X", [C, B, N])
        identf = chip.buf(ctx, "identf", [C, C])
        ident = chip.buf(ctx, "ident", [C, C], BF16)
        gn_avg = chip.buf(ctx, "gn_avg", [C, C])
        mean_w = chip.buf(ctx, "mean_w", [C, C])
        prefer = chip.buf(ctx, "prefer", [C, E])
        bproj = chip.buf(ctx, "bproj", [C, 1])
        gamma, beta = chip.buf(ctx, "gamma", [C, 1]), chip.buf(ctx, "beta", [C, 1])
        eps5 = chip.buf(ctx, "eps5", [C, 1])
        mean_g, rstd_g = chip.buf(ctx, "mean_g", [C, B, 1]), chip.buf(ctx, "rstd_g", [C, B, 1])
        pooled = chip.buf(ctx, "pooled", [C, B])
        load_inputs(chip, x, X, [(identf, dram["ident"]), (gn_avg, dram["gn_avg"]),
                                 (mean_w, dram["mean_w"]), (prefer, dram["prefer"]), (bproj, dram["b_proj"]),
                                 (gamma, dram["gamma"]), (beta, dram["beta"])])
        prepared = chip.sem("prepared")
        with nc.Block() as block:
            @block.vector
            def _(v):
                nc.vector.memset(eps5[:], 1e-5).then_inc(prepared, 1)
                nc.vector.tensor_copy(ident[:], identf[:]).then_inc(prepared, 1)

        def flat(a):
            return a[:].rearrange("p b o -> p (b o)")

        group_norm_stats(chip, X, gn_avg, eps5, flat(mean_g), flat(rstd_g), pooled)
        window_projections(chip, X, mean_g, rstd_g, dram, qk0, v0)

        attention(chip, X, dram, lambda i, k, o: qk0[i, k, :, 64 * o:64 * o + 64, :], v0, m0, ident, identf,
                  None, None, 2, 1, float(D) ** -0.5)

        group_norm_stats(chip, X, gn_avg, eps5, flat(mean_g), flat(rstd_g), pooled)
        conv_stage(chip, X, dram, mean_g, rstd_g, pooled, eps5, identf)

        with ExitStack() as c2:
            XN = chip.buf(c2, "XN", [C, B, N])
            layer_norm(chip, X, mean_w, eps5, identf, dst=XN)
            token_projections(chip, XN, dram, qk2, v2)
        attention(chip, X, dram, lambda i, k, o: qk2[i, o, :, 32 * k:32 * k + 32, :], v2, m2, ident, identf,
                  "w_proj", bproj, 1, 8, 1.0)

        with ExitStack() as c2:
            XN = chip.buf(c2, "XN", [C, B, N])
            layer_norm(chip, X, mean_w, eps5, identf, dst=XN)
            route(chip, XN, dram, "m2_router", identf, prefer, "max", g2)
            gelu_experts(chip, X, XN, dram, g2)
            layer_norm(chip, X, mean_w, eps5, identf, dst=XN)
            with ExitStack() as c3:
                O = chip.buf(c3, "O", [C, B, N])
                local_attention(chip, XN, dram, identf, O)
                layer_norm(chip, O, mean_w, eps5, identf, X=X, gamma=gamma, beta=beta)
            layer_norm(chip, X, mean_w, eps5, identf, dst=XN)
            route(chip, XN, dram, "m3_router", identf, prefer, "add", g3)
            silu_experts(chip, X, XN, dram, g3)
        store(chip, X, out)


def constants():
    import numpy as np

    c = np.arange(C)
    one = np.float32(1)
    key, query = np.arange(C)[:, None], np.arange(QT)[None, :]
    band = np.where((key >= query) & (key <= query + 2 * BAND), one, 0 * one)
    return {
        "ident": np.eye(C, dtype=np.float32),
        "gn_avg": np.where(c[:, None] // 4 == c[None, :] // 4, one / 4, 0 * one).astype(np.float32),
        "mean_w": np.full((C, C), 1 / C, np.float32),
        "prefer": np.tile(np.arange(E, 0, -1, dtype=np.float32), (C, 1)),
        "band": band.astype(np.float32),
    }


def laid_out(a):
    import numpy as np

    out = {}
    wq = a["L0_conv_w_qkv"][:, :, 0, 0]
    head_major = np.array([d * 8 + h for h in range(8) for d in range(D)])
    qk, vv = np.zeros((C, 4, C), np.float32), np.zeros((C, 4, 64), np.float32)
    lepe, taps, bl = np.zeros((C, 2, C), np.float32), np.zeros((2, 9, C), np.float32), np.zeros((C, 2), np.float32)
    for u in range(4):
        s, part = u // 2 * 2, u % 2
        rows = (part * 64 + np.arange(64) + s) % C
        qk[rows, u, 0:64] = wq[head_major].T
        qk[rows, u, 64:128] = wq[64 + head_major].T
        vv[rows, u] = wq[128 + head_major].T
        conv = (np.arange(64) - s) % 64
        at = slice(part * 64, part * 64 + 64)
        lepe[rows, s // 2, at] = wq[128 + conv].T
        taps[s // 2, :, at] = a["L0_conv_w_lepe"][conv, 0].reshape(64, 9).T
        bl[at, s // 2] = a["L0_conv_b_lepe"][conv]
    out["w0_qk"], out["w0_v"], out["w0_lepe"] = qk, vv, lepe
    out["lepe_taps"], out["b_lepe"] = taps.reshape(1, -1), bl
    out["se_w1"], out["se_w2"] = a["L1_conv_attn_w1"].T, a["L1_conv_attn_w2"].T
    out["refine_w"], out["refine_b"] = a["L1_conv_refine_w"].reshape(C, 9), a["L1_conv_refine_b"].reshape(C, 1)
    w = a["L2_attn_w_qkv"]
    out["w2_qk"], out["w2_v"] = w[:, :2 * C].reshape(C, 2, C), w[:, 2 * C:]
    b = a["L2_attn_b_qkv"]
    out["b2_qk"], out["b2_v"] = b[:2 * C].reshape(2, C).T, b[2 * C:].reshape(1, C)
    out["w_proj"], out["b_proj"] = a["L2_attn_w_proj"], a["L2_attn_b_proj"].reshape(C, 1)
    out["m2_router"], out["m3_router"] = a["L2_ffn_router_w"].T, a["L3_ffn_router_w"].T
    out["m2_w1"], out["m2_w2"] = a["L2_ffn_w1"].transpose(1, 0, 2), a["L2_ffn_w2"].transpose(1, 0, 2)
    out["m2_b1"], out["m2_b2"] = a["L2_ffn_b1"].T, a["L2_ffn_b2"]
    out["gamma"], out["beta"] = a["L3_attn_gamma"].reshape(C, 1), a["L3_attn_beta"].reshape(C, 1)
    for name in ("w1", "w3"):
        padded = np.zeros((C, CHUNKS * C), np.float32)
        padded[:, :E * HID] = a[f"L3_ffn_{name}"].reshape(E * HID, C).T
        out["m3_" + name] = padded
    w2 = np.zeros((CHUNKS * C, C), np.float32)
    w2[:E * HID] = a["L3_ffn_w2"].transpose(0, 2, 1).reshape(E * HID, C)
    out["m3_w2"] = w2.reshape(CHUNKS, C, C).transpose(1, 0, 2).reshape(C, -1)
    return out


def kernel(**inputs):
    import numpy as np
    import concourse.bacc as bacc
    from concourse.bass_utils import run_bass_kernel_spmd as run

    inputs = {name: np.asarray(value) for name, value in inputs.items()}
    nc = bacc.Bacc("TRN2", target_bir_lowering=False, num_devices=1)
    arrays, dram = {}, {}
    for name, value in {"x": inputs["x"], **constants(), **laid_out(inputs)}.items():
        value = np.ascontiguousarray(value)
        arrays[f"in_{name}"] = value
        dram[name] = nc.dram_tensor(f"in_{name}", value.shape, mybir.dt.from_np(value.dtype), kind="ExternalInput").ap()
    out = nc.dram_tensor("out", inputs["x"].shape, F32, kind="ExternalOutput").ap()
    network(nc, dram["x"], dram, out)
    return run(nc, [arrays], core_ids=[0]).results[0]["out"]
```

```python
from contextlib import ExitStack, contextmanager

import concourse.bass as bass
from concourse import mybir

F32 = mybir.dt.float32
BF16 = mybir.dt.bfloat16
F16 = mybir.dt.float16
ALU = mybir.AluOpType
ACT = mybir.ActivationFunctionType
AX = mybir.AxisListType

B, C, H, W = 8, 128, 32, 32
N = H * W
HALF = N // 2
D = 8
PARTS = 3
COMBOS = [(0, 0), (0, 1), (0, 2), (1, 0), (1, 1), (2, 0)]
RUNS = ([(0, 3, 0, True), (3, 2, 1, True), (5, 1, 2, False)], [(0, 3, 0, False), (3, 2, 0, False), (5, 1, 0, False)])
STACK = len(COMBOS) * D
ROWS = STACK + PARTS
E = 8
HID = 341
CHUNKS = -(-E * HID // C)
LO = 2.0 ** 11
BAND = 16
QT = C - 2 * BAND
WARM_UP = 5


def grant(nc, scratch, credits):
    for n, (sem, slots) in enumerate(credits):
        nc.vector.memset(scratch[0:1, n:n + 1], 0.0).then_inc(sem, slots)


class Chip:

    def __init__(self, nc):
        self.nc, self.n, self.sems = nc, 0, []

    @contextmanager
    def stage(self):
        outer, self.sems = self.sems, []
        with ExitStack() as ctx:
            yield ctx
        self.nc.clear_and_free_semaphores(self.sems)
        self.nc.all_engine_barrier()
        self.sems = outer

    def sem(self, name):
        self.n += 1
        self.sems.append(self.nc.alloc_semaphore(name=f"{name}_{self.n}"))
        return self.sems[-1]

    def buf(self, ctx, name, shape, dt=F32):
        self.n += 1
        return ctx.enter_context(self.nc.sbuf_tensor(f"{name}_{self.n}", shape, dt))

    def psum(self, ctx, name, shape, dt=F32):
        self.n += 1
        return ctx.enter_context(self.nc.psum_tensor(f"{name}_{self.n}", shape, dt))


def group_norm_stats(chip, X, gn_avg, eps5, mean_g, rstd_g, pooled, x=None, consts=(), ident=None, identf=None):
    nc = chip.nc
    with chip.stage() as ctx:
        st = chip.buf(ctx, "gn_st", [C, B, 12])
        mv = chip.buf(ctx, "gn_mv", [C, B, 2])
        dev = chip.buf(ctx, "gn_dev", [C, B])
        sq = chip.buf(ctx, "gn_sq", [C, B])
        sd = chip.buf(ctx, "gn_sd", [C, B])
        ps = chip.psum(ctx, "gn_ps", [C, 2, HALF])
        stats, aggr, avg, step, rooted, prepared, consts_loaded = (chip.sem(s) for s in (
            "stats", "aggr", "avg", "dvestep", "rooted", "prepared", "consts_loaded"))
        x_loaded = [chip.sem("x_loaded") for _ in range(B)]
        with nc.Block() as block:
            if x is not None:
                @block.sync
                def _(sp):
                    for i in range(B):
                        sp.dma_start(X[:, i, :], x[i].rearrange("c h w -> c (h w)")).then_inc(x_loaded[i], 16)
                    for dst, src in consts:
                        sp.dma_start(dst[:], src).then_inc(consts_loaded, 16)
                    sp.wait_ge(consts_loaded, 16 * len(consts))

            @block.vector
            def _(v):
                if x is not None:
                    nc.vector.memset(eps5[:], 1e-5).then_inc(prepared, 1)
                for i in range(B):
                    if x is not None:
                        v.wait_ge(x_loaded[i], 16)
                    for c in range(2):
                        last = nc.vector.bn_stats(st[:, i, 6 * c:6 * c + 6], X[:, i, c * HALF:(c + 1) * HALF])
                    last.then_inc(stats, 1)
                for i in range(B):
                    v.wait_ge(stats, i + 1)
                    nc.vector.bn_aggr(mv[:, i, :], st[:, i, :]).then_inc(aggr, 1)
                v.wait_ge(aggr, B)
                v.wait_ge(avg, 1)
                if x is not None:
                    v.wait_ge(consts_loaded, 16 * len(consts))
                    nc.vector.tensor_copy(ident[:], identf[:]).then_inc(prepared, 1)
                nc.vector.tensor_copy(mean_g[:], ps[:, 0, 0:B]).then_inc(step, 1)
                nc.vector.tensor_tensor(dev[:], mv[:, :, 0], ps[:, 0, 0:B], ALU.subtract).then_inc(step, 1)
                v.wait_ge(step, 2)
                nc.vector.tensor_tensor(sq[:], dev[:], dev[:], ALU.mult).then_inc(step, 1)
                v.wait_ge(step, 3)
                nc.vector.tensor_tensor(sq[:], sq[:], mv[:, :, 1], ALU.add).then_inc(step, 1)
                v.wait_ge(rooted, 1)
                nc.vector.reciprocal(rstd_g[:], sd[:]).then_inc(step, 1)
                v.wait_ge(step, 5)
                nc.vector.tensor_tensor(pooled[:], dev[:], rstd_g[:], ALU.mult).then_inc(step, 1)

            @block.tensor
            def _(pe):
                if x is not None:
                    pe.wait_ge(consts_loaded, 16 * len(consts))
                pe.wait_ge(aggr, B)
                nc.tensor.matmul(ps[:, 0, 0:B], gn_avg[:], mv[:, :, 0], start=True, stop=True).then_inc(avg, 1)
                pe.wait_ge(step, 4)
                nc.tensor.matmul(ps[:, 1, 0:B], gn_avg[:], sq[:], start=True, stop=True).then_inc(avg, 1)

            @block.scalar
            def _(act):
                act.wait_ge(avg, 2)
                if x is not None:
                    act.wait_ge(prepared, 1)
                nc.scalar.activation(sd[:], ps[:, 1, 0:B], ACT.Sqrt, bias=eps5[:]).then_inc(rooted, 1)


def lepe_pieces(half):
    lo, hi = 16 * half, 16 * half + 16
    out = [(4, 2, lo, 16, lo)]
    for dh in (0, -1, 1):
        for dw in (-1, 0, 1):
            tap = (dh + 1) * 3 + dw + 1
            if tap == 4:
                continue
            if dh == 0:
                out.append((tap, 2, lo, 16, lo))
                continue
            r = lo
            while r < hi:
                src = r + dh
                if r == (31 if dh == 1 else 0):
                    kind = 1
                elif r == (1 if dh == 1 else 2):
                    kind = 0
                else:
                    kind = 2
                n = 1
                while kind == 2 and r + n < hi and r + n != (31 if dh == 1 else 0) and r + n != (1 if dh == 1 else 2):
                    n += 1
                out.append((tap, kind, r, n, src % H))
                r += n
    return out


def window_projections(chip, X, mean_g, rstd_g, dram, qk_scr, v_scr):
    nc = chip.nc
    U = 4
    with chip.stage() as ctx:
        wqk = chip.buf(ctx, "wqk", [C, 4, C])
        wv = chip.buf(ctx, "wv", [C, 4, 64])
        wl = chip.buf(ctx, "wl", [C, 2, C])
        taps = chip.buf(ctx, "taps", [C, 2, 9, C])
        wt = chip.buf(ctx, "wt", [C, 3, 9, C])
        bl = chip.buf(ctx, "bl", [C, 2])
        bsum = chip.buf(ctx, "bsum", [C, 1])
        scratch = chip.buf(ctx, "scratch", [1, 16])
        xn = chip.buf(ctx, "xn", [C, 2, N + 64])
        xw = chip.buf(ctx, "xw", [C, 2, N])
        xp = chip.buf(ctx, "xp", [C, 2, H, W + 2])
        parts = chip.buf(ctx, "parts", [C, 2, PARTS, N], BF16)
        rest = chip.buf(ctx, "rest", [C, 2, N])
        vs = chip.buf(ctx, "vs", [C, 2, HALF])
        qk_ps = chip.psum(ctx, "qk_ps", [C, 2, N])
        v_ps = chip.psum(ctx, "v_ps", [C, 2, HALF])
        l_ps = chip.psum(ctx, "l_ps", [C, N])
        w_loaded, weights, normed, padded, edge, strips = (chip.sem(s) for s in (
            "w_loaded", "weights", "normed", "padded", "edge", "strips"))
        qk_ready, hi_done, rest_done, mid_done, lo_done = (chip.sem(s) for s in (
            "qk_ready", "hi_done", "rest_done", "mid_done", "lo_done"))
        v_ready, v_copied, l_ready, l_added = (chip.sem(s) for s in ("v_ready", "v_copied", "l_ready", "l_added"))
        parts_out = [chip.sem("parts_out") for _ in range(2)]
        v_out = [chip.sem("v_out") for _ in range(2)]

        def images(engine, image):
            with engine.Fori(0, B // 2 - 1) as i:
                image(i * 2, 0, False)
                image(i * 2 + 1, 1, False)
            image(B - 2, 0, False)
            image(B - 1, 1, True)

        with nc.Block() as block:
            @block.sync
            def _(sp):
                for dst, name in ((wqk, "w0_qk"), (wv, "w0_v"), (wl, "w0_lepe"), (bl, "b_lepe")):
                    sp.dma_start(dst[:], dram[name]).then_inc(w_loaded, 16)
                sp.dma_start(taps[:].rearrange("p s t c -> p (s t c)"),
                             dram["lepe_taps"].to_broadcast([C, 2 * 9 * C])).then_inc(w_loaded, 16)
                with sp.Fori(0, B) as i:
                    for u in range(U):
                        sp.wait_ge(lo_done, i * U + u + 3)
                        sp.dma_start(qk_scr[i, u].rearrange("a r t -> r a t"),
                                     parts[:, u % 2]).then_inc(parts_out[u % 2], 16)
                        sp.wait_ge(v_copied, i * U + u + 3)
                        sp.dma_start(v_scr[i, u], vs[:, u % 2]).then_inc(v_out[u % 2], 16)
                for s in (*parts_out, *v_out):
                    sp.wait_ge(s, 16 * (B * U // 2 + 1))

            @block.vector
            def _(v):
                grant(nc, scratch, [(rest_done, 2), (lo_done, 2), (v_copied, 2), (l_added, 1),
                                    (parts_out[0], 16), (parts_out[1], 16), (v_out[0], 16), (v_out[1], 16)])
                nc.vector.memset(xp[:], 0.0).then_inc(weights, 1)
                v.wait_ge(w_loaded, 16 * 5)
                for s in range(2):
                    nc.vector.tensor_tensor(wt[:, s], taps[:, s],
                                            wl[:, s].unsqueeze(1).to_broadcast([C, 9, C]), ALU.mult).then_inc(weights, 1)
                nc.vector.tensor_tensor(bsum[:], bl[:, 0:1], bl[:, 1:2], ALU.add).then_inc(weights, 1)
                v.wait_ge(weights, 4)
                nc.vector.tensor_tensor(wt[:, 2], wt[:, 0], wt[:, 1], ALU.add).then_inc(weights, 1)

                def prepare(i, slot):
                    nc.vector.tensor_scalar(xn[:, slot, 0:N], X[:, i, :], mean_g[:, i, :], rstd_g[:, i, :],
                                            ALU.subtract, ALU.mult).then_inc(normed, 1)
                    v.wait_ge(normed, i + 1)
                    nc.vector.tensor_copy(xn[:, slot, N:N + 64], xn[:, slot, 0:64]).then_inc(edge, 1)
                    nc.vector.tensor_copy(xw[:, slot].rearrange("p (n h w) -> p n h w", n=8, w=4),
                                          xn[:, slot, 0:N].rearrange("p (h n w) -> p n h w", n=8, w=4)).then_inc(strips, 1)

                def image(i, slot, last):
                    for u in range(U):
                        v.wait_ge(hi_done, i * U + u + 1)
                        v.wait_ge(lo_done, i * U + u + 1)
                        nc.vector.tensor_tensor(rest[:, u % 2], qk_ps[:, u % 2], parts[:, u % 2, 0],
                                                ALU.subtract).then_inc(rest_done, 1)
                        if u == 0 and not last:
                            prepare(i + 1, 1 - slot)
                    v.wait_ge(l_ready, i + 1)
                    nc.vector.scalar_tensor_tensor(X[:, i, :], l_ps[:], bsum[:], X[:, i, :],
                                                   ALU.add, ALU.add).then_inc(l_added, 1)

                prepare(0, 0)
                images(v, image)

            @block.gpsimd
            def _(pool):
                with pool.Fori(0, B) as i:
                    for u in range(U):
                        pool.wait_ge(mid_done, i * U + u + 1)
                        nc.gpsimd.tensor_tensor(parts[:, u % 2, 2], rest[:, u % 2], parts[:, u % 2, 1],
                                                ALU.subtract).then_inc(lo_done, 1)

            @block.scalar
            def _(act):
                act.wait_ge(weights, 1)

                def pad(i, slot):
                    act.wait_ge(normed, i + 1)
                    nc.scalar.copy(xp[:, slot, :, 1:W + 1],
                                   xn[:, slot, 0:N].rearrange("p (h w) -> p h w", h=H)).then_inc(padded, 1)

                def image(i, slot, last):
                    for u in range(U):
                        act.wait_ge(qk_ready, i * U + u + 1)
                        act.wait_ge(parts_out[u % 2], i * 32 + (u // 2 * 16 + 16))
                        nc.scalar.copy(parts[:, u % 2, 0], qk_ps[:, u % 2]).then_inc(hi_done, 1)
                        act.wait_ge(v_ready, i * U + u + 1)
                        act.wait_ge(v_out[u % 2], i * 32 + (u // 2 * 16 + 16))
                        nc.scalar.copy(vs[:, u % 2], v_ps[:, u % 2]).then_inc(v_copied, 1)
                        act.wait_ge(rest_done, i * U + u + 3)
                        nc.scalar.copy(parts[:, u % 2, 1], rest[:, u % 2]).then_inc(mid_done, 1)
                    if not last:
                        pad(i + 1, 1 - slot)

                pad(0, 0)
                images(act, image)

            @block.tensor
            def _(pe):
                pe.wait_ge(weights, 5)
                def image(i, slot, last):
                    pe.wait_ge(strips, i + 1)
                    for u in range(U):
                        src = (xw if u % 2 == 0 else xn)[:, slot]
                        at = 64 if u == 3 else 0
                        if u == 1:
                            pe.wait_ge(edge, i + 1)
                        pe.wait_ge(rest_done, i * U + u + 1)
                        for c in range(2):
                            last = nc.tensor.matmul(qk_ps[:, u % 2, c * HALF:(c + 1) * HALF], wqk[:, u, :],
                                                    src[:, at + c * HALF:at + (c + 1) * HALF], start=True, stop=True)
                        last.then_inc(qk_ready, 1)
                        pe.wait_ge(v_copied, i * U + u + 1)
                        for w in range(8):
                            last = nc.tensor.matmul(v_ps[:, u % 2, w * 64:(w + 1) * 64],
                                                    src[:, at + w * C:at + (w + 1) * C], wv[:, u, :],
                                                    start=True, stop=True)
                        last.then_inc(v_ready, 1)
                    pe.wait_ge(padded, i + 1)
                    pe.wait_ge(l_added, i + 1)
                    for half in range(2):
                        pieces = lepe_pieces(half)
                        for n, (tap, kind, r, rows, r_in) in enumerate(pieces):
                            last = nc.tensor.matmul(
                                l_ps[:, r * W:(r + rows) * W], wt[:, kind, tap, :],
                                xp[:, slot, r_in:r_in + rows, tap % 3:tap % 3 + W],
                                start=(n == 0), stop=(n == len(pieces) - 1))
                    last.then_inc(l_ready, 1)

                images(pe, image)


def attention(chip, X, dram, qk_rows, v_scr, m_scr, ident, identf, proj_name, bias, subs, kt_quads, scale):
    nc = chip.nc
    windowed = kt_quads == 1
    QB = subs * kt_quads
    NQ = 4 * QB
    NG = 4 * subs
    HB = 4 * subs
    HP = 2 * subs
    LAST = B - 1

    def ends_output(q):
        return 0 <= q < NQ and q % kt_quads == kt_quads - 1

    def norm_at(q):
        return (q - 2) // kt_quads if ends_output(q - 2) else None

    def final_at(q):
        g = (q - 3) // kt_quads
        return g // 4 if ends_output(q - 3) and g % 4 == 3 else None

    def turn_at(q, blocks=4):
        return q // QB - 1 if q and q % QB == 0 and q // QB - 1 < blocks else None

    def order(i, kind):
        for q in range(4 if kind == "drain" else NQ):
            for j in range(4):
                if kind != "drain":
                    yield i, q, j, kind == "last"
                if kind != "first" and q < 4:
                    yield i - 1, q + NQ, j, kind == "drain"

    def numbers(kind):
        st, mx = [], []
        for i, q, j, last in order(1, kind):
            blocks = 2 if last else 4
            if q < NQ:
                st.append((i, "exp", q, j))
                if q // QB < blocks:
                    mx += [(i, "max", q, 2 * j), (i, "max", q, 2 * j + 1)]
            if j == 1:
                if turn_at(q, blocks) is not None:
                    mx += [(i, "turn", turn_at(q, blocks), s) for s in range(subs)]
                if norm_at(q) is not None:
                    st.append((i, "norm", norm_at(q)))
            if j == 2 and final_at(q) is not None:
                st.append((i, "back", final_at(q)))
            if j == 3 and final_at(q) is not None and not windowed:
                st.append((i, "proj", final_at(q)))
        return st, mx

    ST, MX = (len(uses) for uses in numbers("mid"))
    assert ST % 2 == 0 and MX % 2 == 0

    def tables(kind):
        out = []
        for uses, middle, size in zip(numbers(kind), numbers("mid"), (ST, MX)):
            left = 0 if kind == "first" else sum(u[0] == 0 for u in middle)
            out.append({u[1:]: n - left + (size if u[0] == 0 else 0) for n, u in enumerate(uses)})
        return out

    NUMBER = {kind: tables(kind) for kind in ("mid", "first", "last", "drain")}
    for kind in ("first", "last", "drain"):
        NUMBER[kind] = [{**NUMBER["mid"][n], **NUMBER[kind][n]} for n in range(2)]

    def norm_places(g, nt):
        if not windowed:
            at = nt[:, :, g % 4 * 4 * D:(g % 4 + 1) * 4 * D]
            return [(at.rearrange("p t (j d) -> p t j d", d=D), 0, 4, 0, D)]
        shift, sub = g // 4 * 2, g % 2
        part = g // 2 % 2
        at = nt[:, :, 64 * part:64 * part + 64].rearrange("p t (d h) -> p t h d", h=8)
        h = 4 * sub + shift
        if h + 4 <= 8:
            return [(at[:, :, h:h + 4, :], 0, 4, 0, D)]
        return [(at[:, :, h:8, :], 0, 8 - h, 0, D),
                (at[:, :, 0:h - 4, 1:D], 8 - h, h - 4, 0, D - 1),
                (at[:, :, 0:h - 4, 0:1], 8 - h, h - 4, D - 1, 1)]

    def window_places(f, x, turned):
        strips = (x[0:64].rearrange("p (h n w) -> p n h w", n=8, w=4),
                  turned[0:64].rearrange("p (n h w) -> p n h w", n=8, w=4))
        if f == 0:
            return [strips, (x[64:C], turned[64:C])]
        return [strips, (x[64:C, 2 * W:N], turned[64:C, 0:N - 2 * W]), (x[64:C, 0:2 * W], turned[64:C, N - 2 * W:N])]

    MXB = 8 * QB + subs
    MX0 = 2 * MXB

    with chip.stage() as ctx:
        QS = chip.buf(ctx, "QS", [C, 4, HP, N], BF16)
        KS = chip.buf(ctx, "KS", [C, 4, HP, N], BF16)
        VS = chip.buf(ctx, "VS", [C, 2, 8, HB * D])
        VA = chip.buf(ctx, "VA", [C, 2, 8, HB, 32])
        PT = chip.buf(ctx, "PT", [C, 8, N])
        OR = chip.buf(ctx, "OR", [C, 2, N])
        RC = chip.buf(ctx, "RC", [C, 2, 8, 4])
        NT = chip.buf(ctx, "NT", [C, 2, 8, C])
        if not windowed:
            ON = chip.buf(ctx, "ON", [C, N])
            wproj = chip.buf(ctx, "wproj", [C, C])
        unit = chip.buf(ctx, "unit", [C, 1])
        mxv = chip.buf(ctx, "mxv", [C, HB, 8, 1 if windowed else 2])
        nm = chip.buf(ctx, "nm", [C, HB * 8])
        nr = chip.buf(ctx, "nr", [C, 2, HB * 8])
        mp = chip.buf(ctx, "mp", [C, subs, PARTS, 32], BF16)
        mT = chip.buf(ctx, "mT", [PARTS * 32, subs, C], BF16)
        scratch = chip.buf(ctx, "scratch", [1, 16])
        st_ps = chip.psum(ctx, "st_ps", [C, 2, N])
        o_ps = chip.psum(ctx, "o_ps", [C, N])
        mx_ps = chip.psum(ctx, "mx_ps", [C, 2, HALF])
        qk_loaded = [chip.sem("qk_loaded") for _ in range(4)]
        rows_loaded = [chip.sem("rows_loaded") for _ in range(4)]
        v_loaded = [chip.sem("v_loaded") for _ in range(2)]
        st_free = [chip.sem("st_free") for _ in range(2)]
        (w_loaded, filled, rows_out, st_ready, mx_ready, mx_free, pv_done, o_free, va_done, max_taken,
         split, inverted, ones_set) = (chip.sem(s) for s in (
             "w_loaded", "filled", "rows_out", "st_ready", "mx_ready", "mx_free", "pv_done", "o_free",
             "va_done", "max_taken", "split", "inverted", "ones_set"))
        QK_DMAS = 2 * sum(len(runs) for runs in RUNS)

        def st_used(i, use):
            return i * ST + use + 1

        def periods(engine, period):
            period(0, "first")
            with engine.Fori(1, LAST) as i:
                period(i, "mid")
            period(LAST, "last")

        def st_wait(use):
            return st_free[use % 2], ST // 2, use // 2 + 2

        with nc.Block() as block:
            @block.sync
            def _(sp):
                def load_qk(i, k):
                    for o, dst in enumerate((QS, KS)):
                        rows = qk_rows(i, k, o).rearrange("a (e d hp) t -> e a d (hp t)", e=2, d=D)
                        for at, count, part, repeat in RUNS[o]:
                            for e in range(2):
                                src = rows[e, part:part + (1 if repeat else count)]
                                if repeat:
                                    src = src.to_broadcast([count, D, HP * N])
                                row = 64 * e + D * at
                                sp.dma_start(dst[row:row + D * count, k].rearrange("p hp t -> p (hp t)"), src
                                             ).then_inc(qk_loaded[k], 16)

                def load_v(i, k, slot):
                    sp.dma_start(VS[:, slot].rearrange("p t c -> p (t c)"), v_scr[i, k]).then_inc(v_loaded[slot], 16)

                def load_rows(k, half, copies, written):
                    sp.wait_ge(mx_free, copies)
                    for s in range(subs):
                        sp.dma_start(m_scr[half, s].rearrange("a h t q -> (a h t) q"), mT[:, s]).then_inc(rows_out, 16)
                    sp.wait_ge(rows_out, written)
                    for s in range(subs):
                        src = m_scr[half, s].rearrange("a (hp e) t q -> e a hp (t q)", e=2)
                        for e in range(2):
                            sp.dma_start(QS[64 * e + STACK:64 * e + ROWS, k, 2 * s:2 * s + 2, :],
                                         src[e]).then_inc(rows_loaded[k], 16)

                if not windowed:
                    sp.dma_start(wproj[:], dram[proj_name]).then_inc(w_loaded, 16)
                load_v(0, 0, 0)
                load_v(0, 1, 1)
                for k in range(4):
                    sp.wait_ge(ones_set, k + 1)
                    load_qk(0, k)
                sp.wait_ge(va_done, 1)
                load_v(0, 2, 0)
                for k in range(2):
                    load_rows(k, k, (k + 1) * MXB + 2, 16 * subs * (k + 1))

                def image(i, kind):
                    last = kind == "last"
                    st_use, mx_use = NUMBER[kind]
                    for k in range(4):
                        if turn_at(k * QB) is not None:
                            if not last or k - 1 < 2:
                                load_rows((k + 1) % 4, (k + 1) % 2, i * MX + (MX0 + 2 + 1 + mx_use["turn", k - 1, subs - 1]),
                                          (i * 4 + k - 1) * (16 * subs) + 16 * subs * 3)
                        if not last:
                            sp.wait_ge(st_ready, st_used(i, st_use["exp", (k + 1) * QB - 1, 3]))
                            load_qk(i + 1, k)
                        if not last or k == 0:
                            sp.wait_ge(va_done, i * 4 + k + 2)
                            load_v(i + (k + 3) // 4, (k + 3) % 4, (k + 3) % 2)
                    if not last:
                        load_rows(1, 1, i * MX + (MX0 + 2 + 1 + mx_use["turn", 3, subs - 1]),
                                  (i * 4 + 3) * (16 * subs) + 16 * subs * 3)

                periods(sp, image)

            @block.tensor
            def _(pe):
                def stack(buf, k, h, rows):
                    e = h % 2
                    return buf[64 * e:64 * e + rows, k, h // 2, :]

                def max_scores(k, n, slot):
                    if windowed:
                        q, kk = (stack(b, k, n // 2, STACK) for b in (QS, KS))
                        for w in range(4):
                            at = ((n % 2) * 4 + w) * C
                            mm = nc.tensor.matmul(mx_ps[:, slot, w * C:(w + 1) * C], q[:, at:at + C], kk[:, at:at + C],
                                                  start=True, stop=True)
                    else:
                        q, kk = (stack(b, k, n // 16, STACK) for b in (QS, KS))
                        at = (n // 2 % 8) * C
                        mm = nc.tensor.matmul(mx_ps[:, slot, :], q[:, at:at + C],
                                              kk[:, (n % 2) * HALF:(n % 2 + 1) * HALF], start=True, stop=True)
                    mm.then_inc(mx_ready, 1)

                def turn(s, slot):
                    nc.tensor.transpose(mx_ps[0:PARTS * 32, slot, 0:C // 2].bitcast(BF16), mp[:, s].rearrange("p a c -> p (a c)"),
                                        ident[:]).then_inc(mx_ready, 1)

                for k in range(2):
                    pe.wait_ge(qk_loaded[k], 16 * QK_DMAS)
                    for n in range(8 * QB):
                        pe.wait_ge(mx_free, k * MXB + n + 1)
                        max_scores(k, n, (k * MXB + n) % 2)
                    pe.wait_ge(split, 4 * (k + 1))
                    for s in range(subs):
                        pe.wait_ge(mx_free, k * MXB + 8 * QB + s + 1)
                        turn(s, (k * MXB + 8 * QB + s) % 2)

                def values(i, q, half, st_use):
                    k, s, kt, g = q // QB, q // kt_quads % subs, q % kt_quads, q // kt_quads
                    if q % QB == 0 and half == 0:
                        pe.wait_ge(va_done, i * 4 + k + 1)
                    if kt == 0:
                        pe.wait_ge(o_free, i * (2 * NG) + 2 * g + half + 1)
                    if half == 0:
                        for use in {st_use["exp", q, j] % 2: st_use["exp", q, j] for j in range(4)}.values():
                            sem, per, val = st_wait(use)
                            pe.wait_ge(sem, i * per + val)
                    width = C if windowed else HALF
                    for t in range(HALF * half // width, HALF * (half + 1) // width):
                        for j in range(4):
                            mm = nc.tensor.matmul(
                                o_ps[32 * j:32 * j + 32, t * width:(t + 1) * width],
                                VA[:, k % 2, t if windowed else kt, 4 * s + j, :],
                                PT[:, (q % 2) * 4 + j, t * width:(t + 1) * width],
                                start=(kt == 0), stop=(kt == kt_quads - 1))
                    mm.then_inc(pv_done, 1)

                def step(i, q, j, last, st_use, mx_use, warm_up):
                    k, s, kt = q // QB, q // kt_quads % subs, q % kt_quads
                    if q < NQ:
                        if q % QB == 0 and j == 0:
                            pe.wait_ge(qk_loaded[k], (i + 1) * (16 * QK_DMAS))
                            pe.wait_ge(rows_loaded[k], (i + 1) * (16 * 2 * subs))
                        use = st_use["exp", q, j]
                        sem, per, _ = st_wait(use)
                        pe.wait_ge(sem, i * per + use // 2 + 1)
                        for _ in range(WARM_UP if warm_up else 0):
                            nc.tensor.matmul(st_ps[:, use % 2, 0:HALF], identf[:], X[:, LAST, 0:HALF], start=True, stop=True)
                        qq, kk = (stack(b, k, 4 * s + j, ROWS) for b in (QS, KS))
                        if windowed:
                            for w in range(8):
                                mm = nc.tensor.matmul(st_ps[:, use % 2, w * C:(w + 1) * C], kk[:, w * C:(w + 1) * C],
                                                      qq[:, w * C:(w + 1) * C], start=True, stop=True)
                        else:
                            for c in range(2):
                                mm = nc.tensor.matmul(st_ps[:, use % 2, c * HALF:(c + 1) * HALF],
                                                      kk[:, kt * C:(kt + 1) * C],
                                                      qq[:, c * HALF:(c + 1) * HALF], start=True, stop=True)
                        mm.then_inc(st_ready, 1)
                    with_max = q < NQ and (not last or k < 2)
                    if with_max and q % QB == 0 and j == 0:
                        pe.wait_ge(qk_loaded[(k + 2) % 4], (i + (1 if k < 2 else 2)) * (16 * QK_DMAS))
                    for x in (2 * j, 2 * j + 1):
                        if with_max:
                            pe.wait_ge(mx_free, i * MX + (MX0 + mx_use["max", q, x] + 1))
                            max_scores((k + 2) % 4, (q % QB) * 8 + x, mx_use["max", q, x] % 2)
                        if x % 4 == 2 and 1 <= q <= NQ:
                            values(i, q - 1, x // 4, st_use)
                    if j == 1 and turn_at(q, 2 if last else 4) is not None:
                        m = turn_at(q)
                        pe.wait_ge(split, i * 16 + 4 * (2 + m + 1))
                        for s2 in range(subs):
                            use = mx_use["turn", m, s2]
                            pe.wait_ge(mx_free, i * MX + (MX0 + use + 1))
                            turn(s2, use % 2)
                    if j == 1 and norm_at(q) is not None:
                        g = norm_at(q)
                        use = st_use["norm", g]
                        sem, per, _ = st_wait(use)
                        pe.wait_ge(o_free, i * (2 * NG) + 2 * g + 4)
                        pe.wait_ge(sem, i * per + use // 2 + 1)
                        for t in range(8):
                            mm = nc.tensor.transpose(st_ps[:, use % 2, t * C:(t + 1) * C],
                                                     OR[:, g % 2, t * C:(t + 1) * C], identf[:])
                        mm.then_inc(st_ready, 1)
                    if j == 2 and final_at(q) is not None:
                        f = final_at(q)
                        use = st_use["back", f]
                        sem, per, _ = st_wait(use)
                        norm_sem, norm_per, norm_val = st_wait(st_use["norm", 4 * f + 3])
                        if norm_sem is not sem:
                            pe.wait_ge(norm_sem, i * norm_per + norm_val)
                        pe.wait_ge(sem, i * per + use // 2 + 1)
                        for t in range(8):
                            mm = nc.tensor.transpose(st_ps[:, use % 2, t * C:(t + 1) * C], NT[:, f % 2, t, :], identf[:])
                        mm.then_inc(st_ready, 1)
                    if j == 3 and final_at(q) is not None and not windowed:
                        use = st_use["proj", final_at(q)]
                        sem, per, _ = st_wait(use)
                        back_sem, back_per, back_val = st_wait(st_use["back", final_at(q)])
                        pe.wait_ge(w_loaded, 16)
                        if back_sem is not sem:
                            pe.wait_ge(back_sem, i * back_per + back_val)
                        pe.wait_ge(sem, i * per + use // 2 + 1)
                        for c in range(2):
                            mm = nc.tensor.matmul(st_ps[:, use % 2, c * HALF:(c + 1) * HALF], wproj[:],
                                                  ON[:, c * HALF:(c + 1) * HALF], start=True, stop=True)
                        mm.then_inc(st_ready, 1)

                def period(i, kind):
                    for n, q, j, last in order(i, kind):
                        step(n, q, j, last, *NUMBER[kind], kind == "first" and (q, j) == (1, 0))

                periods(pe, period)
                period(B, "drain")

            @block.scalar
            def _(act):
                def take_half(i, q, half, st_use):
                    g = q // kt_quads
                    act.wait_ge(pv_done, i * (2 * NQ) + 2 * q + half + 5)
                    if g >= 2:
                        sem, per, val = st_wait(st_use["norm", g - 2])
                        act.wait_ge(sem, i * per + val)
                    at = slice(half * HALF, (half + 1) * HALF)
                    nc.scalar.copy(OR[:, g % 2, at], o_ps[:, at]).then_inc(o_free, 1)

                def step(i, q, j, st_use):
                    if q < NQ:
                        use = st_use["exp", q, j]
                        act.wait_ge(st_ready, st_used(i, use))
                        act.wait_ge(pv_done, i * (2 * NQ) + 2 * q + 2)
                        nc.scalar.activation(PT[:, (q % 2) * 4 + j], st_ps[:, use % 2], ACT.Exp,
                                             scale=scale).then_inc(st_free[use % 2], 1)
                    if j == 0 and ends_output(q - 2):
                        take_half(i, q - 2, 1, st_use)
                    if j == 2 and ends_output(q - 1):
                        take_half(i, q - 1, 0, st_use)
                    if j == 2 and final_at(q) is not None and not windowed:
                        use = st_use["back", final_at(q)]
                        act.wait_ge(st_ready, st_used(i, use))
                        nc.scalar.copy(ON[:], st_ps[:, use % 2]).then_inc(st_free[use % 2], 1)

                def period(i, kind):
                    for n, q, j, _ in order(i, kind):
                        step(n, q, j, NUMBER[kind][0])

                periods(act, period)
                period(B, "drain")

            @block.vector
            def _(v):
                for k in range(4):
                    nc.vector.memset(KS[:, k], 1.0).then_inc(ones_set, 1)
                    if k == 0:
                        nc.vector.memset(VA[:], 0.0).then_inc(filled, 1)
                v.wait_ge(filled, 1)
                nc.vector.memset(unit[:], 1.0)
                nc.vector.memset(VA[:, :, :, :, D:D + 1], 1.0).then_inc(filled, 1)
                grant(nc, scratch, [(st_free[0], 1), (st_free[1], 1), (mx_free, 2), (pv_done, 4), (o_free, 2)])

                def reduce_half(n, slot):
                    if windowed:
                        nc.vector.tensor_reduce(mxv[:, n // 2, (n % 2) * 4:(n % 2) * 4 + 4, 0],
                                                mx_ps[:, slot].rearrange("p (w k) -> p w k", w=4),
                                                AX.X, ALU.max).then_inc(mx_free, 1)
                    else:
                        nc.vector.tensor_reduce(mxv[:, n // 16, n // 2 % 8, n % 2:n % 2 + 1], mx_ps[:, slot],
                                                AX.X, ALU.max).then_inc(mx_free, 1)

                def take_max(freed):
                    v.wait_ge(mx_free, freed)
                    nc.vector.tensor_reduce(nm[:], mxv[:].rearrange("p h t c -> p (h t) c"), AX.X, ALU.max,
                                            negate=True).then_inc(max_taken, 1)

                def copy_turned(s, slot):
                    nc.vector.tensor_copy(mT[:, s], mx_ps[0:PARTS * 32, slot, 0:C // 2].bitcast(BF16)).then_inc(mx_free, 1)

                for k in range(2):
                    if k:
                        v.wait_ge(max_taken, k)
                    for n in range(8 * QB):
                        v.wait_ge(mx_ready, k * MXB + n + 1)
                        reduce_half(n, (k * MXB + n) % 2)
                    take_max(k * MXB + 8 * QB + 2)
                    if k:
                        v.wait_ge(rows_out, 16 * subs * k)
                    for s in range(subs):
                        use = k * MXB + 8 * QB + s
                        v.wait_ge(mx_ready, use + 1)
                        copy_turned(s, use % 2)

                def normalise(i, g, st_use):
                    use = st_use["norm", g]
                    turned = st_ps[:, use % 2].rearrange("p (t j r) -> p t j r", t=8, j=4)
                    v.wait_ge(st_ready, st_used(i, use))
                    nc.vector.reciprocal(RC[:, g % 2], turned[:, :, :, D]).then_inc(inverted, 1)
                    v.wait_ge(inverted, i * NG + g + 1)
                    for dst, j0, js, d0, ds in norm_places(g, NT[:, g // 4 % 2]):
                        ins = nc.vector.tensor_tensor(
                            dst, turned[:, :, j0:j0 + js, d0:d0 + ds],
                            RC[:, g % 2, :, j0:j0 + js].unsqueeze(3).to_broadcast([C, 8, js, ds]), ALU.mult)
                    ins.then_inc(st_free[use % 2], 1)

                def step(i, q, j, last, st_use, mx_use):
                    k = q // QB
                    if q < NQ and (not last or k < 2):
                        if q % QB == 0 and j == 0:
                            v.wait_ge(max_taken, i * 4 + k + 2)
                        for x in (2 * j, 2 * j + 1):
                            v.wait_ge(mx_ready, i * MX + (MX0 + mx_use["max", q, x] + 1))
                            reduce_half((q % QB) * 8 + x, mx_use["max", q, x] % 2)
                    if j == 1 and turn_at(q, 2 if last else 4) is not None:
                        m = turn_at(q)
                        v.wait_ge(rows_out, (i * 4 + m) * (16 * subs) + 16 * subs * 2)
                        for s in range(subs):
                            use = mx_use["turn", m, s]
                            v.wait_ge(mx_ready, i * MX + (MX0 + use + 1))
                            copy_turned(s, use % 2)
                    if j == 1 and norm_at(q) is not None:
                        normalise(i, norm_at(q), st_use)
                    if j == 2 and final_at(q) is not None and windowed:
                        f = final_at(q)
                        use = st_use["back", f]
                        v.wait_ge(st_ready, st_used(i, use))
                        for dst, src in window_places(f, X[:, i, :], st_ps[:, use % 2]):
                            ins = nc.vector.tensor_tensor(dst, src, dst, ALU.add)
                        ins.then_inc(st_free[use % 2], 1)
                    if j == 3 and final_at(q) is not None and not windowed:
                        use = st_use["proj", final_at(q)]
                        v.wait_ge(st_ready, st_used(i, use))
                        nc.vector.scalar_tensor_tensor(X[:, i, :], st_ps[:, use % 2], bias[:], X[:, i, :],
                                                       ALU.add, ALU.add).then_inc(st_free[use % 2], 1)
                    if j == 3 and q < NQ and (q + 1) % QB == 0 and (not last or k < 2):
                        take_max(i * MX + (MX0 + 2 + mx_use["max", q, 7] + 1))

                def period(i, kind):
                    for n, q, j, last in order(i, kind):
                        step(n, q, j, last, *NUMBER[kind])

                periods(v, period)
                period(B, "drain")

            @block.gpsimd
            def _(pool):
                def copy(dst, src):
                    one = unit[:]
                    while len(one.shape) < len(src.shape):
                        one = one.unsqueeze(1)
                    return nc.gpsimd.tensor_tensor(dst, src, one.to_broadcast(list(src.shape)), ALU.mult)

                def expand_v(k, slot):
                    copy(VA[:, slot, :, :, 0:D], VS[:, slot].rearrange("p t (h d) -> p t h d", d=D)).then_inc(va_done, 1)

                def split_max(taken, base):
                    view = nm[:].rearrange("p (s c) -> p s c", s=subs)
                    rv = [nr[:, n].rearrange("p (s c) -> p s c", s=subs) for n in range(2)]
                    pool.wait_ge(max_taken, taken)
                    copy(mp[:, :, 0], view).then_inc(split, 1)
                    pool.wait_ge(split, base + 1)
                    nc.gpsimd.tensor_tensor(rv[0], view, mp[:, :, 0], ALU.subtract).then_inc(split, 1)
                    pool.wait_ge(split, base + 2)
                    copy(mp[:, :, 1], rv[0]).then_inc(split, 1)
                    pool.wait_ge(split, base + 3)
                    nc.gpsimd.tensor_tensor(mp[:, :, 2], rv[0], mp[:, :, 1], ALU.subtract).then_inc(split, 1)

                pool.wait_ge(filled, 2)
                pool.wait_ge(v_loaded[0], 16)
                expand_v(0, 0)
                for k in range(2):
                    split_max(k + 1, 4 * k)

                def image(i, last):
                    for q in range(NQ):
                        k = q // QB
                        if q % QB == 1 and (not last or k < 3):
                            pool.wait_ge(v_loaded[(k + 1) % 2], (i * 2 + (k + 1) // 2) * 16 + 16)
                            pool.wait_ge(pv_done, i * (2 * NQ) + 2 * k * QB + 4)
                            expand_v((k + 1) % 4, (k + 1) % 2)
                        if (q + 1) % QB == 0 and (not last or k < 2):
                            split_max(i * 4 + k + 3, i * 16 + 4 * (2 + k))

                with pool.Fori(0, LAST) as i:
                    image(i, False)
                image(LAST, True)


PE_TAPS = (0, 1, 2, 3, 5)


def conv_stage(chip, X, dram, mean_g, rstd_g, pooled, eps5, identf):
    nc = chip.nc
    VE_TAPS = [t for t in range(9) if t not in PE_TAPS]
    with chip.stage() as ctx:
        w1, w2 = chip.buf(ctx, "se_w1", [C, C // 4]), chip.buf(ctx, "se_w2", [C // 4, C])
        rw, rb = chip.buf(ctx, "rw", [C, 9]), chip.buf(ctx, "rb", [C, 1])
        diag = chip.buf(ctx, "diag", [C, len(PE_TAPS), C])
        h, hl = chip.buf(ctx, "se_h", [C // 4, B]), chip.buf(ctx, "se_hl", [C // 4, B])
        gate = chip.buf(ctx, "se_gate", [C, B])
        scale = chip.buf(ctx, "scale", [C, B, 1])
        xp = chip.buf(ctx, "xp", [C, 2, H + 2, W + 2])
        acc, z = chip.buf(ctx, "acc", [C, 2, N]), chip.buf(ctx, "z", [C, 2, N])
        st, mv = chip.buf(ctx, "st", [C, 2, 12]), chip.buf(ctx, "mv", [C, 2, 2])
        sd, rs, nb, pause = (chip.buf(ctx, n, [C, 2, 1]) for n in ("sd", "rs", "nb", "pause"))
        scratch = chip.buf(ctx, "scratch", [1, 8])
        ps = chip.psum(ctx, "se_ps", [C, 2, HALF])
        c_ps = chip.psum(ctx, "c_ps", [C, 2, N])
        w_loaded, squeezed, chain, gated, padded, conv, aggr, rooted, scaled, ascaled, added = (chip.sem(s) for s in (
            "w_loaded", "squeezed", "chain", "gated", "padded", "conv", "aggr", "rooted", "scaled", "ascaled", "added"))
        with nc.Block() as block:
            @block.sync
            def _(sp):
                for dst, name in ((w1, "se_w1"), (w2, "se_w2"), (rw, "refine_w"), (rb, "refine_b")):
                    sp.dma_start(dst[:], dram[name]).then_inc(w_loaded, 16)
                sp.wait_ge(w_loaded, 64)

            @block.tensor
            def _(pe):
                pe.wait_ge(w_loaded, 64)
                nc.tensor.matmul(ps[0:C // 4, 0, 0:B], w1[:], pooled[:], start=True, stop=True).then_inc(squeezed, 1)
                pe.wait_ge(chain, 4)
                nc.tensor.matmul(ps[:, 1, 0:B], w2[:], hl[:], start=True, stop=True).then_inc(squeezed, 1)
                with pe.Fori(0, B // 2) as i:
                    for s in range(2):
                        pe.wait_ge(padded, i * 2 + s + 1)
                        pe.wait_ge(added, i * 2 + s + 1)
                        for half in range(2):
                            for n, t in enumerate(PE_TAPS):
                                r = 16 * half + t // 3
                                mm = nc.tensor.matmul(c_ps[:, s, half * HALF:(half + 1) * HALF], diag[:, n, :],
                                                      xp[:, s, r:r + 16, t % 3:t % 3 + W],
                                                      start=(n == 0), stop=(n == len(PE_TAPS) - 1))
                        mm.then_inc(conv, 1)

            @block.scalar
            def _(act):
                act.wait_ge(squeezed, 2)
                nc.scalar.activation(gate[:], ps[:, 1, 0:B], ACT.Sigmoid).then_inc(gated, 1)
                with act.Fori(0, B // 2) as i:
                    for s in range(2):
                        act.wait_ge(aggr, i * 2 + s + 1)
                        nc.scalar.activation(sd[:, s], mv[:, s, 1:2], ACT.Sqrt, bias=eps5[:]).then_inc(rooted, 1)
                    for s in range(2):
                        act.wait_ge(scaled, i * 2 + s + 1)
                        nc.scalar.activation(z[:, s], acc[:, s], ACT.Identity, bias=nb[:, s], scale=rs[:, s]).then_inc(ascaled, 1)

            @block.vector
            def _(v):
                count = [0]

                def chained(ins):
                    count[0] += 1
                    ins.then_inc(chain, 1)
                    v.wait_ge(chain, count[0])

                grant(nc, scratch, [(added, 2)])
                chained(nc.vector.memset(xp[:], 0.0))
                v.wait_ge(w_loaded, 64)
                for n, t in enumerate(PE_TAPS):
                    ins = nc.vector.tensor_scalar(diag[:, n, :], identf[:], rw[:, t:t + 1], None, ALU.mult)
                chained(ins)
                v.wait_ge(squeezed, 1)
                chained(nc.vector.tensor_copy(h[:], ps[0:C // 4, 0, 0:B]))
                chained(nc.vector.scalar_tensor_tensor(hl[:], h[:], 0.01, h[:], ALU.mult, ALU.max))
                v.wait_ge(gated, 1)
                chained(nc.vector.tensor_tensor(scale[:].rearrange("p b o -> p (b o)"), gate[:],
                                                rstd_g[:].rearrange("p b o -> p (b o)"), ALU.mult))
                base = count[0]
                STEPS = len(VE_TAPS) + 4
                with v.Fori(0, B // 2) as i:
                    step = [0]

                    def then(ins):
                        step[0] += 1
                        ins.then_inc(chain, 1)
                        return step[0]

                    def after(n):
                        v.wait_ge(chain, i * (2 * STEPS) + (base + n))

                    done = [0, 0]
                    for s in range(2):
                        nc.vector.tensor_scalar(xp[:, s, 1:H + 1, 1:W + 1],
                                                X[:, i * 2 + s, :].rearrange("p (h w) -> p h w", h=H),
                                                mean_g[:, i * 2 + s, :], scale[:, i * 2 + s, :],
                                                ALU.subtract, ALU.mult).then_inc(padded, 1)
                    for s in range(2):
                        v.wait_ge(padded, i * 2 + s + 1)
                        t = VE_TAPS[0]
                        done[s] = then(nc.vector.tensor_scalar(
                            acc[:, s].rearrange("p (h w) -> p h w", h=H), xp[:, s, t // 3:t // 3 + H, t % 3:t % 3 + W],
                            rw[:, t:t + 1], rb[:], ALU.mult, ALU.add))
                    for t in VE_TAPS[1:]:
                        for s in range(2):
                            after(done[s])
                            src = xp[:, s, t // 3:t // 3 + H, t % 3:t % 3 + W]
                            out = acc[:, s].rearrange("p (h w) -> p h w", h=H)
                            done[s] = then(nc.vector.scalar_tensor_tensor(out, src, rw[:, t:t + 1], out, ALU.mult, ALU.add))
                    for s in range(2):
                        v.wait_ge(conv, i * 2 + s + 1)
                        after(done[s])
                        done[s] = then(nc.vector.tensor_tensor(acc[:, s], c_ps[:, s], acc[:, s], ALU.add))
                    for s in range(2):
                        after(done[s])
                        for c in range(2):
                            ins = nc.vector.bn_stats(st[:, s, 6 * c:6 * c + 6], acc[:, s, c * HALF:(c + 1) * HALF])
                        done[s] = then(ins)
                    for s in range(2):
                        after(done[s])
                        nc.vector.memset(pause[:, s], 0.0)
                        nc.vector.bn_aggr(mv[:, s], st[:, s]).then_inc(aggr, 1)
                    for s in range(2):
                        v.wait_ge(rooted, i * 2 + s + 1)
                        done[s] = then(nc.vector.reciprocal(rs[:, s], sd[:, s]))
                    for s in range(2):
                        after(done[s])
                        nc.vector.scalar_tensor_tensor(nb[:, s], mv[:, s, 0:1], -1.0, rs[:, s],
                                                       ALU.mult, ALU.mult).then_inc(scaled, 1)
                    for s in range(2):
                        v.wait_ge(ascaled, i * 2 + s + 1)
                        done[s] = then(nc.vector.scalar_tensor_tensor(z[:, s], z[:, s], 0.01, z[:, s], ALU.mult, ALU.max))
                    for s in range(2):
                        after(done[s])
                        nc.vector.tensor_tensor(X[:, i * 2 + s, :], X[:, i * 2 + s, :], z[:, s], ALU.add).then_inc(added, 1)
                    assert step[0] == 2 * STEPS, step[0]


def layer_norm(chip, src, mean_w, eps5, identf, dst=None, X=None, gamma=None, beta=None):
    nc = chip.nc
    TILES = HALF // C
    with chip.stage() as ctx:
        xc = chip.buf(ctx, "xc", [C, 2, 2, HALF])
        sq, t = (chip.buf(ctx, n, [C, 2, HALF]) for n in ("sq", "t"))
        sd, rs = (chip.buf(ctx, n, [C, 2, TILES]) for n in ("sd", "rs"))
        scratch = chip.buf(ctx, "scratch", [1, 8])
        m_ps, v_ps, r_ps = (chip.psum(ctx, n, [C, 2, HALF]) for n in ("m_ps", "v_ps", "r_ps"))
        mean_ready, centred, squared, var_ready, rooted, inverted, spread, scaled, stored = (chip.sem(s) for s in (
            "mean_ready", "centred", "squared", "var_ready", "rooted", "inverted", "spread", "scaled", "stored"))

        def periods(engine, front, back):
            front(0, 0)
            with engine.Fori(0, B // 2 - 1) as i:
                for odd in (1, 0):
                    front(i * 2 + (2 - odd), odd)
                    back(i * 2 + (1 - odd), 1 - odd)
            front(B - 1, 1)
            back(B - 2, 0)
            back(B - 1, 1)

        with nc.Block() as block:
            @block.tensor
            def _(pe):
                def front(i, odd):
                    for c in range(2):
                        pe.wait_ge(centred, i * 2 + c + 1)
                        nc.tensor.matmul(m_ps[:, c], mean_w[:], src[:, i, c * HALF:(c + 1) * HALF],
                                         start=True, stop=True).then_inc(mean_ready, 1)

                def middle(i):
                    for c in range(2):
                        pe.wait_ge(squared, i * 2 + c + 1)
                        pe.wait_ge(rooted, i * 2 + c + 1)
                        for n in range(TILES):
                            mm = nc.tensor.matmul(v_ps[:, c, n:n + 1], sq[:, c, n * C:(n + 1) * C], mean_w[:, 0:1],
                                                  start=True, stop=True)
                        mm.then_inc(var_ready, 1)

                def back(i, odd):
                    middle(i)
                    for c in range(2):
                        pe.wait_ge(inverted, i * 2 + c + 1)
                        pe.wait_ge(scaled, i * 2 + c + 3)
                        for n in range(TILES):
                            mm = nc.tensor.matmul(r_ps[:, c, n * C:(n + 1) * C],
                                                  rs[:, c, n:n + 1].to_broadcast([C, C]), identf[:], start=True, stop=True)
                        mm.then_inc(spread, 1)

                periods(pe, front, back)

            @block.scalar
            def _(act):
                def front(i, odd):
                    for c in range(2):
                        act.wait_ge(centred, i * 2 + c + 3)
                        act.wait_ge(var_ready, i * 2 + c + 1)
                        nc.scalar.activation(sq[:, c], xc[:, odd, c], ACT.Square).then_inc(squared, 1)

                def back(i, odd):
                    for c in range(2):
                        act.wait_ge(var_ready, i * 2 + c + 3)
                        nc.scalar.activation(sd[:, c], v_ps[:, c, 0:TILES], ACT.Sqrt, bias=eps5[:]).then_inc(rooted, 1)

                with act.Fori(0, B // 2) as i:
                    for odd in range(2):
                        front(i * 2 + odd, odd)
                        back(i * 2 + odd, odd)

            @block.vector
            def _(v):
                def front(i, odd):
                    for c in range(2):
                        v.wait_ge(mean_ready, i * 2 + c + 1)
                        v.wait_ge(scaled, i * 2 + c + 1)
                        nc.vector.tensor_tensor(xc[:, odd, c], src[:, i, c * HALF:(c + 1) * HALF], m_ps[:, c],
                                                ALU.subtract).then_inc(centred, 1)

                def back(i, odd):
                    for c in range(2):
                        v.wait_ge(rooted, i * 2 + c + 3)
                        nc.vector.reciprocal(rs[:, c], sd[:, c]).then_inc(inverted, 1)
                    for c in range(2):
                        v.wait_ge(spread, i * 2 + c + 1)
                        if dst is not None:
                            nc.vector.tensor_tensor(dst[:, i, c * HALF:(c + 1) * HALF], xc[:, odd, c], r_ps[:, c],
                                                    ALU.mult).then_inc(scaled, 1)
                            continue
                        nc.vector.scalar_tensor_tensor(t[:, c], xc[:, odd, c], gamma[:], r_ps[:, c],
                                                       ALU.mult, ALU.mult).then_inc(scaled, 1)
                        v.wait_ge(scaled, i * 2 + c + 5)
                        at = X[:, i, c * HALF:(c + 1) * HALF]
                        nc.vector.scalar_tensor_tensor(at, t[:, c], beta[:], at, ALU.add, ALU.add).then_inc(stored, 1)

                grant(nc, scratch, [(centred, 2), (rooted, 2), (var_ready, 2), (scaled, 4)])
                periods(v, front, back)


def token_projections(chip, XN, dram, qk_scr, v_scr):
    nc = chip.nc
    with chip.stage() as ctx:
        wqk, wv = chip.buf(ctx, "wqk", [C, 2, C]), chip.buf(ctx, "wv", [C, C])
        bqk, bv = chip.buf(ctx, "bqk", [C, 2]), chip.buf(ctx, "bv", [C, C])
        xs = chip.buf(ctx, "xs", [C, N])
        parts = chip.buf(ctx, "parts", [C, 2, PARTS, N], BF16)
        rest = chip.buf(ctx, "rest", [C, 2, N])
        vs = chip.buf(ctx, "vs", [C, 4, 8, 32])
        scratch = chip.buf(ctx, "scratch", [1, 8])
        qk_ps = chip.psum(ctx, "qk_ps", [C, 2, N])
        v_ps = chip.psum(ctx, "v_ps", [C, 8, C])
        w_loaded, staged, qk_ready, hi_done, rest_done, mid_done, lo_done, v_ready, v_copied, v_out = (
            chip.sem(s) for s in ("w_loaded", "staged", "qk_ready", "hi_done", "rest_done", "mid_done", "lo_done",
                                  "v_ready", "v_copied", "v_out"))
        parts_out = [chip.sem("parts_out") for _ in range(2)]
        with nc.Block() as block:
            @block.sync
            def _(sp):
                for dst, name in ((wqk, "w2_qk"), (wv, "w2_v"), (bqk, "b2_qk")):
                    sp.dma_start(dst[:], dram[name]).then_inc(w_loaded, 16)
                sp.dma_start(bv[:], dram["b2_v"].to_broadcast([C, C])).then_inc(w_loaded, 16)
                with sp.Fori(0, B) as i:
                    for u in range(2):
                        sp.wait_ge(lo_done, i * 2 + u + 3)
                        sp.dma_start(qk_scr[i, u].rearrange("a r t -> r a t"), parts[:, u]).then_inc(parts_out[u], 16)
                    sp.wait_ge(v_copied, i + 2)
                    sp.dma_start(v_scr[i].rearrange("k p c -> p k c"),
                                 vs[:].rearrange("p k t c -> p k (t c)")).then_inc(v_out, 16)
                for s in (*parts_out, v_out):
                    sp.wait_ge(s, 16 * (B + 1))

            @block.tensor
            def _(pe):
                pe.wait_ge(w_loaded, 64)
                with pe.Fori(0, B) as i:
                    pe.wait_ge(staged, i + 1)
                    for u in range(2):
                        pe.wait_ge(rest_done, i * 2 + u + 1)
                        for c in range(2):
                            mm = nc.tensor.matmul(qk_ps[:, u, c * HALF:(c + 1) * HALF], wqk[:, u, :],
                                                  xs[:, c * HALF:(c + 1) * HALF], start=True, stop=True)
                        mm.then_inc(qk_ready, 1)
                    pe.wait_ge(v_copied, i + 1)
                    for t in range(8):
                        mm = nc.tensor.matmul(v_ps[:, t, :], xs[:, t * C:(t + 1) * C], wv[:], start=True, stop=True)
                    mm.then_inc(v_ready, 1)

            @block.scalar
            def _(act):
                act.wait_ge(w_loaded, 64)
                with act.Fori(0, B) as i:
                    for u in range(2):
                        act.wait_ge(qk_ready, i * 2 + u + 1)
                        act.wait_ge(parts_out[u], i * 16 + 16)
                        nc.scalar.activation(parts[:, u, 0], qk_ps[:, u], ACT.Identity,
                                             bias=bqk[:, u:u + 1]).then_inc(hi_done, 1)
                    for u in range(2):
                        act.wait_ge(rest_done, i * 2 + u + 3)
                        nc.scalar.copy(parts[:, u, 1], rest[:, u]).then_inc(mid_done, 1)

            @block.gpsimd
            def _(pool):
                with pool.Fori(0, B) as i:
                    for u in range(2):
                        pool.wait_ge(mid_done, i * 2 + u + 1)
                        nc.gpsimd.tensor_tensor(parts[:, u, 2], rest[:, u], parts[:, u, 1],
                                                ALU.subtract).then_inc(lo_done, 1)

            @block.vector
            def _(v):
                grant(nc, scratch, [(rest_done, 2), (lo_done, 2), (v_copied, 1), (parts_out[0], 16),
                                    (parts_out[1], 16), (v_out, 16), (v_ready, 1)])
                v.wait_ge(w_loaded, 64)
                with v.Fori(0, B) as i:
                    v.wait_ge(v_ready, i + 1)
                    nc.vector.tensor_copy(xs[:], XN[:, i, :]).then_inc(staged, 1)
                    for u in range(2):
                        v.wait_ge(hi_done, i * 2 + u + 1)
                        v.wait_ge(lo_done, i * 2 + u + 1)
                        nc.vector.scalar_tensor_tensor(rest[:, u], qk_ps[:, u], bqk[:, u:u + 1], parts[:, u, 0],
                                                       ALU.add, ALU.subtract).then_inc(rest_done, 1)
                    v.wait_ge(v_ready, i + 2)
                    v.wait_ge(v_out, i * 16 + 16)
                    for k in range(4):
                        ins = nc.vector.tensor_tensor(vs[:, k], v_ps[:, :, 32 * k:32 * k + 32],
                                                      bv[:, 32 * k:32 * k + 32].unsqueeze(1).to_broadcast([C, 8, 32]), ALU.add)
                    ins.then_inc(v_copied, 1)


def route(chip, XN, dram, w_name, identf, prefer, guard, g_scr):
    nc = chip.nc
    T = B * 8
    with chip.stage() as ctx:
        wr = chip.buf(ctx, "wr", [C, E])
        xs = chip.buf(ctx, "xs", [C, 2, N])
        L, P, M, G = (chip.buf(ctx, n, [C, T, E]) for n in ("L", "P", "M", "G"))
        m1, m2, r = (chip.buf(ctx, n, [C, T]) for n in ("m1", "m2", "r"))
        gt = chip.buf(ctx, "gt", [E * 8, B, C])
        scratch = chip.buf(ctx, "scratch", [1, 8])
        l_ps = chip.psum(ctx, "l_ps", [C, 2, HALF])
        g_ps = chip.psum(ctx, "g_ps", [C, B, C])
        w_loaded, staged, logits, copied, chain, expd, gates, turned, gcopied, out = (chip.sem(s) for s in (
            "w_loaded", "staged", "logits", "copied", "chain", "expd", "gates", "turned", "gcopied", "out"))
        wide = lambda a: a[:].unsqueeze(2).to_broadcast([C, T, E])
        with nc.Block() as block:
            @block.sync
            def _(sp):
                sp.dma_start(wr[:], dram[w_name]).then_inc(w_loaded, 16)
                for half in range(2):
                    sp.wait_ge(gcopied, half + 1)
                    for i in range(4 * half, 4 * half + 4):
                        sp.dma_start(g_scr[i].rearrange("e (t q) -> (e t) q", q=C), gt[:, i]).then_inc(out, 16)
                sp.wait_ge(out, 16 * B)

            @block.scalar
            def _(act):
                with act.Fori(0, B // 2) as i:
                    for s in range(2):
                        act.wait_ge(logits, i * 2 + s + 1)
                        nc.scalar.copy(xs[:, s], XN[:, i * 2 + s, :]).then_inc(staged, 1)
                act.wait_ge(chain, 2)
                nc.scalar.activation(P[:], L[:], ACT.Exp).then_inc(expd, 1)

            @block.tensor
            def _(pe):
                pe.wait_ge(w_loaded, 16)
                with pe.Fori(0, B // 2) as i:
                    for s in range(2):
                        pe.wait_ge(staged, i * 2 + s + 1)
                        pe.wait_ge(copied, i * 2 + s + 1)
                        for t in range(8):
                            mm = nc.tensor.matmul(l_ps[:, s, t * E:(t + 1) * E], xs[:, s, t * C:(t + 1) * C], wr[:],
                                                  start=True, stop=True)
                        mm.then_inc(logits, 1)
                pe.wait_ge(gates, 1)
                for i in range(B):
                    mm = nc.tensor.transpose(g_ps[0:E * 8, i, :], G[:, i * 8:(i + 1) * 8, :].rearrange("p t e -> p (t e)"), identf[:])
                    if i % 4 == 3:
                        mm.then_inc(turned, 1)

            @block.vector
            def _(v):
                count = [0]

                def chained(ins):
                    count[0] += 1
                    ins.then_inc(chain, 1)
                    v.wait_ge(chain, count[0])

                grant(nc, scratch, [(logits, 2), (copied, 2)])
                with v.Fori(0, B // 2) as i:
                    for s in range(2):
                        v.wait_ge(logits, i * 2 + s + 3)
                        nc.vector.tensor_copy(L[:].rearrange("p (i c) e -> p i (c e)", i=B)[:, i * 2 + s, :],
                                              l_ps[:, s, 0:8 * E]).then_inc(copied, 1)
                v.wait_ge(copied, B + 2)
                chained(nc.vector.tensor_reduce(m1[:], L[:], AX.X, ALU.max))
                chained(nc.vector.tensor_tensor(L[:], L[:], wide(m1), ALU.subtract))
                v.wait_ge(expd, 1)
                chained(nc.vector.tensor_reduce(m1[:], P[:], AX.X, ALU.add))
                chained(nc.vector.reciprocal(r[:], m1[:]))
                chained(nc.vector.tensor_tensor(P[:], P[:], wide(r), ALU.mult))
                pref = prefer[:].unsqueeze(1).to_broadcast([C, T, E])
                chained(nc.vector.tensor_reduce(m1[:], P[:], AX.X, ALU.max))
                chained(nc.vector.tensor_tensor(M[:], P[:], wide(m1), ALU.is_equal))
                chained(nc.vector.tensor_tensor(M[:], M[:], pref, ALU.mult))
                chained(nc.vector.tensor_reduce(r[:], M[:], AX.X, ALU.max))
                chained(nc.vector.tensor_tensor(G[:], M[:], wide(r), ALU.is_equal))
                chained(nc.vector.scalar_tensor_tensor(L[:].rearrange("p t e -> p (t e)"), G[:].rearrange("p t e -> p (t e)"),
                                                       -4.0, P[:].rearrange("p t e -> p (t e)"), ALU.mult, ALU.add))
                chained(nc.vector.tensor_reduce(m2[:], L[:], AX.X, ALU.max))
                chained(nc.vector.tensor_tensor(M[:], L[:], wide(m2), ALU.is_equal))
                chained(nc.vector.tensor_tensor(M[:], M[:], pref, ALU.mult))
                chained(nc.vector.tensor_reduce(r[:], M[:], AX.X, ALU.max))
                chained(nc.vector.tensor_tensor(M[:], M[:], wide(r), ALU.is_equal))
                chained(nc.vector.tensor_tensor(G[:], G[:], M[:], ALU.add))
                chained(nc.vector.tensor_tensor(m1[:], m1[:], m2[:], ALU.add))
                if guard == "max":
                    chained(nc.vector.tensor_scalar(m1[:], m1[:], 1e-12, None, ALU.max))
                else:
                    chained(nc.vector.tensor_scalar(m1[:], m1[:], 1e-9, None, ALU.add))
                chained(nc.vector.reciprocal(r[:], m1[:]))
                chained(nc.vector.tensor_tensor(P[:], P[:], wide(r), ALU.mult))
                chained(nc.vector.tensor_tensor(P[:], P[:], G[:], ALU.mult))
                nc.vector.tensor_copy(G[:].rearrange("p (i c) e -> p i (c e)", i=B).rearrange("p i (e t) -> p i e t", e=E),
                                      P[:].rearrange("p (i t) e -> p i e t", i=B)).then_inc(gates, 1)
                for half in range(2):
                    v.wait_ge(turned, half + 1)
                    nc.vector.tensor_copy(gt[:, 4 * half:4 * half + 4], g_ps[0:E * 8, 4 * half:4 * half + 4]).then_inc(gcopied, 1)


def gelu_experts(chip, X, XN, dram, g_scr):
    nc = chip.nc
    GS = 4
    with chip.stage() as ctx:
        w1, w2 = chip.buf(ctx, "w1", [C, E, C]), chip.buf(ctx, "w2", [C, E, C])
        wh, wl = (chip.buf(ctx, n, [C, E, C], F16) for n in ("wh", "wl"))
        b1, b2 = chip.buf(ctx, "b1", [C, E]), chip.buf(ctx, "b2", [E, C])
        xh, xs, xl = (chip.buf(ctx, n, [C, 2, N], F16) for n in ("xh", "xs", "xl"))
        gb = chip.buf(ctx, "gb", [C, GS, N])
        gt = chip.buf(ctx, "gt", [E, 2, N])
        hs, hg = chip.buf(ctx, "hs", [C, 2, N]), chip.buf(ctx, "hg", [C, 2, N])
        scratch = chip.buf(ctx, "scratch", [1, 8])
        h_ps = chip.psum(ctx, "h_ps", [C, 2, N])
        y_ps = chip.psum(ctx, "y_ps", [C, N])
        w_loaded, h_ready, gelu_done, gated, gated_ve, residual, added, y_steps = (chip.sem(s) for s in (
            "w_loaded", "h_ready", "gelu_done", "gated", "gated_ve", "residual", "added", "y_steps"))
        w_hi, w_rest, w_split, x_hi, x_scaled, x_lo = (chip.sem(s) for s in (
            "w_hi", "w_rest", "w_split", "x_hi", "x_scaled", "x_lo"))
        gb_loaded = [chip.sem("gb_loaded") for _ in range(GS)]
        gt_loaded = [chip.sem("gt_loaded") for _ in range(2)]

        def images(engine, image):
            with engine.Fori(0, B // 2 - 1) as i:
                image(i, 0, False)
                image(i, 1, False)
            image(B // 2 - 1, 0, False)
            image(B // 2 - 1, 1, True)

        with nc.Block() as block:
            @block.sync
            def _(sp):
                for dst, name in ((w1, "m2_w1"), (w2, "m2_w2"), (b1, "m2_b1"), (b2, "m2_b2")):
                    sp.dma_start(dst[:], dram[name]).then_inc(w_loaded, 16)
                with sp.Fori(0, B // 2) as i:
                    for s in range(2):
                        sp.wait_ge(added, i * 2 + s + 1)
                        sp.dma_start(gt[:, s], g_scr[i * 2 + s]).then_inc(gt_loaded[s], 16)
                        for e in range(E):
                            sp.wait_ge(gated, i * 2 * E + (s * E + e) + 1)
                            sp.wait_ge(gated_ve, i * 2 * E + (s * E + e) + 1)
                            sp.dma_start(gb[:, e % GS], g_scr[i * 2 + s, e:e + 1].to_broadcast([C, N])).then_inc(gb_loaded[e % GS], 16)

            @block.tensor
            def _(pe):
                def hidden(i, odd, e):
                    if e == 0:
                        pe.wait_ge(x_scaled, i * 2 + odd + 1)
                        pe.wait_ge(x_lo, i * 2 + odd + 1)
                    pe.wait_ge(gelu_done, i * 2 * E + odd * E + e + 1)
                    for c in range(2):
                        at = slice(c * HALF, (c + 1) * HALF)
                        out = h_ps[:, e % 2, at]
                        nc.tensor.matmul(out, wh[:, e, :], xh[:, odd, at], start=True, stop=False)
                        nc.tensor.matmul(out, wh[:, e, :], xl[:, odd, at], start=False, stop=False)
                        mm = nc.tensor.matmul(out, wl[:, e, :], xs[:, odd, at], start=False, stop=True)
                    mm.then_inc(h_ready, 1)

                def output(i, odd, e):
                    if e == 0:
                        pe.wait_ge(gt_loaded[odd], i * 16 + 16)
                        pe.wait_ge(added, i * 2 + odd + 2)
                        for c in range(2):
                            nc.tensor.matmul(y_ps[:, c * HALF:(c + 1) * HALF], b2[:],
                                             gt[:, odd, c * HALF:(c + 1) * HALF], start=True, stop=False)
                    pe.wait_ge(gated, i * 2 * E + odd * E + e + GS + 1)
                    pe.wait_ge(gated_ve, i * 2 * E + odd * E + e + GS + 1)
                    for c in range(2):
                        mm = nc.tensor.matmul(y_ps[:, c * HALF:(c + 1) * HALF], w2[:, e, :],
                                              hg[:, e % 2, c * HALF:(c + 1) * HALF], start=False, stop=(e == E - 1))
                    mm.then_inc(y_steps, 1)

                def image(i, odd, last):
                    for e in range(E):
                        if e + 1 < E:
                            hidden(i, odd, e + 1)
                        elif not last:
                            hidden(i + odd, 1 - odd, 0)
                        output(i, odd, e)

                pe.wait_ge(w_loaded, 64)
                pe.wait_ge(w_split, 1)
                hidden(0, 0, 0)
                images(pe, image)

            @block.scalar
            def _(act):
                def high(i, odd):
                    x = XN[:, i * 2 + odd, :]
                    nc.scalar.copy(xh[:, odd], x).then_inc(x_hi, 1)
                    nc.scalar.activation(xs[:, odd], x, ACT.Copy, scale=1 / LO).then_inc(x_scaled, 1)

                def image(i, odd, last):
                    for e in range(E):
                        act.wait_ge(h_ready, i * 2 * E + odd * E + e + 1)
                        act.wait_ge(gated, i * 2 * E + odd * E + e + GS - 1)
                        act.wait_ge(gated_ve, i * 2 * E + odd * E + e + GS - 1)
                        nc.scalar.activation(hs[:, e % 2], h_ps[:, e % 2], ACT.Gelu, bias=b1[:, e:e + 1]).then_inc(gelu_done, 1)
                        if e == 2 and not last:
                            high(i + odd, 1 - odd)

                act.wait_ge(w_loaded, 64)
                nc.scalar.copy(wh[:], w1[:]).then_inc(w_hi, 1)
                high(0, 0)
                images(act, image)

            @block.gpsimd
            def _(pool):
                with pool.Fori(0, B) as i:
                    for e in range(E):
                        pool.wait_ge(gelu_done, i * E + e + 3)
                        pool.wait_ge(gb_loaded[e % GS], (i * (E // GS) + e // GS) * 16 + 16)
                        pool.wait_ge(y_steps, i * E + e + 1)
                        nc.gpsimd.tensor_tensor(hg[:, e % 2, 0:HALF], hs[:, e % 2, 0:HALF], gb[:, e % GS, 0:HALF],
                                                ALU.mult).then_inc(gated, 1)

            @block.vector
            def _(v):
                def low(i, odd):
                    v.wait_ge(x_hi, i * 2 + odd + 1)
                    nc.vector.tensor_tensor(xl[:, odd], XN[:, i * 2 + odd, :], xh[:, odd], ALU.subtract).then_inc(x_lo, 1)

                def image(i, odd, last):
                    at = X[:, i * 2 + odd, :]
                    for e in range(E):
                        v.wait_ge(gelu_done, i * 2 * E + odd * E + e + 3)
                        v.wait_ge(gb_loaded[e % GS], i * (2 * E // GS * 16) + (odd * (E // GS) + e // GS + 1) * 16)
                        v.wait_ge(y_steps, i * 2 * E + odd * E + e + 1)
                        nc.vector.tensor_tensor(hg[:, e % 2, HALF:N], hs[:, e % 2, HALF:N], gb[:, e % GS, HALF:N],
                                                ALU.mult).then_inc(gated_ve, 1)
                        if e == 2:
                            nc.vector.tensor_tensor(at, at, XN[:, i * 2 + odd, :], ALU.add).then_inc(residual, 1)
                        if e == 4 and not last:
                            low(i + odd, 1 - odd)
                    v.wait_ge(y_steps, i * 2 * E + odd * E + E + 2)
                    v.wait_ge(residual, i * 2 + odd + 1)
                    nc.vector.tensor_tensor(at, y_ps[:], at, ALU.add).then_inc(added, 1)

                grant(nc, scratch, [(gelu_done, 2), (gated, GS), (gated_ve, GS), (y_steps, 2), (added, 2)])
                v.wait_ge(w_hi, 1)
                nc.vector.tensor_tensor(w1[:], w1[:], wh[:], ALU.subtract).then_inc(w_rest, 1)
                v.wait_ge(w_rest, 1)
                nc.vector.tensor_scalar(wl[:], w1[:], LO, None, ALU.mult).then_inc(w_split, 1)
                low(0, 0)
                images(v, image)


def chunk_experts(c):
    first, last = c * C // HID, min((c + 1) * C, E * HID) - 1
    return first, last // HID, (first + 1) * HID - c * C


def silu_experts(chip, X, XN, dram, g_scr, out):
    nc = chip.nc
    MIXED = [c for c in range(CHUNKS) if chunk_experts(c)[0] != chunk_experts(c)[1]]
    GB = E + len(MIXED)
    H_SLOTS, HG_SLOTS, LAG = 2, 4, 2
    PER = 2 * CHUNKS
    assert PER % HG_SLOTS == 0
    with chip.stage() as ctx:
        wh, wl = (chip.buf(ctx, n, [C, 2, CHUNKS, C], F16) for n in ("wh", "wl"))
        w2 = chip.buf(ctx, "w2", [C, CHUNKS, C])
        xh, xs, xl = (chip.buf(ctx, n, [C, 2, HALF], F16) for n in ("xh", "xs", "xl"))
        gb = chip.buf(ctx, "gb", [C, 2, GB, HALF])
        s1, u = (chip.buf(ctx, n, [C, H_SLOTS, HALF]) for n in ("s1", "u"))
        hg = chip.buf(ctx, "hg", [C, HG_SLOTS, HALF])
        scratch = chip.buf(ctx, "scratch", [1, 8])
        h_ps = chip.psum(ctx, "h_ps", [C, H_SLOTS, 2, HALF])
        y_ps = chip.psum(ctx, "y_ps", [C, 2, HALF])
        w_loaded, w_hi, w_split, x_hi, x_scaled, x_lo = (chip.sem(s) for s in (
            "w_loaded", "w_hi", "w_split", "x_hi", "x_scaled", "x_lo"))
        w_rest = [chip.sem("w_rest") for _ in range(2)]
        w2_loaded, h_ready, silu_done, hidden, gated, y_steps, added, stored = (chip.sem(s) for s in (
            "w2_loaded", "h_ready", "silu_done", "hidden", "gated", "y_steps", "added", "stored"))
        gb_loaded = [chip.sem("gb_loaded") for _ in range(2)]

        def whole(n):
            return gb[:, n].rearrange("p g t -> p (g t)")[:, 0:CHUNKS * C]

        def flat(part, n):
            return part[:, n].rearrange("p c m -> p (c m)")

        with nc.Block() as block:
            @block.sync
            def _(sp):
                for n, name in enumerate(("m3_w1", "m3_w3")):
                    sp.dma_start(whole(n), dram[name]).then_inc(w_loaded, 16)
                sp.dma_start(w2[:].rearrange("p c m -> p (c m)"), dram["m3_w2"]).then_inc(w2_loaded, 16)
                sp.wait_ge(w_split, 2)
                def store(i, s):
                    at = slice(s * HALF, (s + 1) * HALF)
                    sp.dma_start(out[i].rearrange("c h w -> c (h w)")[:, at], X[:, i, at]).then_inc(stored, 16)

                def image(i, first):
                    for s in range(2):
                        gates = g_scr[i, :, s * HALF:(s + 1) * HALF]
                        sp.wait_ge(added, i * 2 + s + 1)
                        if not first:
                            store(i - 1, s)
                        sp.dma_start(gb[:, s, 0:E], gates.unsqueeze(0).to_broadcast([C, E, HALF])).then_inc(gb_loaded[s], 16)
                        for n, c in enumerate(MIXED):
                            first_e, last_e, row = chunk_experts(c)
                            for e, rows in ((first_e, slice(0, row)), (last_e, slice(row, C))):
                                sp.dma_start(gb[rows, s, E + n],
                                             gates[e:e + 1].to_broadcast([rows.stop - rows.start, HALF])
                                             ).then_inc(gb_loaded[s], 16)

                image(0, True)
                with sp.Fori(1, B) as i:
                    image(i, False)
                for s in range(2):
                    sp.wait_ge(added, B * 2 + s + 1)
                    store(B - 1, s)
                sp.wait_ge(stored, 16 * 2 * B)

            @block.tensor
            def _(pe):
                def image(i):
                    for n in range(PER + LAG):
                        if n < PER:
                            s, c = n // CHUNKS, n % CHUNKS
                            if c == 0:
                                pe.wait_ge(x_scaled, i * 2 + s + 1)
                                pe.wait_ge(x_lo, i * 2 + s + 1)
                            pe.wait_ge(hidden, i * PER + n + 1)
                            for m in range(2):
                                out = h_ps[:, n % H_SLOTS, m]
                                nc.tensor.matmul(out, wh[:, m, c, :], xh[:, s], start=True, stop=False)
                                nc.tensor.matmul(out, wh[:, m, c, :], xl[:, s], start=False, stop=False)
                                mm = nc.tensor.matmul(out, wl[:, m, c, :], xs[:, s], start=False, stop=True)
                            mm.then_inc(h_ready, 1)
                        if n >= LAG:
                            m = n - LAG
                            s, c = m // CHUNKS, m % CHUNKS
                            if c == 0:
                                pe.wait_ge(added, i * 2 + s + 1)
                            pe.wait_ge(gated, i * PER + m + H_SLOTS + 1)
                            nc.tensor.matmul(y_ps[:, s], w2[:, c, :], hg[:, m % HG_SLOTS], start=(c == 0),
                                             stop=(c == CHUNKS - 1)).then_inc(y_steps, 1)

                pe.wait_ge(w_split, 2)
                pe.wait_ge(w2_loaded, 16)
                with pe.Fori(0, B) as i:
                    image(i)

            @block.scalar
            def _(act):
                def high(i, s):
                    x = XN[:, i, s * HALF:(s + 1) * HALF]
                    nc.scalar.copy(xh[:, s], x).then_inc(x_hi, 1)
                    nc.scalar.activation(xs[:, s], x, ACT.Copy, scale=1 / LO).then_inc(x_scaled, 1)

                def image(i, last):
                    for n in range(PER):
                        act.wait_ge(h_ready, i * PER + n + 1)
                        nc.scalar.activation(s1[:, n % H_SLOTS], h_ps[:, n % H_SLOTS, 0], ACT.Silu).then_inc(silu_done, 1)
                        if n == CHUNKS // 2:
                            high(i, 1)
                        if n == CHUNKS // 2 + CHUNKS and not last:
                            high(i + 1, 0)

                act.wait_ge(w_loaded, 32)
                for n in (1, 0):
                    nc.scalar.copy(flat(wh, n), whole(n)).then_inc(w_hi, 1)
                high(0, 0)
                with act.Fori(0, B - 1) as i:
                    image(i, False)
                image(B - 1, True)

            @block.vector
            def _(v):
                def low(i, s):
                    v.wait_ge(x_hi, i * 2 + s + 1)
                    nc.vector.tensor_tensor(xl[:, s], XN[:, i, s * HALF:(s + 1) * HALF], xh[:, s],
                                            ALU.subtract).then_inc(x_lo, 1)

                def image(i, last):
                    for n in range(PER):
                        v.wait_ge(silu_done, i * PER + n + 1)
                        v.wait_ge(gated, i * PER + n + 1)
                        nc.vector.tensor_tensor(u[:, n % H_SLOTS], h_ps[:, n % H_SLOTS, 1], s1[:, n % H_SLOTS],
                                                ALU.mult).then_inc(hidden, 1)
                        if n == CHUNKS // 2:
                            low(i, 1)
                        if n == CHUNKS // 2 + CHUNKS and not last:
                            low(i + 1, 0)
                        if n == CHUNKS + LAG + 1:
                            v.wait_ge(y_steps, i * PER + (CHUNKS + HG_SLOTS))
                            at = X[:, i, 0:HALF]
                            nc.vector.tensor_tensor(at, y_ps[:, 0], at, ALU.add).then_inc(added, 1)
                    v.wait_ge(y_steps, i * PER + (PER + HG_SLOTS))
                    at = X[:, i, HALF:N]
                    nc.vector.tensor_tensor(at, y_ps[:, 1], at, ALU.add).then_inc(added, 1)

                grant(nc, scratch, [(hidden, H_SLOTS), (gated, H_SLOTS), (y_steps, HG_SLOTS), (added, 2)])
                v.wait_ge(w_hi, 2)
                nc.vector.tensor_tensor(whole(0), whole(0), flat(wh, 0), ALU.subtract).then_inc(w_rest[0], 1)
                for n in range(2):
                    v.wait_ge(w_rest[n], 1)
                    nc.vector.tensor_scalar(flat(wl, n), whole(n), LO, None, ALU.mult).then_inc(w_split, 1)
                low(0, 0)
                with v.Fori(0, B - 1) as i:
                    image(i, False)
                image(B - 1, True)

            @block.gpsimd
            def _(pool):
                pool.wait_ge(w_hi, 1)
                nc.gpsimd.tensor_tensor(whole(1), whole(1), flat(wh, 1), ALU.subtract).then_inc(w_rest[1], 1)
                with pool.Fori(0, B) as i:
                    for n in range(PER):
                        s, c = n // CHUNKS, n % CHUNKS
                        if c == 0:
                            pool.wait_ge(gb_loaded[s], (i + 1) * (16 * (1 + 2 * len(MIXED))))
                        tile = E + MIXED.index(c) if c in MIXED else chunk_experts(c)[0]
                        pool.wait_ge(hidden, i * PER + n + H_SLOTS + 1)
                        pool.wait_ge(y_steps, i * PER + n + 1)
                        nc.gpsimd.tensor_tensor(hg[:, n % HG_SLOTS], u[:, n % H_SLOTS], gb[:, s, tile],
                                                ALU.mult).then_inc(gated, 1)


def local_attention(chip, XN, dram, identf, out):
    nc = chip.nc
    TILES = -(-N // QT)
    GROUPS = [(0, 3), (3, 3), (6, 3), (9, 2)]
    assert GROUPS[-1][0] + GROUPS[-1][1] == TILES
    WIDE = 3 * QT
    with chip.stage() as ctx:
        band = chip.buf(ctx, "band", [C, QT])
        ones = chip.buf(ctx, "ones", [C, C])
        xs = chip.buf(ctx, "xs", [C, 2, N + 64])
        tk = chip.buf(ctx, "tk", [C, 2, 3, C])
        ex, em, rd = (chip.buf(ctx, n, [C, 2, WIDE]) for n in ("ex", "em", "rd"))
        scratch = chip.buf(ctx, "scratch", [1, 8])
        t_ps = chip.psum(ctx, "t_ps", [C, 2, HALF])
        s_ps = chip.psum(ctx, "s_ps", [C, 2, HALF])
        n_ps = chip.psum(ctx, "n_ps", [C, 2, HALF])
        d_ps = chip.psum(ctx, "d_ps", [C, 2, HALF])
        w_loaded, filled, staged, turned, scored, copied, expd, masked, summed, inverted, stored = (chip.sem(s) for s in (
            "w_loaded", "filled", "staged", "turned", "scored", "copied", "expd", "masked", "summed", "inverted", "stored"))

        def queries(t):
            return min(QT, N - t * QT)

        with nc.Block() as block:
            @block.sync
            def _(sp):
                sp.dma_start(band[:], dram["band"]).then_inc(w_loaded, 16)
                sp.wait_ge(w_loaded, 16)

            @block.tensor
            def _(pe):
                def front(i, s, g):
                    n = s * 4 + g
                    t0, cnt = GROUPS[g]
                    if g == 0:
                        pe.wait_ge(staged, i * 2 + s + 1)
                    pe.wait_ge(copied, i * 8 + n + 1)
                    for t in range(cnt):
                        mm = nc.tensor.transpose(t_ps[:, n % 2, t * C:(t + 1) * C],
                                                 xs[:, s, (t0 + t) * QT:(t0 + t) * QT + C], identf[:])
                    mm.then_inc(turned, 1)
                    pe.wait_ge(expd, i * 8 + n + 1)
                    for t in range(cnt):
                        q = queries(t0 + t)
                        at = (t0 + t) * QT
                        mm = nc.tensor.matmul(s_ps[:, n % 2, t * QT:t * QT + q], xs[:, s, at:at + C],
                                              xs[:, s, BAND + at:BAND + at + q], start=True, stop=True)
                    mm.then_inc(scored, 1)

                def back(i, s, g):
                    n = s * 4 + g
                    t0, cnt = GROUPS[g]
                    pe.wait_ge(masked, i * 8 + n + 3)
                    pe.wait_ge(copied, i * 8 + n + 3)
                    pe.wait_ge(stored, i * 8 + n + 1)
                    for t in range(cnt):
                        q = queries(t0 + t)
                        nc.tensor.matmul(n_ps[:, n % 2, t * QT:t * QT + q], tk[:, n % 2, t], em[:, n % 2, t * QT:t * QT + q],
                                         start=True, stop=True)
                    width = (cnt - 1) * QT + queries(t0 + cnt - 1)
                    nc.tensor.matmul(d_ps[:, n % 2, 0:width], ones[:], em[:, n % 2, 0:width],
                                     start=True, stop=True).then_inc(summed, 1)

                pe.wait_ge(filled, 3)
                with pe.Fori(0, B // 2) as i:
                    for n in range(9):
                        if n < 8:
                            front(i, n // 4, n % 4)
                        if n:
                            back(i, (n - 1) // 4, (n - 1) % 4)

            @block.scalar
            def _(act):
                act.wait_ge(filled, 3)
                with act.Fori(0, B // 2) as i:
                    for n in range(8):
                        s, g = n // 4, n % 4
                        t0, cnt = GROUPS[g]
                        if g == 0:
                            act.wait_ge(summed, i * 8 + 4 * s + 1)
                            nc.scalar.copy(xs[:, s, BAND:BAND + N], XN[:, i * 2 + s, :]).then_inc(staged, 1)
                        width = (cnt - 1) * QT + queries(t0 + cnt - 1)
                        act.wait_ge(scored, i * 8 + n + 1)
                        act.wait_ge(masked, i * 8 + n + 1)
                        nc.scalar.activation(ex[:, n % 2, 0:width], s_ps[:, n % 2, 0:width], ACT.Exp,
                                             scale=float(C) ** -0.5).then_inc(expd, 1)

            @block.vector
            def _(v):
                nc.vector.memset(xs[:], 0.0).then_inc(filled, 1)
                nc.vector.memset(ones[:], 1.0).then_inc(filled, 1)
                grant(nc, scratch, [(copied, 2), (expd, 2), (masked, 2), (stored, 2), (summed, 4), (filled, 1)])
                v.wait_ge(w_loaded, 16)

                def finish(i, n):
                    s, g = n // 4, n % 4
                    t0, cnt = GROUPS[g]
                    width = (cnt - 1) * QT + queries(t0 + cnt - 1)
                    v.wait_ge(summed, i * 8 + n + 5)
                    nc.vector.reciprocal(rd[:, n % 2, 0:width], d_ps[:, n % 2, 0:width]).then_inc(inverted, 1)
                    v.wait_ge(inverted, i * 8 + n + 1)
                    nc.vector.tensor_tensor(out[:, i * 2 + s, t0 * QT:t0 * QT + width], n_ps[:, n % 2, 0:width],
                                            rd[:, n % 2, 0:width], ALU.mult).then_inc(stored, 1)

                with v.Fori(0, B // 2) as i:
                    for n in range(9):
                        if n < 8:
                            cnt = GROUPS[n % 4][1]
                            t0 = GROUPS[n % 4][0]
                            v.wait_ge(turned, i * 8 + n + 1)
                            v.wait_ge(summed, i * 8 + n + 3)
                            nc.vector.tensor_copy(tk[:, n % 2, 0:cnt].rearrange("p t c -> p (t c)"),
                                                  t_ps[:, n % 2, 0:cnt * C]).then_inc(copied, 1)
                            v.wait_ge(expd, i * 8 + n + 3)
                            full = cnt if queries(t0 + cnt - 1) == QT else cnt - 1
                            ins = nc.vector.tensor_tensor(
                                em[:, n % 2, 0:full * QT].rearrange("p (t q) -> p t q", q=QT),
                                ex[:, n % 2, 0:full * QT].rearrange("p (t q) -> p t q", q=QT),
                                band[:].unsqueeze(1).to_broadcast([C, full, QT]), ALU.mult)
                            if full < cnt:
                                q = queries(t0 + full)
                                ins = nc.vector.tensor_tensor(em[:, n % 2, full * QT:full * QT + q],
                                                              ex[:, n % 2, full * QT:full * QT + q], band[:, 0:q], ALU.mult)
                            ins.then_inc(masked, 1)
                        if n:
                            finish(i, n - 1)


def network(nc, x, dram, out):
    def scratch(name, shape, dt=F32):
        return nc.dram_tensor(name, shape, dt, kind="Internal").ap()

    qk0 = scratch("qk0", [B, 4, PARTS, C, N], BF16)
    v0 = scratch("v0", [B, 4, C, 8 * 64])
    qk2 = scratch("qk2", [B, 2, PARTS, C, N], BF16)
    v2 = scratch("v2", [B, 4, C, 8 * 32])
    m0 = scratch("m0", [2, 2, PARTS, 4, 8, C], BF16)
    m2 = scratch("m2", [2, 1, PARTS, 4, 8, C], BF16)
    g2 = scratch("g2", [B, E, N])
    g3 = scratch("g3", [B, E, N])

    with ExitStack() as ctx:
        chip = Chip(nc)
        X = chip.buf(ctx, "X", [C, B, N])
        identf = chip.buf(ctx, "identf", [C, C])
        ident = chip.buf(ctx, "ident", [C, C], BF16)
        gn_avg = chip.buf(ctx, "gn_avg", [C, C])
        mean_w = chip.buf(ctx, "mean_w", [C, C])
        prefer = chip.buf(ctx, "prefer", [C, E])
        bproj = chip.buf(ctx, "bproj", [C, 1])
        gamma, beta = chip.buf(ctx, "gamma", [C, 1]), chip.buf(ctx, "beta", [C, 1])
        eps5 = chip.buf(ctx, "eps5", [C, 1])
        mean_g, rstd_g = chip.buf(ctx, "mean_g", [C, B, 1]), chip.buf(ctx, "rstd_g", [C, B, 1])
        pooled = chip.buf(ctx, "pooled", [C, B])
        def flat(a):
            return a[:].rearrange("p b o -> p (b o)")

        group_norm_stats(chip, X, gn_avg, eps5, flat(mean_g), flat(rstd_g), pooled, x,
                         [(identf, dram["ident"]), (gn_avg, dram["gn_avg"]), (mean_w, dram["mean_w"]),
                          (prefer, dram["prefer"]), (bproj, dram["b_proj"]), (gamma, dram["gamma"]),
                          (beta, dram["beta"])], ident, identf)
        window_projections(chip, X, mean_g, rstd_g, dram, qk0, v0)

        attention(chip, X, dram, lambda i, k, o: qk0[i, k, :, 64 * o:64 * o + 64, :], v0, m0, ident, identf,
                  None, None, 2, 1, float(D) ** -0.5)

        group_norm_stats(chip, X, gn_avg, eps5, flat(mean_g), flat(rstd_g), pooled)
        conv_stage(chip, X, dram, mean_g, rstd_g, pooled, eps5, identf)

        with ExitStack() as c2:
            XN = chip.buf(c2, "XN", [C, B, N])
            layer_norm(chip, X, mean_w, eps5, identf, dst=XN)
            token_projections(chip, XN, dram, qk2, v2)
        attention(chip, X, dram, lambda i, k, o: qk2[i, o, :, 32 * k:32 * k + 32, :], v2, m2, ident, identf,
                  "w_proj", bproj, 1, 8, 1.0)

        with ExitStack() as c2:
            XN = chip.buf(c2, "XN", [C, B, N])
            layer_norm(chip, X, mean_w, eps5, identf, dst=XN)
            route(chip, XN, dram, "m2_router", identf, prefer, "max", g2)
            gelu_experts(chip, X, XN, dram, g2)
            layer_norm(chip, X, mean_w, eps5, identf, dst=XN)
            with ExitStack() as c3:
                O = chip.buf(c3, "O", [C, B, N])
                local_attention(chip, XN, dram, identf, O)
                layer_norm(chip, O, mean_w, eps5, identf, X=X, gamma=gamma, beta=beta)
            layer_norm(chip, X, mean_w, eps5, identf, dst=XN)
            route(chip, XN, dram, "m3_router", identf, prefer, "add", g3)
            silu_experts(chip, X, XN, dram, g3, out)


def constants():
    import numpy as np

    c = np.arange(C)
    one = np.float32(1)
    key, query = np.arange(C)[:, None], np.arange(QT)[None, :]
    band = np.where((key >= query) & (key <= query + 2 * BAND), one, 0 * one)
    return {
        "ident": np.eye(C, dtype=np.float32),
        "gn_avg": np.where(c[:, None] // 4 == c[None, :] // 4, one / 4, 0 * one).astype(np.float32),
        "mean_w": np.full((C, C), 1 / C, np.float32),
        "prefer": np.tile(np.arange(E, 0, -1, dtype=np.float32), (C, 1)),
        "band": band.astype(np.float32),
    }


def laid_out(a):
    import numpy as np

    out = {}
    wq = a["L0_conv_w_qkv"][:, :, 0, 0]
    head_major = np.array([d * 8 + h for h in range(8) for d in range(D)])
    stacked = np.array([d * 8 + 2 * hp + e for e in range(2) for d in range(D) for hp in range(4)])
    qk, vv = np.zeros((C, 4, C), np.float32), np.zeros((C, 4, 64), np.float32)
    lepe, taps, bl = np.zeros((C, 2, C), np.float32), np.zeros((2, 9, C), np.float32), np.zeros((C, 2), np.float32)
    for u in range(4):
        s, part = u // 2 * 2, u % 2
        rows = (part * 64 + np.arange(64) + s) % C
        qk[rows, u, 0:64] = wq[stacked].T
        qk[rows, u, 64:128] = wq[64 + stacked].T
        vv[rows, u] = wq[128 + head_major].T
        conv = (np.arange(64) - s) % 64
        at = slice(part * 64, part * 64 + 64)
        lepe[rows, s // 2, at] = wq[128 + conv].T
        taps[s // 2, :, at] = a["L0_conv_w_lepe"][conv, 0].reshape(64, 9).T
        bl[at, s // 2] = a["L0_conv_b_lepe"][conv]
    out["w0_qk"], out["w0_v"], out["w0_lepe"] = qk, vv, lepe
    out["lepe_taps"], out["b_lepe"] = taps.reshape(1, -1), bl
    out["se_w1"], out["se_w2"] = a["L1_conv_attn_w1"].T, a["L1_conv_attn_w2"].T
    out["refine_w"], out["refine_b"] = a["L1_conv_refine_w"].reshape(C, 9), a["L1_conv_refine_b"].reshape(C, 1)
    w = a["L2_attn_w_qkv"]
    stacked = np.array([32 * k + (2 * hp + e) * D + d for k in range(4) for e in range(2) for d in range(D) for hp in range(2)])
    out["w2_qk"], out["w2_v"] = w[:, :2 * C].reshape(C, 2, C)[:, :, stacked], w[:, 2 * C:]
    b = a["L2_attn_b_qkv"]
    out["b2_qk"], out["b2_v"] = b[:2 * C].reshape(2, C)[:, stacked].T, b[2 * C:].reshape(1, C)
    out["w_proj"], out["b_proj"] = a["L2_attn_w_proj"], a["L2_attn_b_proj"].reshape(C, 1)
    out["m2_router"], out["m3_router"] = a["L2_ffn_router_w"].T, a["L3_ffn_router_w"].T
    out["m2_w1"], out["m2_w2"] = a["L2_ffn_w1"].transpose(1, 0, 2), a["L2_ffn_w2"].transpose(1, 0, 2)
    out["m2_b1"], out["m2_b2"] = a["L2_ffn_b1"].T, a["L2_ffn_b2"]
    out["gamma"], out["beta"] = a["L3_attn_gamma"].reshape(C, 1), a["L3_attn_beta"].reshape(C, 1)
    for name in ("w1", "w3"):
        padded = np.zeros((C, CHUNKS * C), np.float32)
        padded[:, :E * HID] = a[f"L3_ffn_{name}"].reshape(E * HID, C).T
        out["m3_" + name] = padded
    w2 = np.zeros((CHUNKS * C, C), np.float32)
    w2[:E * HID] = a["L3_ffn_w2"].transpose(0, 2, 1).reshape(E * HID, C)
    out["m3_w2"] = w2.reshape(CHUNKS, C, C).transpose(1, 0, 2).reshape(C, -1)
    return out


def kernel(**inputs):
    import numpy as np
    import concourse.bacc as bacc
    from concourse.bass_utils import run_bass_kernel_spmd as run

    inputs = {name: np.asarray(value) for name, value in inputs.items()}
    nc = bacc.Bacc("TRN2", target_bir_lowering=False, num_devices=1)
    arrays, dram = {}, {}
    for name, value in {"x": inputs["x"], **constants(), **laid_out(inputs)}.items():
        value = np.ascontiguousarray(value)
        arrays[f"in_{name}"] = value
        dram[name] = nc.dram_tensor(f"in_{name}", value.shape, mybir.dt.from_np(value.dtype), kind="ExternalInput").ap()
    out = nc.dram_tensor("out", inputs["x"].shape, F32, kind="ExternalOutput").ap()
    network(nc, dram["x"], dram, out)
    return run(nc, [arrays], core_ids=[0]).results[0]["out"]
```
